# Optimizing a Trainium2 kernel written in Bass

```python
import numpy as np
import jax
import jax.numpy as jnp

def _softmax(x, axis=-1):
    return jax.nn.softmax(x, axis=axis)

def _gelu(x):
    return jax.nn.gelu(x, approximate=True)

def _silu(x):
    return jax.nn.silu(x)

def _sigmoid(x):
    return jax.nn.sigmoid(x)

def _layernorm(x, axis=-1, eps=1e-05):
    m = jnp.mean(x, axis=axis, keepdims=True)
    v = jnp.var(x, axis=axis, keepdims=True)
    return (x - m) / jnp.sqrt(v + eps)

def _scatter_add(tgt, idx, src, axis=0):
    return tgt.at[idx].add(src)

def _segment_sum(src, seg, n):
    return jax.ops.segment_sum(src, seg, n)
kernel_name = 'mk_adaln_d1_jaxref_r8_065c93'

def setup_inputs(seed: int=0):
    np.random.seed(seed)
    _w = jnp.asarray

    def _L0_attn_setup():
        import jax, jax.numpy as jnp
        import numpy as np
        B, T, D, H, R = (1, 512, 128, 16, 64)
        HD = D // H
        STD = 0.02

        def _low_rank_proj(x, a, b):
            mid = jnp.einsum('btd,hdr->bhtr', x, a)
            return jnp.einsum('bhtr,hrd->bhtd', mid, b)
        key = jax.random.key(seed)
        ks = jax.random.split(key, 8)
        return {'hidden_states': jax.random.normal(ks[0], (B, T, D), jnp.float32), 'q_a': STD * jax.random.normal(ks[1], (H, D, R), jnp.float32), 'q_b': STD * jax.random.normal(ks[2], (H, R, HD), jnp.float32), 'k_a': STD * jax.random.normal(ks[3], (H, D, R), jnp.float32), 'k_b': STD * jax.random.normal(ks[4], (H, R, HD), jnp.float32), 'v_w': STD * jax.random.normal(ks[5], (D, D), jnp.float32), 'v_b': jnp.zeros((D,), jnp.float32), 'o_w': STD * jax.random.normal(ks[6], (D, D), jnp.float32), 'o_b': jnp.zeros((D,), jnp.float32)}
    _L0_attn_in = _L0_attn_setup()

    def _L0_ffn_setup():
        import jax, jax.numpy as jnp
        import numpy as np
        H = 128
        I = 4 * H
        E = 8
        K = 2
        B, S = (2, 128)
        STD = 0.02 / np.sqrt(H)
        key = jax.random.key(seed)
        ks = jax.random.split(key, 8)
        x = jax.random.normal(ks[0], (B, S, H), dtype=jnp.float32)
        gate_w = jax.random.normal(ks[1], (H, E), dtype=jnp.float32) * STD
        bias = jnp.zeros((E,), dtype=jnp.float32)
        up_w = jax.random.normal(ks[2], (E, H, I), dtype=jnp.float32) * STD
        up_b = jnp.zeros((E, I), dtype=jnp.float32)
        down_w = jax.random.normal(ks[3], (E, I, H), dtype=jnp.float32) * STD
        down_b = jnp.zeros((E, H), dtype=jnp.float32)
        sw_up = jax.random.normal(ks[4], (H, I), dtype=jnp.float32) * STD
        sb_up = jnp.zeros((I,), dtype=jnp.float32)
        sw_down = jax.random.normal(ks[5], (I, H), dtype=jnp.float32) * STD
        sb_down = jnp.zeros((H,), dtype=jnp.float32)
        return {'x': x, 'gate_w': gate_w, 'bias': bias, 'up_w': up_w, 'up_b': up_b, 'down_w': down_w, 'down_b': down_b, 'sw_up': sw_up, 'sb_up': sb_up, 'sw_down': sw_down, 'sb_down': sb_down}
    _L0_ffn_in = _L0_ffn_setup()
    _L0_c = _w((lambda *s: np.random.randn(*s).astype(np.float32) * 0.05)(4, 128))
    _L0_wmod = _w((lambda *s: np.random.randn(*s).astype(np.float32) * 0.05)(128, 6 * 128) * 128 ** (-0.5))
    _d = {'L0_attn_hidden_states': _L0_attn_in['hidden_states'], 'L0_attn_q_a': _L0_attn_in['q_a'], 'L0_attn_q_b': _L0_attn_in['q_b'], 'L0_attn_k_a': _L0_attn_in['k_a'], 'L0_attn_k_b': _L0_attn_in['k_b'], 'L0_attn_v_w': _L0_attn_in['v_w'], 'L0_attn_v_b': _L0_attn_in['v_b'], 'L0_attn_o_w': _L0_attn_in['o_w'], 'L0_attn_o_b': _L0_attn_in['o_b'], 'L0_ffn_gate_w': _L0_ffn_in['gate_w'], 'L0_ffn_bias': _L0_ffn_in['bias'], 'L0_ffn_up_w': _L0_ffn_in['up_w'], 'L0_ffn_up_b': _L0_ffn_in['up_b'], 'L0_ffn_down_w': _L0_ffn_in['down_w'], 'L0_ffn_down_b': _L0_ffn_in['down_b'], 'L0_ffn_sw_up': _L0_ffn_in['sw_up'], 'L0_ffn_sb_up': _L0_ffn_in['sb_up'], 'L0_ffn_sw_down': _L0_ffn_in['sw_down'], 'L0_ffn_sb_down': _L0_ffn_in['sb_down'], 'L0_c': _L0_c, 'L0_wmod': _L0_wmod}
    _x0 = _d['L0_attn_hidden_states']
    _d['L0_attn_hidden_states'] = jax.random.normal(jax.random.fold_in(jax.random.key(seed), 1), (4, 1024, 128), dtype=_x0.dtype)
    del _x0
    return _d

def reference(L0_attn_hidden_states, L0_attn_q_a, L0_attn_q_b, L0_attn_k_a, L0_attn_k_b, L0_attn_v_w, L0_attn_v_b, L0_attn_o_w, L0_attn_o_b, L0_ffn_gate_w, L0_ffn_bias, L0_ffn_up_w, L0_ffn_up_b, L0_ffn_down_w, L0_ffn_down_b, L0_ffn_sw_up, L0_ffn_sb_up, L0_ffn_sw_down, L0_ffn_sb_down, L0_c, L0_wmod):

    def _L0_attn_ref(hidden_states, q_a, q_b, k_a, k_b, v_w, v_b, o_w, o_b):
        import jax, jax.numpy as jnp
        import numpy as np
        B, T, D, H, R = (1, 512, 128, 16, 64)
        HD = D // H
        STD = 0.02

        def _low_rank_proj(x, a, b):
            mid = jnp.einsum('btd,hdr->bhtr', x, a)
            return jnp.einsum('bhtr,hrd->bhtd', mid, b)
        Bc, Tc, Dc = hidden_states.shape
        q = _low_rank_proj(hidden_states, q_a, q_b)
        k = _low_rank_proj(hidden_states, k_a, k_b)
        v = hidden_states @ v_w.T + v_b
        v = v.reshape(Bc, Tc, H, HD).transpose(0, 2, 1, 3)
        scale = 1.0 / np.sqrt(HD).astype(np.float32)
        att = jnp.einsum('bhtd,bhsd->bhts', q, k) * scale
        causal = jnp.tril(jnp.ones((Tc, Tc), dtype=bool))
        att = jnp.where(causal[None, None], att, jnp.finfo(att.dtype).min)
        att = jax.nn.softmax(att, axis=-1)
        y = jnp.einsum('bhts,bhsd->bhtd', att, v)
        y = y.transpose(0, 2, 1, 3).reshape(Bc, Tc, Dc)
        return y @ o_w.T + o_b

    def _L0_ffn_ref(x, gate_w, bias, up_w, up_b, down_w, down_b, sw_up, sb_up, sw_down, sb_down):
        import jax, jax.numpy as jnp
        import numpy as np
        H = 128
        I = 4 * H
        E = 8
        K = 2
        B, S = (2, 128)
        STD = 0.02 / np.sqrt(H)
        b, s, h = x.shape
        xf = x.reshape(-1, h)
        T = xf.shape[0]
        scores = jax.nn.sigmoid(xf @ gate_w + bias)
        top_scores, top_idx = jax.lax.top_k(scores, K)
        top_scores = top_scores / (jnp.sum(top_scores, axis=-1, keepdims=True) + 1e-06)
        w = jnp.zeros((T, E), dtype=xf.dtype).at[jnp.arange(T)[:, None], top_idx].add(top_scores)
        up = jnp.einsum('th,ehi->tei', xf, up_w) + up_b
        hact = jax.nn.gelu(up, approximate=False)
        eo = jnp.einsum('tei,eih->teh', hact, down_w) + down_b
        combined = jnp.einsum('teh,te->th', eo * 0.1, w)
        shared = (jax.nn.gelu(xf @ sw_up + sb_up, approximate=False) @ sw_down + sb_down) * 0.1
        out = (shared + combined).reshape(b, s, h)
        out = out / (jnp.max(jnp.abs(out), axis=-1, keepdims=True) + 1e-06)
        return out
    x = L0_attn_hidden_states
    mod = (_silu(L0_c) @ L0_wmod).reshape(L0_c.shape[0], 6, 1, -1)
    sa, ca, ga, sb, cb, gb = (mod[:, 0], mod[:, 1], mod[:, 2], mod[:, 3], mod[:, 4], mod[:, 5])
    ga = (2 * (ga >= 0) - 1) * jnp.maximum(jnp.abs(ga), 0.25)
    gb = (2 * (gb >= 0) - 1) * jnp.maximum(jnp.abs(gb), 0.25)
    h = _layernorm(x, axis=-1) * (1 + ca) + sa
    x = x + ga * _L0_attn_ref(h, L0_attn_q_a, L0_attn_q_b, L0_attn_k_a, L0_attn_k_b, L0_attn_v_w, L0_attn_v_b, L0_attn_o_w, L0_attn_o_b)
    h = _layernorm(x, axis=-1) * (1 + cb) + sb
    x = x + gb * _L0_ffn_ref(h, L0_ffn_gate_w, L0_ffn_bias, L0_ffn_up_w, L0_ffn_up_b, L0_ffn_down_w, L0_ffn_down_b, L0_ffn_sw_up, L0_ffn_sb_up, L0_ffn_sw_down, L0_ffn_sb_down)
    return x

_drawn_inputs = setup_inputs


def setup_inputs(seed=0):
    import zlib

    import numpy as np

    out = dict(_drawn_inputs(seed))
    spreads = {'L0_attn_v_b': (0.0, 0.8),
     'L0_attn_o_b': (0.0, 0.294),
     'L0_ffn_bias': (0.0, 0.1),
     'L0_ffn_up_b': (0.0, 0.8),
     'L0_ffn_down_b': (0.0, 0.311),
     'L0_ffn_sb_up': (0.0, 0.8),
     'L0_ffn_sb_down': (0.0, 0.1)}
    factors = {'L0_attn_q_a': 8.0,
     'L0_attn_q_b': 8.0,
     'L0_attn_k_a': 8.0,
     'L0_attn_k_b': 8.0,
     'L0_attn_v_w': 8.0,
     'L0_attn_o_w': 8.0,
     'L0_ffn_up_w': 50.464,
     'L0_ffn_down_w': 8.0,
     'L0_ffn_sw_up': 34.262,
     'L0_ffn_sw_down': 8.0}
    for name, (base, spread) in spreads.items():
        noise = np.random.default_rng([zlib.crc32(name.encode()), seed]).standard_normal(out[name].shape)
        drawn = base * np.exp(spread * noise) if base else spread * noise
        out[name] = jnp.asarray(drawn.astype(out[name].dtype))
    for name, factor in factors.items():
        out[name] = (out[name] * factor).astype(out[name].dtype)
    return out
```

```python
import concourse.bass as bass
from concourse import mybir
from contextlib import ExitStack

F32 = mybir.dt.float32
BF16 = mybir.dt.bfloat16
ALU = mybir.AluOpType
ACT = mybir.ActivationFunctionType
AX = mybir.AxisListType

B, T, D, H, R = 4, 1024, 128, 16, 64
HD = D // H
P = 128
TT = T // P
NT = B * TT
CH = 512
NC = B * T // CH
HG = 4
NG = H // HG
E, I = 8, 512
NE = E + 1
IT = I // P
EPS = 1e-5
NEG = -1.0e30
KA = 9 * HD
KB = KA + 3
SCALE = float(HD) ** -0.5


def pack(width):
    return {128: 4, 256: 2}.get(width, 1)


def row_fills():
    out = []
    for i in range(TT):
        for c in range(0, P * (i + 1), CH):
            w = min(CH, P * (i + 1) - c)
            out += [(i, c, w, h, pack(w)) for h in range(0, HG, pack(w))]
    return out


def col_units():
    return [(c, j, max(P * j, CH * c), CH * (c + 1) - max(P * j, CH * c))
            for c in range(T // CH) for j in range(4 * (c + 1))]


ROWS = row_fills()
UNITS = col_units()
NR = len(ROWS)
NU = len(UNITS)
COLS_PER_UNIT = [HG // pack(u[3]) for u in UNITS]
AREA = HG * sum(u[3] for u in UNITS)
NX = sum(COLS_PER_UNIT)
LEAD = 12
XR = 3
PR = 4
LAG = 2


def plan(last):
    steps = []
    row_at = NR + LEAD
    row_end = NG * NR if last else (NG + 1) * NR + LEAD
    pending = []
    clock = 0
    if not last:
        pending += [(1, ("stat", 0)), (2, ("stat", 1)), (2, ("scale", 0)), (3, ("scale", 1))]
        pending += [(4 + 2 * n, ("prep", k, c)) for n, (c, k) in enumerate(
            (c, k) for c in range(2) for k in ("norm", "q", "k", "v"))]

    def rows_to(n):
        nonlocal row_at
        while row_at < min(n, row_end):
            steps.append(("row", row_at // NR, row_at % NR))
            row_at += 1
            if row_at % NR == 0:
                pending.append((clock + 1, ("maxstat", row_at // NR - 1)))
                pending.append((clock + 2, ("max", row_at // NR - 1)))

    def due():
        for item in sorted([p for p in pending if p[0] <= clock], key=lambda p: p[0]):
            pending.remove(item)
            steps.append(item[1])

    for q in range(NG):
        done = 0
        for u in range(NU):
            w = UNITS[u][3]
            fills = COLS_PER_UNIT[u]
            for k in range(fills):
                steps.append(("exp", q, u, k))
                done += w * pack(w)
                if k < fills - 1 or u < NU - 1:
                    rows_to(NR * (q + 1) + LEAD + NR * done // AREA - (3 if u == NU - 1 else 0))
            if u >= LAG:
                steps.append(("pv", q, u - LAG))
                if u - LAG == 3:
                    pending.append((clock + 1, ("evac", q, 0)))
                    pending.append((clock + 2, ("norm", q, 0)))
            if u == NU - 1:
                rows_to(NR * (q + 1) + LEAD + NR - 2)
                steps.append(("pv", q, NU - 2))
                rows_to(NR * (q + 1) + LEAD + NR)
                steps.append(("pv", q, NU - 1))
                pending.append((clock + 1, ("evac", q, 1)))
                pending.append((clock + 2, ("norm", q, 1)))
            clock += 1
            due()
    clock += 100
    due()
    return steps


def first_rows():
    steps = [("row", 0, f) for f in range(NR)] + [("maxstat", 0)]
    steps += [("row", 1, f) for f in range(LEAD // 2)] + [("max", 0)]
    return steps + [("row", 1, f) for f in range(LEAD // 2, LEAD)]


PLAN = {last: plan(last) for last in (False, True)}
PREP = [(c, what) for c in range(2) for what in ("norm", "q", "k", "v")]
DIAG = [n for n in range(NU) if UNITS[n][1] // 4 == UNITS[n][0]]


def turn_numbers(last):
    uses = [s for s in PLAN[last] if s[0] in ("max", "norm", "prep")]
    return {s: n for n, s in enumerate(uses)}


TURN = {last: turn_numbers(last) for last in (False, True)}
LOOP_TURNS = len(TURN[False])
TURN0 = len(PREP) + 1
ALL_TURNS = TURN0 + (B - 1) * LOOP_TURNS + len(TURN[True])


def exp_banks():
    n = NG * NX
    last_user = {k % XR: k - n for k in range(n)}
    out = []
    for k in range(n):
        out.append((k % XR, last_user[k % XR]))
        last_user[k % XR] = k
    return out


XBANK = exp_banks()
SLOT_BYTES = 18 * 16
PART_BYTES = 3 * 16
PV_FREE = PR


def adaln_block(nc, x, qaT, kaT, qb, kb, vwT, owT, v_b, o_b, cT, wmod, gate_w, gate_b,
                up_w, up_b, down_w, down_b, sw_up, sb_up, sw_down, sb_down, out):
    parts_dram = nc.dram_tensor("qk_parts", [B, 2, 3, H, HD, T], BF16).ap()
    ctx = ExitStack()
    with ctx:
        def sb(name, shape, dt=F32):
            return ctx.enter_context(nc.sbuf_tensor(name, shape, dt))

        def sem(name):
            return ctx.enter_context(nc.semaphore(name))

        x_sb = sb("x_sb", [P, NT, D])
        y_all = sb("y_all", [P, NT, D])
        v_all = sb("v_all", [P, NT, D])
        QS = sb("QS", [P, NG * HG * T], BF16)
        KS = sb("KS", [P, NG * HG * T], BF16)
        probs = sb("probs", [P, PR * HG * CH])
        vg = sb("vg", [P, 2, TT, HG, 32])
        xn = sb("xn", [P, 2, 4, D])
        hT = sb("hT", [P, 2, CH])
        qf = sb("qf", [P, 2, CH])
        rest = sb("rest", [P, 2, CH])
        parts = sb("parts", [P, 2, 3, CH], BF16)
        o_sb = sb("o_sb", [P, 2, CH])
        stats = sb("stats", [P, 2, 4, 6])
        mv = sb("mv", [P, 2, 4, 2])
        rstd = sb("rstd", [P, 2, 4])
        mhalf = sb("mhalf", [P, NT])
        rowmax = sb("rowmax", [P, 2, HG, TT, 2])
        gmax = sb("gmax", [P, 2, HG * TT])
        grest = sb("grest", [P, 2, HG * TT])
        gparts = sb("gparts", [P, 2, 3, HG * TT], BF16)
        shift = sb("shift", [3 * HG * TT, 2, P], BF16)
        rden = sb("rden", [P, 2, 4 * HG])
        ident = sb("ident", [P, P])
        identb = sb("identb", [P, P], BF16)
        maskb = sb("maskb", [P, P], BF16)
        ones = sb("ones", [1, P])
        ones16 = sb("ones16", [16, T], BF16)
        wq = sb("wq", [P, D])
        wk = sb("wk", [P, D])
        wv = sb("wv", [P, D])
        wo = sb("wo", [P, D])
        wog = sb("wog", [P, B, D])
        vb_sb = sb("vb_sb", [1, D])
        ob_sb = sb("ob_sb", [1, D])
        obg = sb("obg", [1, B, D])
        cT_sb = sb("cT_sb", [P, B])
        silu = sb("silu", [P, 3, B])
        wm = sb("wm", [P, 6 * D])
        modT = sb("modT", [P, 6, B])
        modc = sb("modc", [P, 2])
        gates = sb("gates", [P, 2, B, D])
        gw = sb("gw", [P, E])
        gb_sb = sb("gb_sb", [1, E])
        ub = sb("ub", [P, NE, IT])
        db_sb = sb("db_sb", [NE, D])
        score = sb("score", [P, NT, E])
        below = sb("below", [P, E, E])
        rank = sb("rank", [P, NT, E])
        wsum = sb("wsum", [P, NT])
        wts = sb("wts", [P, NT, NE])
        st2 = sb("st2", [P, NT, 6])
        mv2 = sb("mv2", [P, NT, 2])
        rs2 = sb("rs2", [P, NT])
        amax = sb("amax", [P, 2, 4])
        QS4 = QS[:, :].rearrange("p (g h t) -> p g h t", g=NG, h=HG)
        KS4 = KS[:, :].rearrange("p (g h t) -> p g h t", g=NG, h=HG)
        pr4 = probs[:, :].rearrange("p (s h t) -> p s h t", s=PR, h=HG)
        qaT_sb = probs[:, 0:1024].rearrange("p (n d) -> p n d", n=8)
        kaT_sb = probs[:, 1024:2048].rearrange("p (n d) -> p n d", n=8)
        qbd = probs[:, 2048:2176].rearrange("p (n d) -> p n d", n=8)
        kbd = probs[:, 2176:2304].rearrange("p (n d) -> p n d", n=8)
        siluB = probs[:, 2304:2304 + B * P].rearrange("p (b m) -> p b m", b=B)
        gsign = probs[:, 2816:2816 + 2 * B * D].rearrange("p (j b d) -> p j b d", j=2, b=B)
        uw = QS[:, 0:NE * I * 2].bitcast(F32).rearrange("p (e i) -> p e i", e=NE)
        dw = KS[:, 0:NE * I * 2].bitcast(F32).rearrange("p (e c h) -> p e c h", e=NE, c=IT)
        spare = QS[:, NE * I * 2:].bitcast(F32)
        wT = spare[0:NE, 0:2 * CH].rearrange("e (s t) -> e s t", s=2)
        fin = spare[:, 2 * CH:4 * CH].rearrange("p (s n d) -> p s n d", s=2, n=4)
        yT = probs[:, 0:NT * P]
        xn2 = probs[:, NT * P:2 * NT * P].rearrange("p (n d) -> p n d", n=NT)
        h2T = v_all[:, :, :].rearrange("p n d -> p (n d)")
        acc = y_all
        hact = probs[:, 0:2 * IT * CH].rearrange("p (s c t) -> p s c t", s=2, c=IT)
        larger = probs[:, 4096:4096 + NT * E * E].rearrange("p (n e f) -> p n e f", n=NT, e=E)
        equal = probs[:, 6144:6144 + NT * E * E].rearrange("p (n e f) -> p n e f", n=NT, e=E)

        ps = [ctx.enter_context(nc.psum_tensor(f"bank{n}", [P, CH], F32)) for n in range(8)]
        row_bank, exp_bank, out_bank, turn_bank = ps[0:2], ps[2:5], ps[5:7], ps[7]
        turn_b16 = turn_bank[0:3 * HG * TT, 0:P // 2].bitcast(BF16)

        waited_pool = sem("waited_pool")
        waited_dve = sem("waited_dve")
        x_first = sem("x_first")
        x_rest = sem("x_rest")
        small_loaded = sem("small_loaded")
        lowrank_loaded = sem("lowrank_loaded")
        lowrank_zeroed = sem("lowrank_zeroed")
        consts_zeroed = sem("consts_zeroed")
        consts_made = sem("consts_made")
        vg_ready = sem("vg_ready")
        ones_stored = sem("ones_stored")
        ones_made = sem("ones_made")
        silu_exp = sem("silu_exp")
        silu_step = sem("silu_step")
        silu_done = sem("silu_done")
        qk_folded = sem("qk_folded")
        qk_copied = sem("qk_copied")
        mod_filled = sem("mod_filled")
        mod_step = sem("mod_step")
        mod_done = sem("mod_done")
        turn_filled = sem("turn_filled")
        turn_free = sem("turn_free")
        stat_step = sem("stat_step")
        var_done = sem("var_done")
        rstd_done = sem("rstd_done")
        norm_done = sem("norm_done")
        split_step = sem("split_step")
        split_done = sem("split_done")
        parts_stored = [sem("q_parts_stored"), sem("k_parts_stored")]
        slot_loaded = [sem(f"slot_loaded{q}") for q in range(NG)]
        shift_loaded = [sem(f"shift_loaded{q}") for q in range(NG)]
        vg_done = sem("vg_done")
        row_filled = sem("row_filled")
        row_free = sem("row_free")
        gmax_done = sem("gmax_done")
        gpart_step = sem("gpart_step")
        exp_filled = sem("exp_filled")
        exp_done = sem("exp_done")
        tri_done = sem("tri_done")
        pv_done = sem("pv_done")
        out_copied = sem("out_copied")
        rden_done = sem("rden_done")
        ffn_loaded = sem("ffn_loaded")
        bias_loaded = sem("bias_loaded")
        yt_filled = sem("yt_filled")
        yt_copied = sem("yt_copied")
        proj_filled = sem("proj_filled")
        x2_done = sem("x2_done")
        st2_done = sem("st2_done")
        var2_done = sem("var2_done")
        rs2_done = sem("rs2_done")
        xn2_done = sem("xn2_done")
        h2_filled = sem("h2_filled")
        h2_done = sem("h2_done")
        gate_filled = sem("gate_filled")
        gate_exp = sem("gate_exp")
        route_step = sem("route_step")
        wts_done = sem("wts_done")
        wt_filled = sem("wt_filled")
        wt_copied = sem("wt_copied")
        bias_filled = sem("bias_filled")
        acc_started = sem("acc_started")
        up_filled = sem("up_filled")
        act_done = sem("act_done")
        down_filled = sem("down_filled")
        acc_done = sem("acc_done")
        fin_step = sem("fin_step")
        fin_done = sem("fin_done")
        stored = sem("stored")

        block = ctx.enter_context(nc.Block())
        xt = x.rearrange("(n p) d -> p n d", p=P)
        ot = out.rearrange("(n p) d -> p n d", p=P)

        def batches(eng, body):
            with eng.Fori(0, B - 1) as b:
                body(b, False)
            body(B - 1, True)

        def turn(b, last, step):
            return TURN0 + LOOP_TURNS * b + TURN[last][step]

        def units(b, q):
            return NU * (NG * b + q) + PV_FREE

        def exps(b, q, u):
            return NX * (NG * b + q) + sum(COLS_PER_UNIT[:u + 1]) + XR

        @block.sync
        def _(sp):
            sp.dma_start(x_sb[:, 0:TT, :], xt[:, 0:TT, :]).then_inc(x_first, 16)
            sp.wait_ge(ones_made, 2)
            for r in range(KA, KB):
                sp.dma_start(KS[r:r + 1, :], ones16[:, :]).then_inc(ones_stored, 16)
            sp.dma_start(cT_sb[:, :], cT).then_inc(small_loaded, 16)
            sp.dma_start(wm[:, :], wmod).then_inc(small_loaded, 16)
            sp.dma_start(wv[:, :], vwT).then_inc(small_loaded, 16)
            sp.dma_start(wo[:, :], owT).then_inc(small_loaded, 16)
            sp.dma_start(vb_sb[:, :], v_b).then_inc(small_loaded, 16)
            sp.dma_start(ob_sb[:, :], o_b).then_inc(small_loaded, 16)
            sp.dma_start(gw[:, :], gate_w).then_inc(small_loaded, 16)
            sp.dma_start(gb_sb[:, :], gate_b).then_inc(small_loaded, 16)
            sp.dma_start(x_sb[:, TT:NT, :], xt[:, TT:NT, :]).then_inc(x_rest, 16)
            sp.dma_start(ub[:, 0:E, :], up_b).then_inc(bias_loaded, 16)
            sp.dma_start(ub[:, E, :], sb_up).then_inc(bias_loaded, 16)
            sp.dma_start(db_sb[0:E, :], down_b).then_inc(bias_loaded, 16)
            sp.dma_start(db_sb[E:NE, :], sb_down).then_inc(bias_loaded, 16)

            def store_parts(b, c, side):
                sp.wait_ge(split_done, 2 * (2 * b + c) + side + 1)
                for part in range(3):
                    dst = parts_dram[bass.ds(b, 1), side, part, :, :, CH * c:CH * c + CH]
                    sp.dma_start(dst.rearrange("b h d t -> (b h d) t"), parts[:, side, part, :])\
                      .then_inc(parts_stored[side], 16)

            def load_slot(b, q):
                for i in range(3):
                    for j in range(3):
                        r = HD * (3 * i + j)
                        for side, part, rows in ((0, i, QS4), (1, j, KS4)):
                            src = parts_dram[bass.ds(b, 1), side, part, HG * q:HG * q + HG, :, :]
                            sp.dma_start(rows[r:r + HD, q, :, :], src.rearrange("b h d t -> d (b h) t"))\
                              .then_inc(slot_loaded[q], 16)

            def store_shift(b, q, t):
                sp.wait_ge(turn_free, t + 1)
                for part in range(3):
                    sp.dma_start(QS4[KA + part:KA + part + 1, q % NG, :, :],
                                 shift[part * HG * TT:(part + 1) * HG * TT, q % 2, :])\
                      .then_inc(shift_loaded[q % NG], 16)

            for c in range(2):
                for side in range(2):
                    store_parts(0, c, side)
            for side in range(2):
                sp.wait_ge(parts_stored[side], 2 * PART_BYTES)
            for q in range(NG):
                load_slot(0, q)
            store_shift(0, 0, TURN0 - 1)

            def body(b, last):
                for s in PLAN[last]:
                    if s[0] == "max":
                        store_shift(b, s[1], turn(b, last, s))
                    elif s[0] == "prep" and s[1] in ("q", "k"):
                        store_parts(b + 1, s[2], "qk".index(s[1]))
                    elif s[0] == "exp" and s[2:] == (0, 0) and s[1] >= 1 and not last:
                        q = s[1] - 1
                        if q >= 1:
                            sp.wait_ge(exp_filled, NX * (NG * b + q + 1))
                            load_slot(b + 1, q)
                    if not last and s == ("exp", 1, 8, 0):
                        for side in range(2):
                            sp.wait_ge(parts_stored[side], 2 * PART_BYTES * (b + 2))
                        sp.wait_ge(exp_filled, NX * (NG * b + 1))
                        load_slot(b + 1, 0)
                if not last:
                    sp.wait_ge(exp_filled, NX * NG * (b + 1))
                    load_slot(b + 1, NG - 1)

            batches(sp, body)
            sp.wait_ge(exp_filled, NX * NG * B)
            sp.wait_ge(row_filled, NR * NG * B)
            sp.dma_start(uw[:, 0:E, :], up_w).then_inc(ffn_loaded, 16)
            sp.dma_start(uw[:, E, :], sw_up).then_inc(ffn_loaded, 16)
            for e in range(E):
                sp.dma_start(dw[:, e, :, :], down_w[e, :, :].rearrange("(c p) h -> p c h", p=P)).then_inc(ffn_loaded, 16)
            sp.dma_start(dw[:, E, :, :], sw_down.rearrange("(c p) h -> p c h", p=P)).then_inc(ffn_loaded, 16)
            with sp.Fori(0, B) as b:
                for cc in range(2):
                    sp.wait_ge(fin_done, 2 * b + cc + 1)
                    sp.dma_start(ot[:, bass.ds(TT * b + 4 * cc, 4), :], fin[:, cc, :, :]).then_inc(stored, 16)
            sp.wait_ge(stored, 16 * (NC + 1))

        @block.gpsimd
        def _(pool):
            pool.memset(ident[:, :], 0.0).then_inc(consts_zeroed, 1)
            pool.memset(identb[:, :], 0.0).then_inc(consts_zeroed, 1)
            pool.memset(maskb[:, :], 0.0).then_inc(consts_zeroed, 1)
            pool.memset(below[:, :, :], 1.0).then_inc(consts_zeroed, 1)
            pool.memset(mhalf[:, :], -0.5).then_inc(consts_zeroed, 1)
            pool.memset(vg[:, :, :, :, :], 0.0).then_inc(consts_zeroed, 1)
            pool.wait_ge(consts_zeroed, 6)
            for m in (ident, identb):
                pool.affine_select(out=m[:, :], in_=m[:, :], compare_op=ALU.not_equal, fill=1.0, base=0,
                                   pattern=[[-1, P]], channel_multiplier=1).then_inc(consts_made, 1)
            pool.affine_select(out=maskb[:, :], in_=maskb[:, :], compare_op=ALU.is_ge, fill=NEG, base=0,
                               pattern=[[-1, P]], channel_multiplier=1).then_inc(consts_made, 1)
            pool.affine_select(out=below[:, :, :], in_=below[:, :, :], compare_op=ALU.is_gt, fill=0.0, base=0,
                               pattern=[[1, E], [-1, E]], channel_multiplier=0).then_inc(consts_made, 1)
            pool.memset(vg[:, :, :, :, HD:HD + 1], 1.0).then_inc(vg_ready, 1)

            def norm(b, c):
                m = 2 * b + c
                pool.wait_ge(var_done, m + 1)
                pool.tensor_tensor(rstd[:, c, :], rstd[:, c, :], mhalf[:, 0:4], ALU.pow).then_inc(rstd_done, 1)
            def split(b, c, side, t):
                k = 2 * (2 * b + c) + side
                pool.wait_ge(turn_free, t + 1)
                pool.tensor_tensor(rest[:, side, :], qf[:, side, :], parts[:, side, 0, :], ALU.subtract)\
                    .then_inc(split_step, 1)
                pool.wait_ge(split_step, 2 * k + 1)
                pool.sem_inc(waited_pool, 1)
                pool.tensor_copy(parts[:, side, 1, :], rest[:, side, :]).then_inc(split_step, 1)
                pool.wait_ge(split_step, 2 * k + 2)
                pool.tensor_tensor(parts[:, side, 2, :], rest[:, side, :], parts[:, side, 1, :], ALU.subtract)\
                    .then_inc(split_done, 1)

            def group_v(b, q):
                pool.sem_inc(waited_pool, 1)
                for j in range(TT):
                    last = pool.tensor_copy(
                        vg[:, q % 2, j, :, 0:HD],
                        v_all[:, bass.ds(TT * b + j, 1), 32 * q:32 * q + 32].rearrange("p n (h d) -> p (n h) d", h=HG))
                last.then_inc(vg_done, 1)

            def maxima(b, q):
                n, r = NG * b + q, q % 2
                pool.wait_ge(gmax_done, n + 1)
                pool.sem_inc(waited_pool, 1)
                pool.tensor_scalar(gparts[:, r, 0, :], gmax[:, r, :], -1.0, None, ALU.mult).then_inc(gpart_step, 1)
                pool.tensor_scalar(grest[:, r, :], gmax[:, r, :], -1.0, None, ALU.mult).then_inc(gpart_step, 1)
                pool.wait_ge(gpart_step, 5 * n + 2)
                pool.tensor_tensor(grest[:, r, :], grest[:, r, :], gparts[:, r, 0, :], ALU.subtract)\
                    .then_inc(gpart_step, 1)
                pool.wait_ge(gpart_step, 5 * n + 3)
                pool.sem_inc(waited_pool, 1)
                pool.tensor_copy(gparts[:, r, 1, :], grest[:, r, :]).then_inc(gpart_step, 1)
                pool.wait_ge(gpart_step, 5 * n + 4)
                pool.tensor_tensor(gparts[:, r, 2, :], grest[:, r, :], gparts[:, r, 1, :], ALU.subtract)\
                    .then_inc(gpart_step, 1)

            pool.wait_ge(x_first, 16)
            norm(0, 0)
            norm(0, 1)
            for t, (c, what) in enumerate(PREP):
                if what in ("q", "k"):
                    split(0, c, "qk".index(what), t)
            pool.wait_ge(vg_ready, 1)
            pool.wait_ge(turn_free, len(PREP))
            group_v(0, 0)
            maxima(0, 0)
            pool.wait_ge(x_rest, 16)

            def body(b, last):
                for s in PLAN[last]:
                    if s[0] == "exp":
                        _, q, u, k = s
                        if (u, k) == (2, 0) and q < NG - 1:
                            pool.wait_ge(pv_done, units(b, q))
                            group_v(b, q + 1)
                        if u in DIAG and k == COLS_PER_UNIT[u] - 1:
                            pool.wait_ge(exp_done, exps(b, q, u))
                            pool.sem_inc(waited_pool, 1)
                            pool.affine_select(out=pr4[:, u % PR, :, 0:P], in_=pr4[:, u % PR, :, 0:P],
                                               compare_op=ALU.is_ge, fill=0.0, base=0,
                                               pattern=[[0, HG], [1, P]], channel_multiplier=-1)\
                                .then_inc(tri_done, 1)
                    elif s[0] == "maxstat":
                        maxima(b, s[1])
                    elif s[0] == "stat":
                        norm(b + 1, s[1])
                    elif s[0] == "prep":
                        _, what, c = s
                        if what in ("q", "k"):
                            split(b + 1, c, "qk".index(what), turn(b, last, s))
                if not last:
                    pool.wait_ge(turn_free, turn(b, last, ("prep", "v", 1)) + 1)
                    pool.wait_ge(pv_done, units(b, NG - 1))
                    group_v(b + 1, 0)

            batches(pool, body)
            pool.wait_ge(var2_done, 1)
            pool.tensor_tensor(rs2[:, :], rs2[:, :], mhalf[:, :], ALU.pow).then_inc(rs2_done, 1)

        @block.scalar
        def _(act):
            act.dma_start(qaT_sb, qaT).then_inc(lowrank_loaded, 16)
            act.dma_start(kaT_sb, kaT).then_inc(lowrank_loaded, 16)
            act.wait_ge(lowrank_zeroed, 1)
            for dst, src in ((qbd, qb), (kbd, kb)):
                for h2 in range(2):
                    act.dma_start(dst[R * h2:R * h2 + R, :, HD * h2:HD * h2 + HD], src[R * h2:R * h2 + R, :, :])\
                        .then_inc(lowrank_loaded, 16)
            act.wait_ge(small_loaded, 16 * 8)
            act.activation(silu[:, 0, :], cT_sb[:, :], ACT.Exp, scale=-1.0).then_inc(silu_exp, 1)

            def prep_read(b, c, what, t, first=False):
                act.wait_ge(turn_filled, t + 1)
                if what == "norm":
                    act.activation(hT[:, c, :], turn_bank[:, :], ACT.Identity, bias=modc[:, 0:1], scale=modc[:, 1:2])\
                        .then_inc(turn_free, 1)
                elif what == "v":
                    act.activation(v_all[:, bass.ds(TT * b + 4 * c, 4), :],
                                   turn_bank[:, :].rearrange("p (n d) -> p n d", n=4), ACT.Copy).then_inc(turn_free, 1)
                else:
                    side = "qk".index(what)
                    if not first:
                        act.wait_ge(split_done, 2 * (2 * b + c) + side - 1)
                        act.wait_ge(parts_stored[side], PART_BYTES * (2 * b + c))
                    scale = SCALE if what == "q" else 1.0
                    act.activation(qf[:, side, :], turn_bank[:, :], ACT.Copy, scale=scale)
                    act.activation(parts[:, side, 0, :], turn_bank[:, :], ACT.Copy, scale=scale).then_inc(turn_free, 1)

            def max_read(q, t):
                act.wait_ge(turn_filled, t + 1)
                act.activation(shift[:, q % 2, :], turn_b16, ACT.Copy).then_inc(turn_free, 1)

            act.wait_ge(mod_done, 1)
            for t, (c, what) in enumerate(PREP):
                prep_read(0, c, what, t, first=(c == 0))
            max_read(0, TURN0 - 1)

            def body(b, last):
                nx = 0
                for s in PLAN[last]:
                    if s[0] == "exp":
                        _, q, u, k = s
                        w = UNITS[u][3]
                        h = k * pack(w)
                        if k == 0:
                            act.wait_ge(pv_done, units(b, q) + u + 1 - PR)
                        act.wait_ge(exp_filled, NG * NX * b + nx + 1)
                        act.activation(pr4[:, u % PR, h:h + pack(w), 0:w],
                                       exp_bank[XBANK[nx][0]][:, 0:w * pack(w)].rearrange(
                                           "p (h t) -> p h t", h=pack(w)), ACT.Exp).then_inc(exp_done, 1)
                        nx += 1
                    elif s[0] == "evac":
                        _, q, c = s
                        act.wait_ge(pv_done, units(b, q) + (4 if c == 0 else NU))
                        act.activation(o_sb[:, c, :], out_bank[c][:, :], ACT.Copy).then_inc(out_copied, 1)
                    elif s[0] == "max":
                        max_read(s[1], turn(b, last, s))
                    elif s[0] == "prep":
                        prep_read(b + 1, s[2], s[1], turn(b, last, s))

            batches(act, body)
            for c in range(NC):
                act.wait_ge(yt_filled, c + 1)
                act.activation(yT[:, CH * c:CH * c + CH], ps[c % 2][:, :], ACT.Copy).then_inc(yt_copied, 1)
            for c in range(NC):
                b = c // 2
                act.wait_ge(h2_filled, c + 1)
                act.activation(h2T[:, CH * c:CH * c + CH], ps[4 + c % 2][:, :], ACT.Identity,
                               bias=modT[:, 3, b:b + 1], scale=modT[:, 4, b:b + 1]).then_inc(h2_done, 1)
            act.wait_ge(gate_filled, 1)
            act.activation(score[:, :, :], ps[6][:, 0:NT * E].rearrange("p (n e) -> p n e", n=NT), ACT.Exp,
                           scale=-1.0).then_inc(gate_exp, 1)
            for c in range(NC):
                act.wait_ge(wt_filled, c + 1)
                if c >= 2:
                    act.wait_ge(bias_filled, c - 1)
                act.activation(wT[:, c % 2, :], ps[c % 2][0:NE, :], ACT.Copy).then_inc(wt_copied, 1)
            act.wait_ge(bias_loaded, 64)
            with act.Fori(0, B) as b:
                for n in range(2 * NE):
                    e = n % NE
                    act.wait_ge(down_filled, 2 * NE * b + n + 1)
                    for i in range(IT):
                        act.wait_ge(up_filled, IT * (2 * NE * b + n) + i + 1)
                        act.activation(hact[:, n % 2, i, :], ps[i][:, :], ACT.Gelu, bias=ub[:, e, i:i + 1])\
                            .then_inc(act_done, 1)

        @block.tensor
        def _(pe):
            mm, tr = nc.tensor.matmul, nc.tensor.transpose
            pe.wait_ge(lowrank_loaded, 16 * 6)
            for side, (a, bd) in enumerate(((qaT_sb, qbd), (kaT_sb, kbd))):
                for n in range(8):
                    m = mm(ps[0][:, D * side + 16 * n:D * side + 16 * n + 16], a[:, n, :], bd[:, n, :],
                           start=True, stop=True)
            m.then_inc(qk_folded, 1)
            pe.wait_ge(silu_done, 1)
            for j in range(6):
                mm(ps[1][:, B * j:B * j + B], wm[:, D * j:D * j + D], silu[:, 2, :], start=True, stop=True)
            for j in range(2):
                for b in range(B):
                    m = mm(ps[2 + j][:, D * b:D * b + D], siluB[:, b, :], wm[:, D * (3 * j + 2):D * (3 * j + 3)],
                           start=True, stop=True)
            m.then_inc(mod_filled, 1)
            pe.wait_ge(consts_made, 4)
            pe.wait_ge(ones_made, 2)
            pe.wait_ge(ones_stored, 48)

            def prep(b, c, what, t):
                m = 2 * b + c
                if t is not None:
                    pe.wait_ge(turn_free, t)
                if what == "norm":
                    pe.wait_ge(norm_done, m + 1)
                    for n in range(4):
                        last = tr(turn_bank[:, P * n:P * n + P], xn[:, c, n, :], ident[:, :])
                elif what == "v":
                    for n in range(4):
                        mm(turn_bank[:, P * n:P * n + P], hT[:, c, P * n:P * n + P], wv[:, :], start=True, stop=False)
                        last = mm(turn_bank[:, P * n:P * n + P], ones[:, :], vb_sb[:, :], start=False, stop=True)
                else:
                    last = mm(turn_bank[:, :], (wq if what == "q" else wk)[:, :], hT[:, c, :], start=True, stop=True)
                last.then_inc(turn_filled, 1)

            pe.wait_ge(qk_copied, 2)
            for t, (c, what) in enumerate(PREP):
                prep(0, c, what, t if t else None)

            def rows(b, q, f, before):
                i, c0, w, h0, nh = ROWS[f]
                if f == 0:
                    pe.wait_ge(slot_loaded[q % NG], SLOT_BYTES * (b + 1))
                if before is not None:
                    pe.wait_ge(row_free, before)
                bank = row_bank[f % 2]
                diagonal = c0 + w == P * (i + 1)
                for n in range(nh):
                    m = mm(bank[:, w * n:w * n + w], QS4[0:KA, q % NG, h0 + n, P * i:P * i + P],
                           KS4[0:KA, q % NG, h0 + n, c0:c0 + w], start=True, stop=not diagonal)
                    if diagonal:
                        m = mm(bank[:, w * n + w - P:w * n + w], identb[:, :], maskb[:, :],
                               start=False, stop=True)
                m.then_inc(row_filled, 1)

            def max_turn(b, q, t):
                pe.wait_ge(gpart_step, 5 * (NG * b + q) + 5)
                pe.wait_ge(turn_free, t)
                tr(turn_b16, gparts[:, q % 2, :, :].rearrange("p a n -> p (a n)"), identb[:, :])\
                    .then_inc(turn_filled, 1)

            for s in first_rows():
                if s[0] == "row":
                    n = NR * s[1] + s[2]
                    rows(0, s[1], s[2], n - 1 if n >= 2 else None)
                elif s[0] == "max":
                    max_turn(0, 0, TURN0 - 1)

            def body(b, last):
                nx = 0
                for s in PLAN[last]:
                    if s[0] == "row":
                        _, q, f = s
                        rows(b + q // NG, q, f, NR * (NG * b + q) + f - 1)
                    elif s[0] == "exp":
                        _, q, u, k = s
                        c, j, t0, w = UNITS[u]
                        h = k * pack(w)
                        if (u, k) == (0, 0):
                            pe.wait_ge(shift_loaded[q], PART_BYTES * (b + 1))
                        bank, user = XBANK[nx]
                        pe.wait_ge(exp_done, NG * NX * b + user + 1 + XR)
                        for n in range(pack(w)):
                            m = mm(exp_bank[bank][:, w * n:w * n + w], KS4[0:KB, q, h + n, P * j:P * j + P],
                                   QS4[0:KB, q, h + n, t0:t0 + w], start=True, stop=True)
                        m.then_inc(exp_filled, 1)
                        nx += 1
                    elif s[0] == "pv":
                        _, q, u = s
                        c, j, t0, w = UNITS[u]
                        if u == 0:
                            pe.wait_ge(vg_done, NG * b + q + 1)
                        if j == 0:
                            pe.wait_ge(out_copied, 2 * (NG * b + q) + c + 1)
                        if u in DIAG:
                            pe.wait_ge(tri_done, len(DIAG) * (NG * b + q) + DIAG.index(u) + 1)
                        else:
                            pe.wait_ge(exp_done, exps(b, q, u))
                        for h in range(HG):
                            m = mm(out_bank[c][32 * h:32 * h + 32, t0 - CH * c:CH], vg[:, q % 2, j, h, :],
                                   pr4[:, u % PR, h, 0:w], start=(j == 0), stop=(j == 4 * c + 3))
                        m.then_inc(pv_done, 1)
                    elif s[0] == "max":
                        max_turn(b, s[1], turn(b, last, s))
                    elif s[0] == "norm":
                        _, q, c = s
                        pe.wait_ge(out_copied, 2 * (NG * b + q) + c + 1 + 2)
                        pe.wait_ge(turn_free, turn(b, last, s))
                        for n in range(4):
                            m = tr(turn_bank[:, P * n:P * n + P], o_sb[:, c, P * n:P * n + P], ident[:, :])
                        m.then_inc(turn_filled, 1)
                    elif s[0] == "prep":
                        prep(b + 1, s[2], s[1], turn(b, last, s))

            batches(pe, body)

            pe.wait_ge(turn_free, ALL_TURNS)
            for c in range(NC):
                if c >= 2:
                    pe.wait_ge(yt_copied, c - 1)
                for n in range(4):
                    m = tr(ps[c % 2][:, P * n:P * n + P], y_all[:, 4 * c + n, :], ident[:, :])
                m.then_inc(yt_filled, 1)
            for c in range(NC):
                pe.wait_ge(yt_copied, c + 1)
                if c >= 2:
                    pe.wait_ge(x2_done, c - 1)
                for n in range(4):
                    mm(ps[2 + c % 2][:, P * n:P * n + P], yT[:, CH * c + P * n:CH * c + P * n + P], wog[:, c // 2, :],
                       start=True, stop=False)
                    m = mm(ps[2 + c % 2][:, P * n:P * n + P], ones[:, :], obg[:, c // 2, :], start=False, stop=True)
                m.then_inc(proj_filled, 1)
            for c in range(NC):
                pe.wait_ge(xn2_done, c + 1)
                if c >= 2:
                    pe.wait_ge(h2_done, c - 1)
                for n in range(4):
                    m = tr(ps[4 + c % 2][:, P * n:P * n + P], xn2[:, 4 * c + n, :], ident[:, :])
                m.then_inc(h2_filled, 1)
            for n in range(NT):
                pe.wait_ge(h2_done, n // 4 + 1)
                mm(ps[6][:, E * n:E * n + E], h2T[:, P * n:P * n + P], gw[:, :], start=True, stop=False)
                m = mm(ps[6][:, E * n:E * n + E], ones[:, :], gb_sb[:, :], start=False, stop=True)
            m.then_inc(gate_filled, 1)
            pe.wait_ge(wts_done, 2)
            pe.wait_ge(bias_loaded, 64)
            for c in range(NC):
                if c >= 2:
                    pe.wait_ge(wt_copied, c - 1)
                for n in range(4):
                    m = tr(ps[c % 2][0:NE, P * n:P * n + P], wts[:, 4 * c + n, :], ident[:, :])
                m.then_inc(wt_filled, 1)
                if c >= 2:
                    pe.wait_ge(acc_started, c - 1)
                pe.wait_ge(wt_copied, c + 1)
                for n in range(4):
                    m = mm(ps[2 + c % 2][:, P * n:P * n + P], wT[:, c % 2, P * n:P * n + P], db_sb[:, :],
                           start=True, stop=True)
                m.then_inc(bias_filled, 1)
            pe.wait_ge(acc_started, NC)
            pe.wait_ge(ffn_loaded, 16 * (3 + E))
            with pe.Fori(0, B) as b:
                def up(n):
                    for i in range(IT):
                        pe.wait_ge(act_done, IT * (2 * NE * b + n) + i + 1)
                        mm(ps[i][:, :], uw[:, n % NE, P * i:P * i + P], h2T[:, bass.ds(T * b + CH * (n // NE), CH)],
                           start=True, stop=True).then_inc(up_filled, 1)

                up(0)
                for n in range(2 * NE):
                    if n + 1 < 2 * NE:
                        up(n + 1)
                    pe.wait_ge(act_done, IT * (2 * NE * b + n) + IT + IT)
                    pe.wait_ge(acc_done, 2 * NE * b + n + 1)
                    for t in range(4):
                        for i in range(IT):
                            m = mm(ps[4 + n % 2][:, P * t:P * t + P], hact[:, n % 2, i, P * t:P * t + P],
                                   dw[:, n % NE, i, :], start=(i == 0), stop=(i == IT - 1))
                    m.then_inc(down_filled, 1)

        @block.vector
        def _(dve):
            dve.memset(probs[:, 2048:2304], 0.0).then_inc(lowrank_zeroed, 1)
            dve.memset(ones16[:, :], 1.0).then_inc(ones_made, 1)
            dve.memset(ones[:, :], 1.0).then_inc(ones_made, 1)

            def stat(b, c):
                m = 2 * b + c
                for t in range(4):
                    ins = dve.bn_stats(stats[:, c, t, :], x_sb[:, bass.ds(TT * b + 4 * c + t, 1), :].rearrange(
                        "p n d -> p (n d)"))
                ins.then_inc(stat_step, 1)
                dve.wait_ge(stat_step, 2 * m + 1)
                dve.sem_inc(waited_dve, 1)
                for t in range(4):
                    ins = dve.bn_aggr(mv[:, c, t, :], stats[:, c, t, :])
                ins.then_inc(stat_step, 1)
                dve.wait_ge(stat_step, 2 * m + 2)
                dve.tensor_scalar(rstd[:, c, :], mv[:, c, :, 1:2].rearrange("p n a -> p (n a)"), EPS, None, ALU.add)\
                    .then_inc(var_done, 1)

            def norm(b, c):
                dve.wait_ge(rstd_done, 2 * b + c + 1)
                for t in range(4):
                    ins = dve.tensor_scalar(xn[:, c, t, :], x_sb[:, bass.ds(TT * b + 4 * c + t, 1), :].rearrange(
                        "p n d -> p (n d)"), mv[:, c, t, 0:1], rstd[:, c, t:t + 1], ALU.subtract, ALU.mult)
                ins.then_inc(norm_done, 1)

            dve.wait_ge(x_first, 16)
            stat(0, 0)
            stat(0, 1)
            norm(0, 0)
            norm(0, 1)
            dve.memset(rowmax[:, :, :, :, :], -3.0e38)
            dve.wait_ge(silu_exp, 1)
            dve.tensor_scalar(silu[:, 1, :], silu[:, 0, :], 1.0, None, ALU.add).then_inc(silu_step, 1)
            dve.wait_ge(silu_step, 1)
            dve.reciprocal(silu[:, 0, :], silu[:, 1, :]).then_inc(silu_step, 1)
            dve.wait_ge(silu_step, 2)
            dve.tensor_tensor(silu[:, 2, :], silu[:, 0, :], cT_sb[:, :], ALU.mult).then_inc(silu_step, 1)
            dve.wait_ge(silu_step, 3)
            dve.tensor_copy(siluB[:, :, :], silu[:, 2, :].unsqueeze(2).broadcast_to([P, B, P])).then_inc(silu_done, 1)
            dve.wait_ge(qk_folded, 1)
            dve.tensor_copy(wq[:, :], ps[0][:, 0:D]).then_inc(qk_copied, 1)
            dve.tensor_copy(wk[:, :], ps[0][:, D:2 * D]).then_inc(qk_copied, 1)
            dve.wait_ge(mod_filled, 1)
            dve.tensor_copy(modT[:, :, :], ps[1][:, 0:6 * B].rearrange("p (j b) -> p j b", j=6)).then_inc(mod_step, 1)
            dve.wait_ge(mod_step, 1)
            dve.tensor_scalar(modT[:, 1:5:3, :], modT[:, 1:5:3, :], 1.0, None, ALU.add).then_inc(mod_step, 1)
            dve.wait_ge(mod_step, 2)
            dve.tensor_copy(modc[:, :], modT[:, 0:2, 0:1].rearrange("p j b -> p (j b)")).then_inc(mod_done, 1)
            gate_flat = gates[:, :, :, :].rearrange("p j b d -> p j (b d)")
            sign_flat = gsign[:, :, :, :].rearrange("p j b d -> p j (b d)")
            for j in range(2):
                dve.tensor_scalar(sign_flat[:, j], ps[2 + j][:, :], 0.0, 2.0, ALU.is_ge, ALU.mult).then_inc(mod_step, 1)
            dve.wait_ge(mod_step, 4)
            for j in range(2):
                dve.scalar_tensor_tensor(out=gate_flat[:, j], in0=sign_flat[:, j], scalar=-1.0, in1=ps[2 + j][:, :],
                                         op0=ALU.add, op1=ALU.mult).then_inc(mod_step, 1)
            dve.wait_ge(mod_step, 6)
            dve.tensor_scalar(gate_flat[:, :], gate_flat[:, :], 0.25, None, ALU.max).then_inc(mod_step, 1)
            dve.wait_ge(mod_step, 7)
            dve.scalar_tensor_tensor(out=gate_flat[:, :], in0=sign_flat[:, :], scalar=-1.0, in1=gate_flat[:, :],
                                     op0=ALU.add, op1=ALU.mult).then_inc(mod_step, 1)
            dve.wait_ge(mod_step, 8)
            dve.tensor_tensor(wog[:, :, :], gates[:, 0, :, :], wo[:, :].unsqueeze(1).broadcast_to([P, B, D]), ALU.mult)
            dve.tensor_tensor(obg[:, :, :], gates[0:1, 0, :, :], ob_sb[:, :].unsqueeze(1).broadcast_to([1, B, D]),
                              ALU.mult)
            for free, count in ((exp_done, XR), (pv_done, PV_FREE), (out_copied, 2), (act_done, IT), (acc_done, 2),
                                (down_filled, 2), (stored, 16)):
                dve.sem_inc(free, count)
            dve.memset(wts[:, :, E:NE], 1.0)

            def row_max(b, q, f):
                i, c0, w, h0, nh = ROWS[f]
                n = NR * (NG * b + q) + f
                dve.wait_ge(row_filled, n + 1)
                dve.tensor_reduce(rowmax[:, q % 2, h0:h0 + nh, i, c0 // CH], row_bank[f % 2][:, 0:w * nh].rearrange(
                    "p (h s) -> p h s", h=nh), AX.X, ALU.max).then_inc(row_free, 1)

            def group_max(b, q):
                n, r = NG * b + q, q % 2
                dve.wait_ge(row_free, NR * (n + 1))
                m = rowmax[:, r, :, :, :].rearrange("p h i c -> p (h i) c")
                dve.tensor_tensor(gmax[:, r, :], m[:, :, 0], m[:, :, 1], ALU.max).then_inc(gmax_done, 1)

            for s in first_rows():
                if s[0] == "row":
                    row_max(0, s[1], s[2])
                elif s[0] == "maxstat":
                    group_max(0, 0)
            dve.wait_ge(x_rest, 16)

            def body(b, last):
                for s in PLAN[last]:
                    if s[0] == "row":
                        row_max(b, s[1], s[2])
                    elif s[0] == "maxstat":
                        group_max(b, s[1])
                    elif s[0] == "stat":
                        if s[1] == 0:
                            dve.tensor_copy(modc[:, :], modT[:, 0:2, bass.ds(b + 1, 1)].rearrange("p j b -> p (j b)"))
                        stat(b + 1, s[1])
                    elif s[0] == "scale":
                        norm(b + 1, s[1])
                    elif s[0] == "norm":
                        _, q, c = s
                        dve.wait_ge(turn_filled, turn(b, last, s) + 1)
                        o = turn_bank[:, :].rearrange("p (n h k) -> p n h k", n=4, h=HG)
                        dve.reciprocal(rden[:, c, :].rearrange("p (n h) -> p n h", n=4), o[:, :, :, HD])\
                            .then_inc(rden_done, 1)
                        dve.wait_ge(rden_done, 2 * (NG * b + q) + c + 1)
                        dve.tensor_tensor(
                            y_all[:, bass.ds(TT * b + 4 * c, 4), 32 * q:32 * q + 32].rearrange(
                                "p n (h d) -> p n h d", h=HG), o[:, :, :, 0:HD],
                            rden[:, c, :].rearrange("p (n h) -> p n h", n=4).unsqueeze(3).broadcast_to([P, 4, HG, HD]),
                            ALU.mult).then_inc(turn_free, 1)

            batches(dve, body)

            for c in range(NC):
                dve.wait_ge(proj_filled, c + 1)
                xc = x_sb[:, 4 * c:4 * c + 4, :].rearrange("p n d -> p (n d)")
                dve.tensor_tensor(xc, ps[2 + c % 2][:, :], xc, ALU.add).then_inc(x2_done, 1)
            for n in range(NT):
                if n % 4 == 0:
                    dve.wait_ge(x2_done, n // 4 + 1)
                dve.bn_stats(st2[:, n, :], x_sb[:, n, :]).then_inc(st2_done, 1)
            for n in range(NT):
                dve.wait_ge(st2_done, n + 1)
                ins = dve.bn_aggr(mv2[:, n, :], st2[:, n, :])
            ins.then_inc(st2_done, 1)
            dve.wait_ge(st2_done, NT + 1)
            dve.tensor_scalar(rs2[:, :], mv2[:, :, 1], EPS, None, ALU.add).then_inc(var2_done, 1)
            dve.wait_ge(rs2_done, 1)
            for n in range(NT):
                ins = dve.tensor_scalar(xn2[:, n, :], x_sb[:, n, :], mv2[:, n, 0:1], rs2[:, n:n + 1],
                                        ALU.subtract, ALU.mult)
                if n % 4 == 3:
                    ins.then_inc(xn2_done, 1)
            dve.wait_ge(gate_exp, 1)
            dve.tensor_scalar(score[:, :, :], score[:, :, :], 1.0, None, ALU.add).then_inc(route_step, 1)
            dve.wait_ge(route_step, 1)
            dve.reciprocal(score[:, :, :], score[:, :, :]).then_inc(route_step, 1)
            dve.wait_ge(route_step, 2)
            other = score[:, :, :].unsqueeze(2).broadcast_to([P, NT, E, E])
            own = score[:, :, :].unsqueeze(3).broadcast_to([P, NT, E, E])
            dve.tensor_tensor(larger, other, own, ALU.is_gt).then_inc(route_step, 1)
            dve.tensor_tensor(equal, other, own, ALU.is_equal).then_inc(route_step, 1)
            dve.wait_ge(route_step, 4)
            dve.tensor_tensor(equal, equal, below[:, :, :].unsqueeze(1).broadcast_to([P, NT, E, E]), ALU.mult)\
                .then_inc(route_step, 1)
            dve.wait_ge(route_step, 5)
            dve.tensor_tensor(larger, larger, equal, ALU.add).then_inc(route_step, 1)
            dve.wait_ge(route_step, 6)
            dve.tensor_reduce(rank[:, :, :], larger, AX.X, ALU.add).then_inc(route_step, 1)
            dve.wait_ge(route_step, 7)
            dve.scalar_tensor_tensor(out=rank[:, :, :].rearrange("p n e -> p (n e)"),
                                     in0=rank[:, :, :].rearrange("p n e -> p (n e)"), scalar=1.5,
                                     in1=score[:, :, :].rearrange("p n e -> p (n e)"),
                                     op0=ALU.is_lt, op1=ALU.mult).then_inc(route_step, 1)
            dve.wait_ge(route_step, 8)
            dve.tensor_reduce(wsum[:, :], rank[:, :, :], AX.X, ALU.add).then_inc(route_step, 1)
            dve.wait_ge(route_step, 9)
            dve.tensor_scalar(wsum[:, :], wsum[:, :], 1e-6, None, ALU.add).then_inc(route_step, 1)
            dve.wait_ge(route_step, 10)
            dve.reciprocal(wsum[:, :], wsum[:, :]).then_inc(route_step, 1)
            dve.wait_ge(route_step, 11)
            dve.tensor_tensor(wts[:, :, 0:E], rank[:, :, :], wsum[:, :].unsqueeze(2).broadcast_to([P, NT, E]), ALU.mult)\
                .then_inc(wts_done, 2)
            for c in range(NC):
                dve.wait_ge(bias_filled, c + 1)
                dve.tensor_copy(acc[:, 4 * c:4 * c + 4, :].rearrange("p n d -> p (n d)"), ps[2 + c % 2][:, :])\
                    .then_inc(acc_started, 1)

            with dve.Fori(0, B) as b:
                for n in range(2 * NE):
                    cc, e = n // NE, n % NE
                    k = 2 * NE * b + n
                    dve.wait_ge(down_filled, k + 1 + 2)
                    dve.wait_ge(acc_done, k + 2)
                    for t in range(4):
                        tile = acc[:, bass.ds(TT * b + 4 * cc + t, 1), :].rearrange("p n d -> p (n d)")
                        w = wts[:, bass.ds(TT * b + 4 * cc + t, 1), e:e + 1].rearrange("p n e -> p (n e)")
                        ins = dve.scalar_tensor_tensor(out=tile, in0=ps[4 + n % 2][:, P * t:P * t + P], scalar=w,
                                                       in1=tile, op0=ALU.mult, op1=ALU.add)
                    ins.then_inc(acc_done, 1)
                    if e == NE - 1:
                        dve.wait_ge(acc_done, k + 3)
                        dve.sem_inc(waited_dve, 1)
                        m = 2 * b + cc
                        sums = acc[:, bass.ds(TT * b + 4 * cc, 4), :]
                        dve.tensor_reduce(amax[:, cc, :], sums, AX.X, ALU.max, apply_absolute_value=True)\
                            .then_inc(fin_step, 1)
                        dve.wait_ge(fin_step, 5 * m + 1)
                        dve.tensor_scalar(amax[:, cc, :], amax[:, cc, :], 0.1, 1e-6, ALU.mult, ALU.add)\
                            .then_inc(fin_step, 1)
                        dve.wait_ge(fin_step, 5 * m + 2)
                        dve.reciprocal(amax[:, cc, :], amax[:, cc, :]).then_inc(fin_step, 1)
                        dve.wait_ge(fin_step, 5 * m + 3)
                        dve.tensor_scalar(amax[:, cc, :], amax[:, cc, :], 0.1, None, ALU.mult).then_inc(fin_step, 1)
                        dve.wait_ge(fin_step, 5 * m + 4)
                        dve.wait_ge(stored, 16 * (2 * b + 1))
                        gb = gates[:, 1, bass.ds(b, 1), :].rearrange("p n d -> p (n d)")
                        for t in range(4):
                            tile = acc[:, bass.ds(TT * b + 4 * cc + t, 1), :].rearrange("p n d -> p (n d)")
                            ins = dve.scalar_tensor_tensor(out=fin[:, cc, t, :], in0=tile, scalar=amax[:, cc, t:t + 1],
                                                           in1=gb, op0=ALU.mult, op1=ALU.mult)
                        ins.then_inc(fin_step, 1)
                        dve.wait_ge(fin_step, 5 * m + 5)
                        dve.tensor_tensor(fin[:, cc, :, :], fin[:, cc, :, :], x_sb[:, bass.ds(TT * b + 4 * cc, 4), :],
                                          ALU.add).then_inc(fin_done, 1)


def kernel(**inputs):
    import numpy as np
    import concourse.bacc as bacc
    from concourse.bass_utils import run_bass_kernel_spmd as run

    a = {k.removeprefix("L0_"): np.asarray(v) for k, v in inputs.items()}

    def low(m):
        return m.transpose(0, 2, 1).reshape(H // 2, 2 * R, D).transpose(1, 0, 2)

    def high(m):
        return m.reshape(H // 2, 2 * R, HD).transpose(1, 0, 2)

    arrays = dict(
        x=a["attn_hidden_states"].reshape(B * T, D), qaT=low(a["attn_q_a"]), kaT=low(a["attn_k_a"]),
        qb=high(a["attn_q_b"]), kb=high(a["attn_k_b"]), vwT=a["attn_v_w"].T, owT=a["attn_o_w"].T,
        v_b=a["attn_v_b"].reshape(1, D), o_b=a["attn_o_b"].reshape(1, D), cT=a["c"].T, wmod=a["wmod"],
        gate_w=a["ffn_gate_w"], gate_b=a["ffn_bias"].reshape(1, E), up_w=a["ffn_up_w"].transpose(1, 0, 2),
        up_b=a["ffn_up_b"].reshape(E, IT, P).transpose(2, 0, 1), down_w=a["ffn_down_w"], down_b=a["ffn_down_b"],
        sw_up=a["ffn_sw_up"], sb_up=a["ffn_sb_up"].reshape(IT, P).T, sw_down=a["ffn_sw_down"],
        sb_down=a["ffn_sb_down"].reshape(1, D))
    arrays = {f"in_{k}": np.ascontiguousarray(v) for k, v in arrays.items()}
    nc = bacc.Bacc("TRN2", target_bir_lowering=False, num_devices=1)
    args = [nc.dram_tensor(k, v.shape, mybir.dt.from_np(v.dtype), kind="ExternalInput").ap()
            for k, v in arrays.items()]
    args.append(nc.dram_tensor("out", (B * T, D), F32, kind="ExternalOutput").ap())
    adaln_block(nc, *args)
    r = run(nc, [arrays], core_ids=[0])
    return np.asarray(r.results[0]["out"]).reshape(B, T, D)
```

```python
import concourse.bass as bass
from concourse import mybir
from contextlib import ExitStack

F32 = mybir.dt.float32
BF16 = mybir.dt.bfloat16
U32 = mybir.dt.uint32
I32 = mybir.dt.int32
ALU = mybir.AluOpType
ACT = mybir.ActivationFunctionType
AX = mybir.AxisListType

B, T, D, H, R = 4, 1024, 128, 16, 64
HD = D // H
P = 128
TT = T // P
NT = B * TT
CH = 512
NC = B * T // CH
HG = 4
NG = H // HG
E, I = 8, 512
NE = E + 1
IT = I // P
F32_ROW = D + 2
W_COL, DEST_COL = D, D + 1
SLOTS = 256
ST = SLOTS // P
MOST = B * T // SLOTS
NS = 2 * MOST + E - 1
NOWHERE = 1 << 20
SCHUNK = 6
EPS = 1e-5
NEG = -1.0e30
KA = 9 * HD
KB = KA + 3
SCALE = float(HD) ** -0.5


def pack(width):
    return {128: 4, 256: 2}.get(width, 1)


def row_fills():
    out = []
    for i in range(TT):
        for c in range(0, P * (i + 1), CH):
            w = min(CH, P * (i + 1) - c)
            out += [(i, c, w, h, pack(w)) for h in range(0, HG, pack(w))]
    return out


def col_units():
    return [(c, j, max(P * j, CH * c), CH * (c + 1) - max(P * j, CH * c))
            for c in range(T // CH) for j in range(4 * (c + 1))]


ROWS = row_fills()
UNITS = col_units()
NR = len(ROWS)
NU = len(UNITS)
COLS_PER_UNIT = [HG // pack(u[3]) for u in UNITS]
AREA = HG * sum(u[3] for u in UNITS)
NX = sum(COLS_PER_UNIT)
LEAD = 12
XR = 3
PR = 4
LAG = 2


def plan(last):
    steps = []
    row_at = NR + LEAD
    row_end = NG * NR if last else (NG + 1) * NR + LEAD
    pending = []
    clock = 0
    if not last:
        pending += [(1, ("stat", 0)), (2, ("stat", 1)), (2, ("scale", 0)), (3, ("scale", 1))]
        pending += [(4 + 2 * n, ("prep", k, c)) for n, (c, k) in enumerate(
            (c, k) for c in range(2) for k in ("norm", "q", "k", "v"))]

    def rows_to(n):
        nonlocal row_at
        while row_at < min(n, row_end):
            steps.append(("row", row_at // NR, row_at % NR))
            row_at += 1
            if row_at % NR == 0:
                pending.append((clock + 1, ("maxstat", row_at // NR - 1)))
                pending.append((clock + 2, ("max", row_at // NR - 1)))

    def due():
        for item in sorted([p for p in pending if p[0] <= clock], key=lambda p: p[0]):
            pending.remove(item)
            steps.append(item[1])

    for q in range(NG):
        done = 0
        for u in range(NU):
            w = UNITS[u][3]
            fills = COLS_PER_UNIT[u]
            for k in range(fills):
                steps.append(("exp", q, u, k))
                done += w * pack(w)
                if k < fills - 1 or u < NU - 1:
                    rows_to(NR * (q + 1) + LEAD + NR * done // AREA - (3 if u == NU - 1 else 0))
            if u >= LAG:
                steps.append(("pv", q, u - LAG))
                if u - LAG == 3:
                    pending.append((clock + 1, ("evac", q, 0)))
                    pending.append((clock + 2, ("norm", q, 0)))
            if u == NU - 1:
                rows_to(NR * (q + 1) + LEAD + NR - 2)
                steps.append(("pv", q, NU - 2))
                rows_to(NR * (q + 1) + LEAD + NR)
                steps.append(("pv", q, NU - 1))
                pending.append((clock + 1, ("evac", q, 1)))
                pending.append((clock + 2, ("norm", q, 1)))
            clock += 1
            due()
    clock += 100
    due()
    return steps


def first_rows():
    steps = [("row", 0, f) for f in range(NR)] + [("maxstat", 0)]
    steps += [("row", 1, f) for f in range(LEAD // 2)] + [("max", 0)]
    return steps + [("row", 1, f) for f in range(LEAD // 2, LEAD)]


PLAN = {last: plan(last) for last in (False, True)}
PREP = [(c, what) for c in range(2) for what in ("norm", "q", "k", "v")]
DIAG = [n for n in range(NU) if UNITS[n][1] // 4 == UNITS[n][0]]


def turn_numbers(last):
    uses = [s for s in PLAN[last] if s[0] in ("max", "norm", "prep")]
    return {s: n for n, s in enumerate(uses)}


TURN = {last: turn_numbers(last) for last in (False, True)}
LOOP_TURNS = len(TURN[False])
TURN0 = len(PREP) + 1
ALL_TURNS = TURN0 + (B - 1) * LOOP_TURNS + len(TURN[True])


def exp_banks():
    n = NG * NX
    last_user = {k % XR: k - n for k in range(n)}
    out = []
    for k in range(n):
        out.append((k % XR, last_user[k % XR]))
        last_user[k % XR] = k
    return out


XBANK = exp_banks()
SLOT_BYTES = 18 * 16
PART_BYTES = 3 * 16
PV_FREE = PR


def adaln_block(nc, x, qaT, kaT, qb, kb, vwT, owT, v_b, o_b, cT, wmod, gate_w, gate_b,
                up_w, up_b, down_w, down_b, sw_up, sb_up, sw_down, sb_down, out):
    parts_dram = nc.dram_tensor("qk_parts", [B, 2, 3, H, HD, T], BF16).ap()
    routed_dram = nc.dram_tensor("routed_rows", [NS * SLOTS, F32_ROW], F32).ap()
    result_dram = nc.dram_tensor("routed_results", [2 * B * T, D], F32).ap()
    ctx = ExitStack()
    with ctx:
        def sb(name, shape, dt=F32):
            return ctx.enter_context(nc.sbuf_tensor(name, shape, dt))

        def sem(name):
            return ctx.enter_context(nc.semaphore(name))

        x_sb = sb("x_sb", [P, NT, D])
        y_all = sb("y_all", [P, NT, D])
        v_all = sb("v_all", [P, NT, D])
        QK = sb("QK", [P, 2 * NG * HG * T], BF16)
        probs = sb("probs", [P, PR * HG * CH])
        vg = sb("vg", [P, 2, TT, HG, 32])
        xn = sb("xn", [P, 2, 4, D])
        hT = sb("hT", [P, 2, CH])
        qf = sb("qf", [P, 2, CH])
        rest = sb("rest", [P, 2, CH])
        parts = sb("parts", [P, 2, 3, CH], BF16)
        o_sb = sb("o_sb", [P, 2, CH])
        stats = sb("stats", [P, 2, 4, 6])
        mv = sb("mv", [P, 2, 4, 2])
        rstd = sb("rstd", [P, 2, 4])
        mhalf = sb("mhalf", [P, NT])
        rowmax = sb("rowmax", [P, 2, HG, TT, 2])
        gmax = sb("gmax", [P, 2, HG * TT])
        grest = sb("grest", [P, 2, HG * TT])
        gparts = sb("gparts", [P, 2, 3, HG * TT], BF16)
        shift = sb("shift", [3 * HG * TT, 2, P], BF16)
        rden = sb("rden", [P, 2, 4 * HG])
        ident = sb("ident", [P, P])
        identb = sb("identb", [P, P], BF16)
        maskb = sb("maskb", [P, P], BF16)
        ones = sb("ones", [1, P])
        ones16 = sb("ones16", [16, T], BF16)
        wq = sb("wq", [P, D])
        wk = sb("wk", [P, D])
        wv = sb("wv", [P, D])
        wo = sb("wo", [P, D])
        wog = sb("wog", [P, B, D])
        vb_sb = sb("vb_sb", [1, D])
        ob_sb = sb("ob_sb", [1, D])
        obg = sb("obg", [1, B, D])
        cT_sb = sb("cT_sb", [P, B])
        silu = sb("silu", [P, 3, B])
        wm = sb("wm", [P, 6 * D])
        modT = sb("modT", [P, 6, B])
        modc = sb("modc", [P, 2])
        gates = sb("gates", [P, 2, B, D])
        gw = sb("gw", [P, E])
        gb_sb = sb("gb_sb", [1, E])
        ub = sb("ub", [P, NE, IT])
        db_sb = sb("db_sb", [NE, D])
        score = sb("score", [P, NT, E])
        below = sb("below", [P, E, E])
        rank = sb("rank", [P, NT, E])
        wsum = sb("wsum", [P, NT])
        wts = sb("wts", [P, NT, NE])
        st2 = sb("st2", [P, NT, 6])
        mv2 = sb("mv2", [P, NT, 2])
        rs2 = sb("rs2", [P, NT])
        amax = sb("amax", [P, 2, 4])
        scale_row = sb("scale_row", [P, B, D])
        empty_row = sb("empty_row", [P, F32_ROW])
        earlier = sb("earlier", [P, P])
        tile_start = sb("tile_start", [P, MOST])
        tile_number = sb("tile_number", [1, NS])
        expert_tiles = sb("expert_tiles", [P, 3, E])
        expert_f = sb("expert_f", [1, NS])
        expert_of = sb("expert_of", [1, NS], I32)
        row_at = sb("row_at", [P, 2, NT], U32)
        ubr = sb("ubr", [P, SCHUNK, IT])
        QS, KS = QK[:, 0:NG * HG * T], QK[:, NG * HG * T:2 * NG * HG * T]
        QS4 = QS[:, :].rearrange("p (g h t) -> p g h t", g=NG, h=HG)
        KS4 = KS[:, :].rearrange("p (g h t) -> p g h t", g=NG, h=HG)
        pr4 = probs[:, :].rearrange("p (s h t) -> p s h t", s=PR, h=HG)
        qaT_sb = probs[:, 0:1024].rearrange("p (n d) -> p n d", n=8)
        kaT_sb = probs[:, 1024:2048].rearrange("p (n d) -> p n d", n=8)
        qbd = probs[:, 2048:2176].rearrange("p (n d) -> p n d", n=8)
        kbd = probs[:, 2176:2304].rearrange("p (n d) -> p n d", n=8)
        siluB = probs[:, 2304:2304 + B * P].rearrange("p (b m) -> p b m", b=B)
        gsign = probs[:, 2816:2816 + 2 * B * D].rearrange("p (j b d) -> p j b d", j=2, b=B)
        qk = QK[:, :].bitcast(F32)
        rows_end = NT * 2 * F32_ROW
        h2rows = qk[:, 0:rows_end].rearrange("p (n r d) -> p n r d", n=NT, r=2)
        routed = qk[:, 0:2 * NT * D].rearrange("p (r n d) -> p r n d", r=2, n=NT)
        at = rows_end + E * I
        uw = qk[:, rows_end:at].rearrange("p (e i) -> p e i", e=E)
        shared_uw = qk[:, at:at + I]
        shared_dw = qk[:, at + I:at + 2 * I].rearrange("p (c h) -> p c h", c=IT)
        at += 2 * I
        larger = QK[:, 2 * at:2 * at + NT * E * E].rearrange("p (n e f) -> p n e f", n=NT, e=E)
        equal = QK[:, 2 * at + NT * E * E:2 * at + 2 * NT * E * E].rearrange("p (n e f) -> p n e f", n=NT, e=E)
        fin = qk[:, at:at + 2 * CH].rearrange("p (s n d) -> p s n d", s=2, n=4)
        shift_row = wm[:, 0:B * D].rearrange("p (b d) -> p b d", b=B)
        not_first = wm[:, B * D:B * D + E * NT].rearrange("p (e n) -> p e n", e=E)
        ones128 = wo
        by_rank = xn[:, :, :, :].rearrange("p a n d -> p (a n d)").rearrange("p (a n e) -> p a n e", a=4, n=NT)
        qf_flat = qf[:, :, :].rearrange("p a t -> p (a t)")
        chosen = qf_flat[:, 0:NT * E].rearrange("p (n e) -> p n e", n=NT)
        position = qf_flat[:, NT * E:2 * NT * E].rearrange("p (n e) -> p n e", n=NT)
        totals = qf_flat[:, NT * E:2 * NT * E].rearrange("p (e n) -> p e n", e=E)
        running = qf_flat[:, 2 * NT * E:3 * NT * E].rearrange("p (e n) -> p e n", e=E)
        before_tile = qf_flat[:, 3 * NT * E:4 * NT * E].rearrange("p (e n) -> p e n", e=E)
        picked = wk[:, 0:4 * NT].rearrange("p (a n) -> p a n", a=4)
        filled = wq[:, 0:E * MOST].rearrange("p (e k) -> p e k", e=E)
        past = ones16[0:1, 0:2 * NS * E].bitcast(F32).rearrange("p (k e) -> p k e", k=NS)
        dw = v_all[:, :, :].rearrange("p (e c) h -> p e c h", e=E)
        wT = rest[0:NE, :, :]
        yT = probs[:, 0:NT * P]
        h2T = probs[:, NT * P:2 * NT * P]
        xn2 = h2rows[:, :, 0, 0:D]
        acc = y_all
        hact = probs[:, 0:2 * IT * CH].rearrange("p (s c t) -> p s c t", s=2, c=IT)
        vg_flat = vg[:, :, :, :, :].rearrange("p s j h d -> p (s j h d)")
        ur = vg_flat[:, 0:2 * I].rearrange("p (s i) -> p s i", s=2)
        dr = vg_flat[:, 2 * I:4 * I].rearrange("p (s c h) -> p s c h", s=2, c=IT)
        ring = SCHUNK * ST * F32_ROW
        slot_rows = qk[:, 0:ring].rearrange("p (s t d) -> p s t d", s=SCHUNK, t=ST)
        slotT = hT[:, :, 0:SLOTS]
        slot_out = qk[:, ring:ring + SCHUNK * ST * D].rearrange("p (s t d) -> p s t d", s=SCHUNK, t=ST)

        ps = [ctx.enter_context(nc.psum_tensor(f"bank{n}", [P, CH], F32)) for n in range(8)]
        row_bank, exp_bank, out_bank, turn_bank = ps[0:2], ps[2:5], ps[5:7], ps[7]
        turn_b16 = turn_bank[0:3 * HG * TT, 0:P // 2].bitcast(BF16)

        waited_pool = sem("waited_pool")
        waited_dve = sem("waited_dve")
        x_first = sem("x_first")
        x_rest = sem("x_rest")
        small_loaded = sem("small_loaded")
        lowrank_loaded = sem("lowrank_loaded")
        lowrank_zeroed = sem("lowrank_zeroed")
        consts_zeroed = sem("consts_zeroed")
        consts_made = sem("consts_made")
        vg_ready = sem("vg_ready")
        ones_stored = sem("ones_stored")
        ones_made = sem("ones_made")
        silu_exp = sem("silu_exp")
        silu_step = sem("silu_step")
        silu_done = sem("silu_done")
        qk_folded = sem("qk_folded")
        qk_copied = sem("qk_copied")
        mod_filled = sem("mod_filled")
        o_folded = sem("o_folded")
        mod_step = sem("mod_step")
        mod_done = sem("mod_done")
        modrow_done = sem("modrow_done")
        turn_filled = sem("turn_filled")
        turn_free = sem("turn_free")
        stat_step = sem("stat_step")
        var_done = sem("var_done")
        rstd_done = sem("rstd_done")
        norm_done = sem("norm_done")
        split_step = sem("split_step")
        split_done = sem("split_done")
        parts_stored = [sem("q_parts_stored"), sem("k_parts_stored")]
        slot_loaded = [sem(f"slot_loaded{q}") for q in range(NG)]
        shift_loaded = [sem(f"shift_loaded{q}") for q in range(NG)]
        vg_done = sem("vg_done")
        row_filled = sem("row_filled")
        row_free = sem("row_free")
        gmax_done = sem("gmax_done")
        gpart_step = sem("gpart_step")
        exp_filled = sem("exp_filled")
        exp_done = sem("exp_done")
        tri_done = sem("tri_done")
        pv_done = sem("pv_done")
        out_copied = sem("out_copied")
        rden_done = sem("rden_done")
        ffn_loaded = sem("ffn_loaded")
        bias_loaded = sem("bias_loaded")
        yt_filled = sem("yt_filled")
        yt_copied = sem("yt_copied")
        proj_filled = sem("proj_filled")
        x2_done = sem("x2_done")
        st2_done = sem("st2_done")
        var2_done = sem("var2_done")
        rs2_done = sem("rs2_done")
        xn2_done = sem("xn2_done")
        h2_filled = sem("h2_filled")
        h2_done = sem("h2_done")
        gate_filled = sem("gate_filled")
        gate_exp = sem("gate_exp")
        route_step = sem("route_step")
        wts_done = sem("wts_done")
        wt_filled = sem("wt_filled")
        wt_copied = sem("wt_copied")
        bias_filled = sem("bias_filled")
        acc_started = sem("acc_started")
        prefilled = sem("prefilled")
        route_consts = sem("route_consts")
        chosen_ready = sem("chosen_ready")
        counted = sem("counted")
        shared_loaded = sem("shared_loaded")
        totals_done = sem("totals_done")
        table_done = sem("table_done")
        positions_done = sem("positions_done")
        row_weight_done = sem("row_weight_done")
        dest_made = sem("dest_made")
        scaled_rows = sem("scaled_rows")
        h2rows_done = sem("h2rows_done")
        second_rows = sem("second_rows")
        rows_sent = sem("rows_sent")
        shared_up = sem("shared_up")
        shared_gelu = sem("shared_gelu")
        shared_down = sem("shared_down")
        shared_copied = sem("shared_copied")
        slot_rows_loaded = [sem(f"slot_rows_loaded{k}") for k in range(SCHUNK)]
        slotT_filled = sem("slotT_filled")
        slotT_copied = sem("slotT_copied")
        up_copied = sem("up_copied")
        down_copied = sem("down_copied")
        slot_gelu = sem("slot_gelu")
        slot_up = sem("slot_up")
        slot_down = sem("slot_down")
        slot_weighted = sem("slot_weighted")
        results_sent = [sem(f"results_sent{k}") for k in range(SCHUNK)]
        results_loaded = [sem(f"results_loaded{c}") for c in range(NC)]
        rank0_added = sem("rank0_added")
        fin_step = sem("fin_step")
        fin_done = sem("fin_done")
        stored = [sem(f"stored{cc}") for cc in range(2)]

        block = ctx.enter_context(nc.Block())
        xt = x.rearrange("(n p) d -> p n d", p=P)
        ot = out.rearrange("(n p) d -> p n d", p=P)

        def batches(eng, body):
            with eng.Fori(0, B - 1) as b:
                body(b, False)
            body(B - 1, True)

        def slot_tiles(eng, step):
            for k in range(SCHUNK):
                step(0, k, False)
            with eng.Fori(1, NS // SCHUNK) as turn_of_ring:
                for k in range(SCHUNK):
                    step(turn_of_ring, k, False)
            for k in range(NS % SCHUNK):
                step(NS // SCHUNK, k, True)

        def turn(b, last, step):
            return TURN0 + LOOP_TURNS * b + TURN[last][step]

        def units(b, q):
            return NU * (NG * b + q) + PV_FREE

        def exps(b, q, u):
            return NX * (NG * b + q) + sum(COLS_PER_UNIT[:u + 1]) + XR

        @block.sync
        def _(sp):
            sp.dma_start(x_sb[:, 0:TT, :], xt[:, 0:TT, :]).then_inc(x_first, 16)
            sp.wait_ge(ones_made, 2)
            for r in range(KA, KB):
                sp.dma_start(KS[r:r + 1, :], ones16[:, :]).then_inc(ones_stored, 16)
            sp.dma_start(cT_sb[:, :], cT).then_inc(small_loaded, 16)
            sp.dma_start(wm[:, :], wmod).then_inc(small_loaded, 16)
            sp.dma_start(wv[:, :], vwT).then_inc(small_loaded, 16)
            sp.dma_start(wo[:, :], owT).then_inc(small_loaded, 16)
            sp.dma_start(vb_sb[:, :], v_b).then_inc(small_loaded, 16)
            sp.dma_start(ob_sb[:, :], o_b).then_inc(small_loaded, 16)
            sp.dma_start(gw[:, :], gate_w).then_inc(small_loaded, 16)
            sp.dma_start(gb_sb[:, :], gate_b).then_inc(small_loaded, 16)
            sp.dma_start(x_sb[:, TT:NT, :], xt[:, TT:NT, :]).then_inc(x_rest, 16)
            sp.dma_start(ub[:, 0:E, :], up_b).then_inc(bias_loaded, 16)
            sp.dma_start(ub[:, E, :], sb_up).then_inc(bias_loaded, 16)
            sp.dma_start(db_sb[0:E, :], down_b).then_inc(bias_loaded, 16)
            sp.dma_start(db_sb[E:NE, :], sb_down).then_inc(bias_loaded, 16)

            sp.wait_ge(route_consts, 6)
            sp.dma_start(routed_dram.rearrange("(n p) d -> p n d", p=P),
                         empty_row[:, :].unsqueeze(1).broadcast_to([P, NS * ST, F32_ROW])).then_inc(prefilled, 16)

            def store_parts(b, c, side):
                sp.wait_ge(split_done, 2 * (2 * b + c) + side + 1)
                for part in range(3):
                    dst = parts_dram[bass.ds(b, 1), side, part, :, :, CH * c:CH * c + CH]
                    sp.dma_start(dst.rearrange("b h d t -> (b h d) t"), parts[:, side, part, :])\
                      .then_inc(parts_stored[side], 16)

            def load_slot(b, q):
                for i in range(3):
                    for j in range(3):
                        r = HD * (3 * i + j)
                        for side, part, rows in ((0, i, QS4), (1, j, KS4)):
                            src = parts_dram[bass.ds(b, 1), side, part, HG * q:HG * q + HG, :, :]
                            sp.dma_start(rows[r:r + HD, q, :, :], src.rearrange("b h d t -> d (b h) t"))\
                              .then_inc(slot_loaded[q], 16)

            def store_shift(b, q, t):
                sp.wait_ge(turn_free, t + 1)
                for part in range(3):
                    sp.dma_start(QS4[KA + part:KA + part + 1, q % NG, :, :],
                                 shift[part * HG * TT:(part + 1) * HG * TT, q % 2, :])\
                      .then_inc(shift_loaded[q % NG], 16)

            for c in range(2):
                for side in range(2):
                    store_parts(0, c, side)
            for side in range(2):
                sp.wait_ge(parts_stored[side], 2 * PART_BYTES)
            for q in range(NG):
                load_slot(0, q)
            store_shift(0, 0, TURN0 - 1)

            def body(b, last):
                for s in PLAN[last]:
                    if s[0] == "max":
                        store_shift(b, s[1], turn(b, last, s))
                    elif s[0] == "prep" and s[1] in ("q", "k"):
                        store_parts(b + 1, s[2], "qk".index(s[1]))
                    elif s[0] == "exp" and s[2:] == (0, 0) and s[1] >= 1 and not last:
                        q = s[1] - 1
                        if q >= 1:
                            sp.wait_ge(exp_filled, NX * (NG * b + q + 1))
                            load_slot(b + 1, q)
                    if not last and s == ("exp", 1, 8, 0):
                        for side in range(2):
                            sp.wait_ge(parts_stored[side], 2 * PART_BYTES * (b + 2))
                        sp.wait_ge(exp_filled, NX * (NG * b + 1))
                        load_slot(b + 1, 0)
                if not last:
                    sp.wait_ge(exp_filled, NX * NG * (b + 1))
                    load_slot(b + 1, NG - 1)

            batches(sp, body)
            sp.wait_ge(exp_filled, NX * NG * B)
            sp.wait_ge(row_filled, NR * NG * B)
            sp.dma_start(shared_uw, sw_up).then_inc(shared_loaded, 16)
            sp.dma_start(shared_dw, sw_down.rearrange("(c p) h -> p c h", p=P)).then_inc(shared_loaded, 16)
            sp.dma_start(uw, up_w).then_inc(ffn_loaded, 16)
            sp.wait_ge(vg_done, NG * B)
            for e in range(E):
                sp.dma_start(dw[:, e, :, :], down_w[e, :, :].rearrange("(c p) h -> p c h", p=P)).then_inc(ffn_loaded, 16)

            sp.wait_ge(rows_sent, 16 * 2 * NT)
            rd = routed_dram.rearrange("(n t p) d -> p n t d", t=ST, p=P)

            def load(j, k, peeled):
                if not isinstance(j, int) or j > 0:
                    sp.wait_ge(results_sent[k], 16 * ST * j)
                sp.dma_start(slot_rows[:, k, :, :],
                             rd[:, bass.ds(SCHUNK * j + k, 1), :, :].rearrange("p n t d -> p (n t) d"))\
                  .then_inc(slot_rows_loaded[k], 16)

            slot_tiles(sp, load)
            for k in range(SCHUNK):
                sp.wait_ge(results_sent[k], 16 * ST * ((NS + SCHUNK - 1 - k) // SCHUNK))
            res = result_dram.rearrange("(r n p) d -> p r n d", r=2, p=P)
            for c in range(NC):
                for r in range(2):
                    sp.dma_start(routed[:, r, 4 * c:4 * c + 4, :], res[:, r, 4 * c:4 * c + 4, :])\
                      .then_inc(results_loaded[c], 16)
            with sp.Fori(0, B) as b:
                for cc in range(2):
                    sp.wait_ge(fin_done, 2 * b + cc + 1)
                    sp.dma_start(ot[:, bass.ds(TT * b + 4 * cc, 4), :], fin[:, cc, :, :]).then_inc(stored[cc], 16)
            for cc in range(2):
                sp.wait_ge(stored[cc], 16 * B)

        @block.gpsimd
        def _(pool):
            pool.memset(ident[:, :], 0.0).then_inc(consts_zeroed, 1)
            pool.memset(identb[:, :], 0.0).then_inc(consts_zeroed, 1)
            pool.memset(maskb[:, :], 0.0).then_inc(consts_zeroed, 1)
            pool.memset(below[:, :, :], 1.0).then_inc(consts_zeroed, 1)
            pool.memset(mhalf[:, :], -0.5).then_inc(consts_zeroed, 1)
            pool.memset(vg[:, :, :, :, :], 0.0).then_inc(consts_zeroed, 1)
            pool.wait_ge(consts_zeroed, 6)
            for m in (ident, identb):
                pool.affine_select(out=m[:, :], in_=m[:, :], compare_op=ALU.not_equal, fill=1.0, base=0,
                                   pattern=[[-1, P]], channel_multiplier=1).then_inc(consts_made, 1)
            pool.affine_select(out=maskb[:, :], in_=maskb[:, :], compare_op=ALU.is_ge, fill=NEG, base=0,
                               pattern=[[-1, P]], channel_multiplier=1).then_inc(consts_made, 1)
            pool.affine_select(out=below[:, :, :], in_=below[:, :, :], compare_op=ALU.is_gt, fill=0.0, base=0,
                               pattern=[[1, E], [-1, E]], channel_multiplier=0).then_inc(consts_made, 1)
            pool.memset(vg[:, :, :, :, HD:HD + 1], 1.0).then_inc(vg_ready, 1)
            pool.memset(earlier[:, :], 1.0).then_inc(route_consts, 1)
            pool.memset(empty_row[:, :], 0.0).then_inc(route_consts, 1)
            pool.wait_ge(route_consts, 2)
            pool.iota(empty_row[:, DEST_COL:DEST_COL + 1].bitcast(U32), pattern=[[0, 1]], base=NOWHERE,
                      channel_multiplier=0).then_inc(route_consts, 1)
            pool.sem_inc(waited_pool, 1)
            pool.affine_select(out=earlier[:, :], in_=earlier[:, :], compare_op=ALU.is_gt, fill=0.0, base=0,
                               pattern=[[1, P]], channel_multiplier=-1).then_inc(route_consts, 1)
            pool.iota(tile_start[:, :], pattern=[[SLOTS, MOST]], base=0, channel_multiplier=0,
                      allow_small_or_imprecise_dtypes=True).then_inc(route_consts, 1)
            pool.iota(tile_number[:, :], pattern=[[1, NS]], base=0, channel_multiplier=0,
                      allow_small_or_imprecise_dtypes=True).then_inc(route_consts, 1)

            def norm(b, c):
                m = 2 * b + c
                pool.wait_ge(var_done, m + 1)
                pool.tensor_tensor(rstd[:, c, :], rstd[:, c, :], mhalf[:, 0:4], ALU.pow).then_inc(rstd_done, 1)
            def split(b, c, side, t):
                k = 2 * (2 * b + c) + side
                pool.wait_ge(turn_free, t + 1)
                pool.tensor_tensor(rest[:, side, :], qf[:, side, :], parts[:, side, 0, :], ALU.subtract)\
                    .then_inc(split_step, 1)
                pool.wait_ge(split_step, 2 * k + 1)
                pool.sem_inc(waited_pool, 1)
                pool.tensor_copy(parts[:, side, 1, :], rest[:, side, :]).then_inc(split_step, 1)
                pool.wait_ge(split_step, 2 * k + 2)
                pool.tensor_tensor(parts[:, side, 2, :], rest[:, side, :], parts[:, side, 1, :], ALU.subtract)\
                    .then_inc(split_done, 1)

            def group_v(b, q):
                pool.sem_inc(waited_pool, 1)
                for j in range(TT):
                    last = pool.tensor_copy(
                        vg[:, q % 2, j, :, 0:HD],
                        v_all[:, bass.ds(TT * b + j, 1), 32 * q:32 * q + 32].rearrange("p n (h d) -> p (n h) d", h=HG))
                last.then_inc(vg_done, 1)

            def maxima(b, q):
                n, r = NG * b + q, q % 2
                pool.wait_ge(gmax_done, n + 1)
                pool.sem_inc(waited_pool, 1)
                pool.tensor_scalar(gparts[:, r, 0, :], gmax[:, r, :], -1.0, None, ALU.mult).then_inc(gpart_step, 1)
                pool.tensor_scalar(grest[:, r, :], gmax[:, r, :], -1.0, None, ALU.mult).then_inc(gpart_step, 1)
                pool.wait_ge(gpart_step, 5 * n + 2)
                pool.tensor_tensor(grest[:, r, :], grest[:, r, :], gparts[:, r, 0, :], ALU.subtract)\
                    .then_inc(gpart_step, 1)
                pool.wait_ge(gpart_step, 5 * n + 3)
                pool.sem_inc(waited_pool, 1)
                pool.tensor_copy(gparts[:, r, 1, :], grest[:, r, :]).then_inc(gpart_step, 1)
                pool.wait_ge(gpart_step, 5 * n + 4)
                pool.tensor_tensor(gparts[:, r, 2, :], grest[:, r, :], gparts[:, r, 1, :], ALU.subtract)\
                    .then_inc(gpart_step, 1)

            pool.wait_ge(x_first, 16)
            norm(0, 0)
            norm(0, 1)
            for t, (c, what) in enumerate(PREP):
                if what in ("q", "k"):
                    split(0, c, "qk".index(what), t)
            pool.wait_ge(vg_ready, 1)
            pool.wait_ge(turn_free, len(PREP))
            group_v(0, 0)
            maxima(0, 0)
            pool.wait_ge(x_rest, 16)

            def body(b, last):
                for s in PLAN[last]:
                    if s[0] == "exp":
                        _, q, u, k = s
                        if (u, k) == (2, 0) and q < NG - 1:
                            pool.wait_ge(pv_done, units(b, q))
                            group_v(b, q + 1)
                        if u in DIAG and k == COLS_PER_UNIT[u] - 1:
                            pool.wait_ge(exp_done, exps(b, q, u))
                            pool.sem_inc(waited_pool, 1)
                            pool.affine_select(out=pr4[:, u % PR, :, 0:P], in_=pr4[:, u % PR, :, 0:P],
                                               compare_op=ALU.is_ge, fill=0.0, base=0,
                                               pattern=[[0, HG], [1, P]], channel_multiplier=-1)\
                                .then_inc(tri_done, 1)
                    elif s[0] == "maxstat":
                        maxima(b, s[1])
                    elif s[0] == "stat":
                        norm(b + 1, s[1])
                    elif s[0] == "prep":
                        _, what, c = s
                        if what in ("q", "k"):
                            split(b + 1, c, "qk".index(what), turn(b, last, s))
                if not last:
                    pool.wait_ge(turn_free, turn(b, last, ("prep", "v", 1)) + 1)
                    pool.wait_ge(pv_done, units(b, NG - 1))
                    group_v(b + 1, 0)

            batches(pool, body)
            pool.wait_ge(var2_done, 1)
            pool.tensor_tensor(rs2[:, :], rs2[:, :], mhalf[:, :], ALU.pow).then_inc(rs2_done, 1)
            pool.iota(h2rows[:, :, :, DEST_COL].bitcast(U32), pattern=[[P, NT], [B * T, 2]], base=0,
                      channel_multiplier=1).then_inc(dest_made, 1)
            for c in range(NC):
                pool.wait_ge(h2_filled, c + 1)
                xc = xn2[:, 4 * c:4 * c + 4, :]
                for step, (row, op) in enumerate(((1, ALU.mult), (0, ALU.add))):
                    if step:
                        pool.wait_ge(scaled_rows, c + 1)
                    pool.tensor_tensor(xc, xc, (shift_row, scale_row)[row][:, c // 2, :].unsqueeze(1).broadcast_to([P, 4, D]), op)\
                        .then_inc((scaled_rows, h2rows_done)[step], 1)
            pool.wait_ge(prefilled, 16)
            pool.wait_ge(dest_made, 1)
            pool.wait_ge(positions_done, 1)
            for r in range(2):
                for n in range(NT):
                    if n % 4 == 0:
                        if r == 0:
                            pool.wait_ge(h2rows_done, n // 4 + 1)
                        else:
                            pool.wait_ge(second_rows, n // 4 + 1)
                    pool.indirect_dma_start(routed_dram, bass.IndirectOffsetOnAxis(ap=row_at[:, r, n:n + 1], axis=0),
                                            h2rows[:, n, r, :], None).then_inc(rows_sent, 16)

            def send(j, k, peeled):
                pool.wait_ge(slot_weighted, SCHUNK * j + k + 1 + 2)
                pool.sem_inc(waited_pool, 1)
                for t in range(ST):
                    pool.indirect_dma_start(
                        result_dram, bass.IndirectOffsetOnAxis(ap=slot_rows[:, k, t, DEST_COL:DEST_COL + 1].bitcast(U32),
                                                               axis=0),
                        slot_out[:, k, t, :], None, bounds_check=2 * B * T - 1, oob_is_err=False)\
                        .then_inc(results_sent[k], 16)

            slot_tiles(pool, send)

            for m in range(NC + 1):
                if m < NC:
                    pool.wait_ge(results_loaded[m], 32)
                    a = acc[:, 4 * m:4 * m + 4, :]
                    pool.tensor_tensor(a, a, routed[:, 0, 4 * m:4 * m + 4, :], ALU.add).then_inc(rank0_added, 1)
                if m >= 1:
                    pool.wait_ge(fin_step, 6 * m)
                    pool.tensor_tensor(fin[:, (m - 1) % 2, :, :], fin[:, (m - 1) % 2, :, :],
                                       x_sb[:, 4 * m - 4:4 * m, :], ALU.add).then_inc(fin_done, 1)

        @block.scalar
        def _(act):
            act.dma_start(qaT_sb, qaT).then_inc(lowrank_loaded, 16)
            act.dma_start(kaT_sb, kaT).then_inc(lowrank_loaded, 16)
            act.wait_ge(lowrank_zeroed, 1)
            for dst, src in ((qbd, qb), (kbd, kb)):
                for h2 in range(2):
                    act.dma_start(dst[R * h2:R * h2 + R, :, HD * h2:HD * h2 + HD], src[R * h2:R * h2 + R, :, :])\
                        .then_inc(lowrank_loaded, 16)
            act.wait_ge(small_loaded, 16 * 8)
            act.activation(silu[:, 0, :], cT_sb[:, :], ACT.Exp, scale=-1.0).then_inc(silu_exp, 1)

            def prep_read(b, c, what, t, first=False):
                act.wait_ge(turn_filled, t + 1)
                if what == "norm":
                    act.activation(hT[:, c, :], turn_bank[:, :], ACT.Identity, bias=modc[:, 0:1], scale=modc[:, 1:2])\
                        .then_inc(turn_free, 1)
                elif what == "v":
                    act.activation(v_all[:, bass.ds(TT * b + 4 * c, 4), :],
                                   turn_bank[:, :].rearrange("p (n d) -> p n d", n=4), ACT.Copy).then_inc(turn_free, 1)
                else:
                    side = "qk".index(what)
                    if not first:
                        act.wait_ge(split_done, 2 * (2 * b + c) + side - 1)
                        act.wait_ge(parts_stored[side], PART_BYTES * (2 * b + c))
                    scale = SCALE if what == "q" else 1.0
                    act.activation(qf[:, side, :], turn_bank[:, :], ACT.Copy, scale=scale)
                    act.activation(parts[:, side, 0, :], turn_bank[:, :], ACT.Copy, scale=scale).then_inc(turn_free, 1)

            def max_read(q, t):
                act.wait_ge(turn_filled, t + 1)
                act.activation(shift[:, q % 2, :], turn_b16, ACT.Copy).then_inc(turn_free, 1)

            act.wait_ge(mod_done, 1)
            for t, (c, what) in enumerate(PREP):
                prep_read(0, c, what, t, first=(c == 0))
            max_read(0, TURN0 - 1)

            def body(b, last):
                nx = 0
                for s in PLAN[last]:
                    if s[0] == "exp":
                        _, q, u, k = s
                        w = UNITS[u][3]
                        h = k * pack(w)
                        if k == 0:
                            act.wait_ge(pv_done, units(b, q) + u + 1 - PR)
                        act.wait_ge(exp_filled, NG * NX * b + nx + 1)
                        act.activation(pr4[:, u % PR, h:h + pack(w), 0:w],
                                       exp_bank[XBANK[nx][0]][:, 0:w * pack(w)].rearrange(
                                           "p (h t) -> p h t", h=pack(w)), ACT.Exp).then_inc(exp_done, 1)
                        nx += 1
                    elif s[0] == "evac":
                        _, q, c = s
                        act.wait_ge(pv_done, units(b, q) + (4 if c == 0 else NU))
                        act.activation(o_sb[:, c, :], out_bank[c][:, :], ACT.Copy).then_inc(out_copied, 1)
                    elif s[0] == "max":
                        max_read(s[1], turn(b, last, s))
                    elif s[0] == "prep":
                        prep_read(b + 1, s[2], s[1], turn(b, last, s))

            batches(act, body)
            for c in range(NC):
                act.wait_ge(yt_filled, c + 1)
                act.activation(yT[:, CH * c:CH * c + CH], ps[c % 2][:, :], ACT.Copy).then_inc(yt_copied, 1)
            for c in range(NC):
                b = c // 2
                act.wait_ge(h2_filled, c + 1)
                act.activation(h2T[:, CH * c:CH * c + CH], ps[4 + c % 2][:, :], ACT.Identity,
                               bias=modT[:, 3, b:b + 1], scale=modT[:, 4, b:b + 1]).then_inc(h2_done, 1)
            act.wait_ge(gate_filled, 1)
            act.activation(score[:, :, :], ps[6][:, 0:NT * E].rearrange("p (n e) -> p n e", n=NT), ACT.Exp,
                           scale=-1.0).then_inc(gate_exp, 1)
            act.wait_ge(bias_loaded, 64)

            def shared(c, first=False, copies=True):
                par = c % 2 if isinstance(c, int) else c[1]
                n = c if isinstance(c, int) else c[0]
                for i in range(IT):
                    act.wait_ge(shared_up, IT * n + i + 1)
                    act.wait_ge(shared_down, n + 1)
                    act.activation(hact[:, par, i, :], ps[i][:, :], ACT.Gelu, bias=ub[:, E, i:i + 1])\
                        .then_inc(shared_gelu, 1)
                if not first:
                    copy_out(n - 1, 1 - par)
                act.wait_ge(h2rows_done, n + 1)
                act.activation(h2rows[:, bass.ds(4 * n, 4), 1, 0:D], h2rows[:, bass.ds(4 * n, 4), 0, 0:D], ACT.Copy)\
                    .then_inc(second_rows, 1)

            def copy_out(n, par):
                act.wait_ge(shared_down, n + 1 + 2)
                act.activation(acc[:, bass.ds(4 * n, 4), :].rearrange("p n d -> p (n d)"), ps[4 + par][:, :], ACT.Copy)\
                    .then_inc(shared_copied, 1)

            shared(0, first=True)
            shared(1)
            with act.Fori(1, NC // 2) as j:
                for par in range(2):
                    shared((2 * j + par, par))
            copy_out(NC - 1, 1)
            for c in range(NC):
                act.wait_ge(wt_filled, c + 1)
                if c >= 2:
                    act.wait_ge(bias_filled, c - 1)
                act.activation(wT[:, c % 2, :], ps[c % 2][0:NE, :], ACT.Copy).then_inc(wt_copied, 1)

            def take(j, k):
                act.wait_ge(slotT_filled, SCHUNK * j + k + 1)
                act.activation(slotT[:, k % 2, :], ps[6 + k % 2][:, 0:SLOTS], ACT.Copy).then_inc(slotT_copied, 1)

            def gelus(j, k):
                act.wait_ge(up_copied, SCHUNK * j + k + 1)
                act.wait_ge(slot_down, SCHUNK * j + k + 1)
                for m in range(IT):
                    act.wait_ge(slot_up, IT * (SCHUNK * j + k) + m + 1)
                    act.activation(hact[:, k % 2, m, 0:SLOTS], ps[m][:, 0:SLOTS], ACT.Gelu,
                                   bias=ubr[:, k % SCHUNK, m:m + 1]).then_inc(slot_gelu, 1)

            take(0, 0)
            take(0, 1)
            gelus(0, 0)

            def step(j, k, peeled):
                if not peeled or k + 2 < NS % SCHUNK:
                    take(j, k + 2)
                if not peeled or k + 1 < NS % SCHUNK:
                    gelus(j, k + 1)

            slot_tiles(act, step)

        @block.tensor
        def _(pe):
            mm, tr = nc.tensor.matmul, nc.tensor.transpose
            pe.wait_ge(lowrank_loaded, 16 * 6)
            for side, (a, bd) in enumerate(((qaT_sb, qbd), (kaT_sb, kbd))):
                for n in range(8):
                    m = mm(ps[0][:, D * side + 16 * n:D * side + 16 * n + 16], a[:, n, :], bd[:, n, :],
                           start=True, stop=True)
            m.then_inc(qk_folded, 1)
            pe.wait_ge(silu_done, 1)
            for j in range(6):
                mm(ps[1][:, B * j:B * j + B], wm[:, D * j:D * j + D], silu[:, 2, :], start=True, stop=True)
            for bank, j in ((2, 2), (3, 5), (4, 3), (5, 4)):
                for b in range(B):
                    m = mm(ps[bank][:, D * b:D * b + D], siluB[:, b, :], wm[:, D * j:D * j + D],
                           start=True, stop=True)
            m.then_inc(mod_filled, 1)
            pe.wait_ge(consts_made, 4)
            pe.wait_ge(ones_made, 2)
            pe.wait_ge(ones_stored, 48)

            def prep(b, c, what, t):
                m = 2 * b + c
                if t is not None:
                    pe.wait_ge(turn_free, t)
                if what == "norm":
                    pe.wait_ge(norm_done, m + 1)
                    for n in range(4):
                        last = tr(turn_bank[:, P * n:P * n + P], xn[:, c, n, :], ident[:, :])
                elif what == "v":
                    for n in range(4):
                        mm(turn_bank[:, P * n:P * n + P], hT[:, c, P * n:P * n + P], wv[:, :], start=True, stop=False)
                        last = mm(turn_bank[:, P * n:P * n + P], ones[:, :], vb_sb[:, :], start=False, stop=True)
                else:
                    last = mm(turn_bank[:, :], (wq if what == "q" else wk)[:, :], hT[:, c, :], start=True, stop=True)
                last.then_inc(turn_filled, 1)

            pe.wait_ge(qk_copied, 2)
            for t, (c, what) in enumerate(PREP):
                prep(0, c, what, t if t else None)

            def rows(b, q, f, before):
                i, c0, w, h0, nh = ROWS[f]
                if f == 0:
                    pe.wait_ge(slot_loaded[q % NG], SLOT_BYTES * (b + 1))
                if before is not None:
                    pe.wait_ge(row_free, before)
                bank = row_bank[f % 2]
                diagonal = c0 + w == P * (i + 1)
                for n in range(nh):
                    m = mm(bank[:, w * n:w * n + w], QS4[0:KA, q % NG, h0 + n, P * i:P * i + P],
                           KS4[0:KA, q % NG, h0 + n, c0:c0 + w], start=True, stop=not diagonal)
                    if diagonal:
                        m = mm(bank[:, w * n + w - P:w * n + w], identb[:, :], maskb[:, :],
                               start=False, stop=True)
                m.then_inc(row_filled, 1)

            def max_turn(b, q, t):
                pe.wait_ge(gpart_step, 5 * (NG * b + q) + 5)
                pe.wait_ge(turn_free, t)
                tr(turn_b16, gparts[:, q % 2, :, :].rearrange("p a n -> p (a n)"), identb[:, :])\
                    .then_inc(turn_filled, 1)

            for s in first_rows():
                if s[0] == "row":
                    n = NR * s[1] + s[2]
                    rows(0, s[1], s[2], n - 1 if n >= 2 else None)
                elif s[0] == "max":
                    max_turn(0, 0, TURN0 - 1)

            def body(b, last):
                nx = 0
                for s in PLAN[last]:
                    if s[0] == "row":
                        _, q, f = s
                        rows(b + q // NG, q, f, NR * (NG * b + q) + f - 1)
                    elif s[0] == "exp":
                        _, q, u, k = s
                        c, j, t0, w = UNITS[u]
                        h = k * pack(w)
                        if (u, k) == (0, 0):
                            pe.wait_ge(shift_loaded[q], PART_BYTES * (b + 1))
                        bank, user = XBANK[nx]
                        pe.wait_ge(exp_done, NG * NX * b + user + 1 + XR)
                        for n in range(pack(w)):
                            m = mm(exp_bank[bank][:, w * n:w * n + w], KS4[0:KB, q, h + n, P * j:P * j + P],
                                   QS4[0:KB, q, h + n, t0:t0 + w], start=True, stop=True)
                        m.then_inc(exp_filled, 1)
                        nx += 1
                    elif s[0] == "pv":
                        _, q, u = s
                        c, j, t0, w = UNITS[u]
                        if u == 0:
                            pe.wait_ge(vg_done, NG * b + q + 1)
                        if j == 0:
                            pe.wait_ge(out_copied, 2 * (NG * b + q) + c + 1)
                        if u in DIAG:
                            pe.wait_ge(tri_done, len(DIAG) * (NG * b + q) + DIAG.index(u) + 1)
                        else:
                            pe.wait_ge(exp_done, exps(b, q, u))
                        for h in range(HG):
                            m = mm(out_bank[c][32 * h:32 * h + 32, t0 - CH * c:CH], vg[:, q % 2, j, h, :],
                                   pr4[:, u % PR, h, 0:w], start=(j == 0), stop=(j == 4 * c + 3))
                        m.then_inc(pv_done, 1)
                    elif s[0] == "max":
                        max_turn(b, s[1], turn(b, last, s))
                    elif s[0] == "norm":
                        _, q, c = s
                        pe.wait_ge(out_copied, 2 * (NG * b + q) + c + 1 + 2)
                        pe.wait_ge(turn_free, turn(b, last, s))
                        for n in range(4):
                            m = tr(turn_bank[:, P * n:P * n + P], o_sb[:, c, P * n:P * n + P], ident[:, :])
                        m.then_inc(turn_filled, 1)
                    elif s[0] == "prep":
                        prep(b + 1, s[2], s[1], turn(b, last, s))

            batches(pe, body)

            pe.wait_ge(turn_free, ALL_TURNS)
            for c in range(NC):
                if c >= 2:
                    pe.wait_ge(yt_copied, c - 1)
                for n in range(4):
                    m = tr(ps[c % 2][:, P * n:P * n + P], y_all[:, 4 * c + n, :], ident[:, :])
                m.then_inc(yt_filled, 1)
            for c in range(NC):
                pe.wait_ge(yt_copied, c + 1)
                if c >= 2:
                    pe.wait_ge(x2_done, c - 1)
                for n in range(4):
                    mm(ps[2 + c % 2][:, P * n:P * n + P], yT[:, CH * c + P * n:CH * c + P * n + P], wog[:, c // 2, :],
                       start=True, stop=False)
                    m = mm(ps[2 + c % 2][:, P * n:P * n + P], ones[:, :], obg[:, c // 2, :], start=False, stop=True)
                m.then_inc(proj_filled, 1)
            for c in range(NC):
                pe.wait_ge(xn2_done, c + 1)
                if c >= 2:
                    pe.wait_ge(h2_done, c - 1)
                for n in range(4):
                    m = tr(ps[4 + c % 2][:, P * n:P * n + P], xn2[:, 4 * c + n, :], ident[:, :])
                m.then_inc(h2_filled, 1)
            for n in range(NT):
                pe.wait_ge(h2_done, n // 4 + 1)
                mm(ps[6][:, E * n:E * n + E], h2T[:, P * n:P * n + P], gw[:, :], start=True, stop=False)
                m = mm(ps[6][:, E * n:E * n + E], ones[:, :], gb_sb[:, :], start=False, stop=True)
            m.then_inc(gate_filled, 1)
            pe.wait_ge(shared_loaded, 32)

            def shared_ups(n, par):
                for i in range(IT):
                    pe.wait_ge(shared_gelu, IT * n + i + 1)
                    mm(ps[i][:, :], shared_uw[:, P * i:P * i + P], h2T[:, bass.ds(CH * n, CH)],
                       start=True, stop=True).then_inc(shared_up, 1)

            def shared_downs(n, par):
                pe.wait_ge(shared_gelu, IT * (n + 2))
                pe.wait_ge(shared_copied, n + 1)
                for t in range(4):
                    for i in range(IT):
                        m = mm(ps[4 + par][:, P * t:P * t + P], hact[:, par, i, P * t:P * t + P],
                               shared_dw[:, i, :], start=(i == 0), stop=(i == IT - 1))
                m.then_inc(shared_down, 1)

            shared_ups(0, 0)
            shared_ups(1, 1)
            shared_downs(0, 0)
            pe.wait_ge(chosen_ready, 1)
            picks = chosen[:, :, :].rearrange("p n e -> p (n e)")
            mm(ps[7][:, 0:NT * E], earlier[:, :], picks, start=True, stop=True)
            mm(ps[7][:, NT * E:2 * NT * E], ones128[:, :], picks, start=True, stop=True).then_inc(counted, 1)
            with pe.Fori(1, NC // 2) as j:
                for par in range(2):
                    shared_ups(2 * j + par, par)
                    shared_downs(2 * j + par - 1, 1 - par)
            shared_downs(NC - 1, 1)
            pe.wait_ge(wts_done, 2)
            pe.wait_ge(bias_loaded, 64)
            pe.wait_ge(shared_gelu, IT * (NC + 1))
            for c in range(NC):
                if c >= 2:
                    pe.wait_ge(wt_copied, c - 1)
                for n in range(4):
                    m = tr(ps[c % 2][0:NE, P * n:P * n + P], wts[:, 4 * c + n, :], ident[:, :])
                m.then_inc(wt_filled, 1)
                if c >= 2:
                    pe.wait_ge(acc_started, c - 1)
                pe.wait_ge(wt_copied, c + 1)
                for n in range(4):
                    m = mm(ps[2 + c % 2][:, P * n:P * n + P], wT[:, c % 2, P * n:P * n + P], db_sb[:, :],
                           start=True, stop=True)
                m.then_inc(bias_filled, 1)
            pe.wait_ge(acc_started, NC)

            def turn_rows(j, k):
                pe.wait_ge(slot_rows_loaded[k % SCHUNK], 16 * (j + k // SCHUNK + 1))
                pe.wait_ge(slotT_copied, SCHUNK * j + k + 1)
                for t in range(ST):
                    m = tr(ps[6 + k % 2][:, P * t:P * t + P], slot_rows[:, k % SCHUNK, t, 0:D], ident[:, :])
                m.then_inc(slotT_filled, 1)

            def up(j, k):
                pe.wait_ge(up_copied, SCHUNK * j + k + 1)
                pe.wait_ge(slotT_copied, SCHUNK * j + k + 1 + 2)
                for m in range(IT):
                    pe.wait_ge(slot_gelu, IT * (SCHUNK * j + k) + m + 1)
                    mm(ps[m][:, 0:SLOTS], ur[:, k % 2, P * m:P * m + P], slotT[:, k % 2, :],
                       start=True, stop=True).then_inc(slot_up, 1)

            turn_rows(0, 0)
            turn_rows(0, 1)
            up(0, 0)

            def step(j, k, peeled):
                if not peeled or k + 2 < NS % SCHUNK:
                    turn_rows(j, k + 2)
                if not peeled or k + 1 < NS % SCHUNK:
                    up(j, k + 1)
                pe.wait_ge(slot_gelu, IT * (SCHUNK * j + k + 2))
                pe.wait_ge(down_copied, SCHUNK * j + k + 1)
                pe.wait_ge(slot_weighted, SCHUNK * j + k + 1)
                for t in range(ST):
                    for m in range(IT):
                        last = mm(ps[4 + k % 2][:, P * t:P * t + P], hact[:, k % 2, m, P * t:P * t + P],
                                  dr[:, k % 2, m, :], start=(m == 0), stop=(m == IT - 1))
                last.then_inc(slot_down, 1)

            slot_tiles(pe, step)

        @block.vector
        def _(dve):
            dve.memset(probs[:, 2048:2304], 0.0).then_inc(lowrank_zeroed, 1)
            dve.memset(ones16[:, :], 1.0).then_inc(ones_made, 1)
            dve.memset(ones[:, :], 1.0).then_inc(ones_made, 1)

            def stat(b, c):
                m = 2 * b + c
                for t in range(4):
                    ins = dve.bn_stats(stats[:, c, t, :], x_sb[:, bass.ds(TT * b + 4 * c + t, 1), :].rearrange(
                        "p n d -> p (n d)"))
                ins.then_inc(stat_step, 1)
                dve.wait_ge(stat_step, 2 * m + 1)
                dve.sem_inc(waited_dve, 1)
                for t in range(4):
                    ins = dve.bn_aggr(mv[:, c, t, :], stats[:, c, t, :])
                ins.then_inc(stat_step, 1)
                dve.wait_ge(stat_step, 2 * m + 2)
                dve.tensor_scalar(rstd[:, c, :], mv[:, c, :, 1:2].rearrange("p n a -> p (n a)"), EPS, None, ALU.add)\
                    .then_inc(var_done, 1)

            def norm(b, c):
                dve.wait_ge(rstd_done, 2 * b + c + 1)
                for t in range(4):
                    ins = dve.tensor_scalar(xn[:, c, t, :], x_sb[:, bass.ds(TT * b + 4 * c + t, 1), :].rearrange(
                        "p n d -> p (n d)"), mv[:, c, t, 0:1], rstd[:, c, t:t + 1], ALU.subtract, ALU.mult)
                ins.then_inc(norm_done, 1)

            dve.wait_ge(x_first, 16)
            stat(0, 0)
            stat(0, 1)
            norm(0, 0)
            norm(0, 1)
            dve.memset(rowmax[:, :, :, :, :], -3.0e38)
            dve.wait_ge(silu_exp, 1)
            dve.tensor_scalar(silu[:, 1, :], silu[:, 0, :], 1.0, None, ALU.add).then_inc(silu_step, 1)
            dve.wait_ge(silu_step, 1)
            dve.reciprocal(silu[:, 0, :], silu[:, 1, :]).then_inc(silu_step, 1)
            dve.wait_ge(silu_step, 2)
            dve.tensor_tensor(silu[:, 2, :], silu[:, 0, :], cT_sb[:, :], ALU.mult).then_inc(silu_step, 1)
            dve.wait_ge(silu_step, 3)
            dve.tensor_copy(siluB[:, :, :], silu[:, 2, :].unsqueeze(2).broadcast_to([P, B, P])).then_inc(silu_done, 1)
            dve.wait_ge(qk_folded, 1)
            dve.tensor_copy(wq[:, :], ps[0][:, 0:D]).then_inc(qk_copied, 1)
            dve.tensor_copy(wk[:, :], ps[0][:, D:2 * D]).then_inc(qk_copied, 1)
            dve.wait_ge(mod_filled, 1)
            dve.tensor_copy(modT[:, :, :], ps[1][:, 0:6 * B].rearrange("p (j b) -> p j b", j=6)).then_inc(mod_step, 1)
            dve.wait_ge(mod_step, 1)
            dve.tensor_scalar(modT[:, 1:5:3, :], modT[:, 1:5:3, :], 1.0, None, ALU.add).then_inc(mod_step, 1)
            dve.wait_ge(mod_step, 2)
            dve.tensor_copy(modc[:, :], modT[:, 0:2, 0:1].rearrange("p j b -> p (j b)")).then_inc(mod_done, 1)
            dve.tensor_copy(wm[:, 0:B * D], ps[4][:, :]).then_inc(modrow_done, 1)
            dve.tensor_scalar(scale_row[:, :, :].rearrange("p b d -> p (b d)"), ps[5][:, :], 1.0, None, ALU.add)\
                .then_inc(modrow_done, 1)
            dve.memset(not_first[:, :, :], 1.0).then_inc(modrow_done, 1)
            dve.wait_ge(modrow_done, 3)
            dve.memset(not_first[:, :, 0:1], 0.0)
            gate_flat = gates[:, :, :, :].rearrange("p j b d -> p j (b d)")
            sign_flat = gsign[:, :, :, :].rearrange("p j b d -> p j (b d)")
            for j in range(2):
                dve.tensor_scalar(sign_flat[:, j], ps[2 + j][:, :], 0.0, 2.0, ALU.is_ge, ALU.mult).then_inc(mod_step, 1)
            dve.wait_ge(mod_step, 4)
            for j in range(2):
                dve.scalar_tensor_tensor(out=gate_flat[:, j], in0=sign_flat[:, j], scalar=-1.0, in1=ps[2 + j][:, :],
                                         op0=ALU.add, op1=ALU.mult).then_inc(mod_step, 1)
            dve.wait_ge(mod_step, 6)
            dve.tensor_scalar(gate_flat[:, :], gate_flat[:, :], 0.25, None, ALU.max).then_inc(mod_step, 1)
            dve.wait_ge(mod_step, 7)
            dve.scalar_tensor_tensor(out=gate_flat[:, :], in0=sign_flat[:, :], scalar=-1.0, in1=gate_flat[:, :],
                                     op0=ALU.add, op1=ALU.mult).then_inc(mod_step, 1)
            dve.wait_ge(mod_step, 8)
            dve.tensor_tensor(wog[:, :, :], gates[:, 0, :, :], wo[:, :].unsqueeze(1).broadcast_to([P, B, D]), ALU.mult)
            dve.tensor_tensor(obg[:, :, :], gates[0:1, 0, :, :], ob_sb[:, :].unsqueeze(1).broadcast_to([1, B, D]),
                              ALU.mult).then_inc(o_folded, 1)
            dve.wait_ge(o_folded, 1)
            dve.memset(ones128[:, :], 1.0)
            for free, count in ((exp_done, XR), (pv_done, PV_FREE), (out_copied, 2), (shared_gelu, IT),
                                (shared_down, 2), (shared_copied, 1), (slotT_copied, 2), (slot_gelu, IT),
                                (slot_down, 2), (slot_weighted, 2)):
                dve.sem_inc(free, count)
            dve.memset(wts[:, :, E:NE], 1.0)

            def row_max(b, q, f):
                i, c0, w, h0, nh = ROWS[f]
                n = NR * (NG * b + q) + f
                dve.wait_ge(row_filled, n + 1)
                dve.tensor_reduce(rowmax[:, q % 2, h0:h0 + nh, i, c0 // CH], row_bank[f % 2][:, 0:w * nh].rearrange(
                    "p (h s) -> p h s", h=nh), AX.X, ALU.max).then_inc(row_free, 1)

            def group_max(b, q):
                n, r = NG * b + q, q % 2
                dve.wait_ge(row_free, NR * (n + 1))
                m = rowmax[:, r, :, :, :].rearrange("p h i c -> p (h i) c")
                dve.tensor_tensor(gmax[:, r, :], m[:, :, 0], m[:, :, 1], ALU.max).then_inc(gmax_done, 1)

            for s in first_rows():
                if s[0] == "row":
                    row_max(0, s[1], s[2])
                elif s[0] == "maxstat":
                    group_max(0, 0)
            dve.wait_ge(x_rest, 16)

            def body(b, last):
                for s in PLAN[last]:
                    if s[0] == "row":
                        row_max(b, s[1], s[2])
                    elif s[0] == "maxstat":
                        group_max(b, s[1])
                    elif s[0] == "stat":
                        if s[1] == 0:
                            dve.tensor_copy(modc[:, :], modT[:, 0:2, bass.ds(b + 1, 1)].rearrange("p j b -> p (j b)"))
                        stat(b + 1, s[1])
                    elif s[0] == "scale":
                        norm(b + 1, s[1])
                    elif s[0] == "norm":
                        _, q, c = s
                        dve.wait_ge(turn_filled, turn(b, last, s) + 1)
                        o = turn_bank[:, :].rearrange("p (n h k) -> p n h k", n=4, h=HG)
                        dve.reciprocal(rden[:, c, :].rearrange("p (n h) -> p n h", n=4), o[:, :, :, HD])\
                            .then_inc(rden_done, 1)
                        dve.wait_ge(rden_done, 2 * (NG * b + q) + c + 1)
                        dve.tensor_tensor(
                            y_all[:, bass.ds(TT * b + 4 * c, 4), 32 * q:32 * q + 32].rearrange(
                                "p n (h d) -> p n h d", h=HG), o[:, :, :, 0:HD],
                            rden[:, c, :].rearrange("p (n h) -> p n h", n=4).unsqueeze(3).broadcast_to([P, 4, HG, HD]),
                            ALU.mult).then_inc(turn_free, 1)

            batches(dve, body)

            for c in range(NC):
                dve.wait_ge(proj_filled, c + 1)
                xc = x_sb[:, 4 * c:4 * c + 4, :].rearrange("p n d -> p (n d)")
                dve.tensor_tensor(xc, ps[2 + c % 2][:, :], xc, ALU.add).then_inc(x2_done, 1)
            for n in range(NT):
                if n % 4 == 0:
                    dve.wait_ge(x2_done, n // 4 + 1)
                dve.bn_stats(st2[:, n, :], x_sb[:, n, :]).then_inc(st2_done, 1)
            for n in range(NT):
                dve.wait_ge(st2_done, n + 1)
                ins = dve.bn_aggr(mv2[:, n, :], st2[:, n, :])
            ins.then_inc(st2_done, 1)
            dve.wait_ge(st2_done, NT + 1)
            dve.tensor_scalar(rs2[:, :], mv2[:, :, 1], EPS, None, ALU.add).then_inc(var2_done, 1)
            dve.wait_ge(rs2_done, 1)
            for n in range(NT):
                ins = dve.tensor_scalar(xn2[:, n, :], x_sb[:, n, :], mv2[:, n, 0:1], rs2[:, n:n + 1],
                                        ALU.subtract, ALU.mult)
                if n % 4 == 3:
                    ins.then_inc(xn2_done, 1)
            dve.wait_ge(gate_exp, 1)
            dve.tensor_scalar(score[:, :, :], score[:, :, :], 1.0, None, ALU.add).then_inc(route_step, 1)
            dve.wait_ge(route_step, 1)
            dve.reciprocal(score[:, :, :], score[:, :, :]).then_inc(route_step, 1)
            dve.wait_ge(route_step, 2)
            other = score[:, :, :].unsqueeze(2).broadcast_to([P, NT, E, E])
            own = score[:, :, :].unsqueeze(3).broadcast_to([P, NT, E, E])
            dve.tensor_tensor(larger, other, own, ALU.is_gt).then_inc(route_step, 1)
            dve.tensor_tensor(equal, other, own, ALU.is_equal).then_inc(route_step, 1)
            dve.wait_ge(route_step, 4)
            dve.tensor_tensor(equal, equal, below[:, :, :].unsqueeze(1).broadcast_to([P, NT, E, E]), ALU.mult)\
                .then_inc(route_step, 1)
            dve.wait_ge(route_step, 5)
            dve.tensor_tensor(larger, larger, equal, ALU.add).then_inc(route_step, 1)
            dve.wait_ge(route_step, 6)
            dve.tensor_reduce(rank[:, :, :], larger, AX.X, ALU.add).then_inc(route_step, 1)
            dve.wait_ge(route_step, 7)
            flat = "p n e -> p (n e)"
            dve.tensor_scalar(chosen[:, :, :], rank[:, :, :], 1.5, None, ALU.is_lt).then_inc(chosen_ready, 1)
            dve.scalar_tensor_tensor(out=wts[:, :, 0:E], in0=rank[:, :, :], scalar=1.5, in1=score[:, :, :],
                                     op0=ALU.is_lt, op1=ALU.mult).then_inc(route_step, 1)
            dve.wait_ge(route_step, 8)
            dve.tensor_reduce(wsum[:, :], wts[:, :, 0:E], AX.X, ALU.add).then_inc(route_step, 1)
            dve.wait_ge(route_step, 9)
            dve.tensor_scalar(wsum[:, :], wsum[:, :], 1e-6, None, ALU.add).then_inc(route_step, 1)
            dve.wait_ge(route_step, 10)
            dve.reciprocal(wsum[:, :], wsum[:, :]).then_inc(route_step, 1)
            dve.wait_ge(route_step, 11)
            dve.tensor_tensor(wts[:, :, 0:E], wts[:, :, 0:E], wsum[:, :].unsqueeze(2).broadcast_to([P, NT, E]), ALU.mult)\
                .then_inc(wts_done, 2)
            dve.wait_ge(wts_done, 2)
            for r in range(2):
                dve.scalar_tensor_tensor(out=by_rank[:, 2 + r, :, :], in0=rank[:, :, :], scalar=float(r),
                                         in1=wts[:, :, 0:E], op0=ALU.is_equal, op1=ALU.mult).then_inc(route_step, 1)
            dve.wait_ge(counted, 1)
            dve.tensor_copy(totals[:, :, :], ps[7][:, NT * E:2 * NT * E].rearrange("p (n e) -> p e n", n=NT))                .then_inc(totals_done, 1)
            dve.wait_ge(totals_done, 1)
            within = ps[7][:, 0:NT * E].rearrange("p (n e) -> p n e", n=NT)
            dve.tensor_tensor_scan(running[:, :, :].rearrange("p e n -> p (e n)"),
                                   not_first[:, :, :].rearrange("p e n -> p (e n)"),
                                   totals[:, :, :].rearrange("p e n -> p (e n)"), 0.0, ALU.mult, ALU.add)\
                .then_inc(route_step, 1)
            dve.wait_ge(route_step, 14)
            dve.tensor_tensor(filled[:, :, :], running[:, :, NT - 1:NT].broadcast_to([P, E, MOST]),
                              tile_start[:, :].unsqueeze(1).broadcast_to([P, E, MOST]), ALU.is_gt)\
                .then_inc(route_step, 1)
            dve.tensor_tensor(before_tile[:, :, :], running[:, :, :], totals[:, :, :], ALU.subtract).then_inc(route_step, 1)
            dve.wait_ge(route_step, 16)
            dve.tensor_reduce(expert_tiles[:, 0, :], filled[:, :, :], AX.X, ALU.add).then_inc(route_step, 1)
            dve.wait_ge(route_step, 17)
            dve.tensor_tensor_scan(expert_tiles[:, 1, :], ones128[:, 0:E], expert_tiles[:, 0, :], 0.0,
                                   ALU.mult, ALU.add).then_inc(route_step, 1)
            dve.wait_ge(route_step, 18)
            dve.tensor_tensor(expert_tiles[:, 2, :], expert_tiles[:, 1, :], expert_tiles[:, 0, :], ALU.subtract)\
                .then_inc(route_step, 1)
            dve.wait_ge(route_step, 19)
            dve.scalar_tensor_tensor(out=before_tile[:, :, :],
                                     in0=expert_tiles[:, 2, :].unsqueeze(2).broadcast_to([P, E, NT]),
                                     scalar=float(SLOTS), in1=before_tile[:, :, :], op0=ALU.mult, op1=ALU.add)\
                .then_inc(route_step, 1)
            dve.wait_ge(route_step, 20)
            dve.tensor_tensor(position[:, :, :], within, before_tile[:, :, :].rearrange("p e n -> p n e"), ALU.add)\
                .then_inc(route_step, 1)
            dve.wait_ge(route_step, 21)
            for r in range(2):
                dve.scalar_tensor_tensor(out=by_rank[:, r, :, :], in0=rank[:, :, :], scalar=float(r),
                                         in1=position[:, :, :], op0=ALU.is_equal, op1=ALU.mult).then_inc(route_step, 1)
            dve.wait_ge(route_step, 23)
            dve.tensor_reduce(picked[:, :, :], by_rank[:, :, :, :], AX.X, ALU.add).then_inc(route_step, 1)
            dve.wait_ge(route_step, 24)
            dve.tensor_copy(h2rows[:, :, :, W_COL], picked[:, 2:4, :].rearrange("p r n -> p n r"))
            dve.tensor_copy(row_at[:, :, :], picked[:, 0:2, :]).then_inc(positions_done, 1)
            dve.tensor_tensor(past[:, :, :], tile_number[:, :].unsqueeze(2).broadcast_to([1, NS, E]),
                              expert_tiles[0:1, 1, :].unsqueeze(1).broadcast_to([1, NS, E]), ALU.is_ge)\
                .then_inc(route_step, 1)
            dve.wait_ge(route_step, 25)
            dve.tensor_reduce(expert_f[:, :], past[:, :, :], AX.X, ALU.add).then_inc(route_step, 1)
            dve.wait_ge(route_step, 26)
            dve.tensor_scalar(expert_of[:, :], expert_f[:, :], float(E - 1), None, ALU.min).then_inc(table_done, 1)

            def copy_up(j, k):
                e = dve.value_load(expert_of[0:1, bass.ds(SCHUNK * j + k, 1)], min_val=0, max_val=E - 1)
                dve.tensor_copy(ubr[:, k % SCHUNK, :], ub[:, bass.ds(e, 1), :].rearrange("p n d -> p (n d)"))
                dve.tensor_copy(ur[:, k % 2, :], uw[:, bass.ds(e, 1), :].rearrange("p n d -> p (n d)"))\
                    .then_inc(up_copied, 1)

            def copy_down(j, k):
                e = dve.value_load(expert_of[0:1, bass.ds(SCHUNK * j + k, 1)], min_val=0, max_val=E - 1)
                dve.tensor_copy(dr[:, k % 2, :, :].rearrange("p c h -> p (c h)"),
                                dw[:, bass.ds(e, 1), :, :].rearrange("p n c h -> p (n c h)")).then_inc(down_copied, 1)

            dve.wait_ge(table_done, 1)
            dve.wait_ge(bias_loaded, 64)
            dve.wait_ge(ffn_loaded, 16 * (1 + E))
            copy_up(0, 0)
            copy_down(0, 0)
            copy_up(0, 1)
            copy_down(0, 1)
            for c in range(NC):
                dve.wait_ge(bias_filled, c + 1)
                dve.wait_ge(shared_copied, c + 1 + 1)
                a = acc[:, 4 * c:4 * c + 4, :].rearrange("p n d -> p (n d)")
                dve.tensor_tensor(a, ps[2 + c % 2][:, :], a, ALU.add).then_inc(acc_started, 1)
            dve.wait_ge(slot_up, IT)
            copy_up(0, 2)

            def step(j, k, peeled):
                dve.wait_ge(slot_down, SCHUNK * j + k + 1 + 2)
                if not isinstance(j, int) or j > 0:
                    dve.wait_ge(results_sent[k], 16 * ST * j)
                for t in range(ST):
                    last = dve.tensor_scalar(slot_out[:, k, t, :], ps[4 + k % 2][:, P * t:P * t + P],
                                             slot_rows[:, k, t, W_COL:W_COL + 1], None, ALU.mult)
                last.then_inc(slot_weighted, 1)
                if not peeled or k + 2 < NS % SCHUNK:
                    copy_down(j, k + 2)
                if not peeled or k + 3 < NS % SCHUNK:
                    copy_up(j, k + 3)

            slot_tiles(dve, step)

            for m in range(NC):
                cc = m % 2
                sums = acc[:, 4 * m:4 * m + 4, :]
                dve.wait_ge(rank0_added, m + 1)
                dve.tensor_tensor(sums, sums, routed[:, 1, 4 * m:4 * m + 4, :], ALU.add).then_inc(fin_step, 1)
                dve.wait_ge(fin_step, 6 * m + 1)
                dve.tensor_reduce(amax[:, cc, :], sums, AX.X, ALU.max, apply_absolute_value=True).then_inc(fin_step, 1)
                dve.wait_ge(fin_step, 6 * m + 2)
                dve.tensor_scalar(amax[:, cc, :], amax[:, cc, :], 0.1, 1e-6, ALU.mult, ALU.add).then_inc(fin_step, 1)
                dve.wait_ge(fin_step, 6 * m + 3)
                dve.reciprocal(amax[:, cc, :], amax[:, cc, :]).then_inc(fin_step, 1)
                dve.wait_ge(fin_step, 6 * m + 4)
                dve.tensor_scalar(amax[:, cc, :], amax[:, cc, :], 0.1, None, ALU.mult).then_inc(fin_step, 1)
                dve.wait_ge(fin_step, 6 * m + 5)
                if m >= 2:
                    dve.wait_ge(stored[cc], 16 * (m // 2))
                for t in range(4):
                    ins = dve.scalar_tensor_tensor(out=fin[:, cc, t, :], in0=acc[:, 4 * m + t, :],
                                                   scalar=amax[:, cc, t:t + 1], in1=gates[:, 1, m // 2, :],
                                                   op0=ALU.mult, op1=ALU.mult)
                ins.then_inc(fin_step, 1)


def kernel(**inputs):
    import numpy as np
    import concourse.bacc as bacc
    from concourse.bass_utils import run_bass_kernel_spmd as run

    a = {k.removeprefix("L0_"): np.asarray(v) for k, v in inputs.items()}

    def low(m):
        return m.transpose(0, 2, 1).reshape(H // 2, 2 * R, D).transpose(1, 0, 2)

    def high(m):
        return m.reshape(H // 2, 2 * R, HD).transpose(1, 0, 2)

    arrays = dict(
        x=a["attn_hidden_states"].reshape(B * T, D), qaT=low(a["attn_q_a"]), kaT=low(a["attn_k_a"]),
        qb=high(a["attn_q_b"]), kb=high(a["attn_k_b"]), vwT=a["attn_v_w"].T, owT=a["attn_o_w"].T,
        v_b=a["attn_v_b"].reshape(1, D), o_b=a["attn_o_b"].reshape(1, D), cT=a["c"].T, wmod=a["wmod"],
        gate_w=a["ffn_gate_w"], gate_b=a["ffn_bias"].reshape(1, E), up_w=a["ffn_up_w"].transpose(1, 0, 2),
        up_b=a["ffn_up_b"].reshape(E, IT, P).transpose(2, 0, 1), down_w=a["ffn_down_w"], down_b=a["ffn_down_b"],
        sw_up=a["ffn_sw_up"], sb_up=a["ffn_sb_up"].reshape(IT, P).T, sw_down=a["ffn_sw_down"],
        sb_down=a["ffn_sb_down"].reshape(1, D))
    arrays = {f"in_{k}": np.ascontiguousarray(v) for k, v in arrays.items()}
    nc = bacc.Bacc("TRN2", target_bir_lowering=False, num_devices=1)
    args = [nc.dram_tensor(k, v.shape, mybir.dt.from_np(v.dtype), kind="ExternalInput").ap()
            for k, v in arrays.items()]
    args.append(nc.dram_tensor("out", (B * T, D), F32, kind="ExternalOutput").ap())
    adaln_block(nc, *args)
    r = run(nc, [arrays], core_ids=[0])
    return np.asarray(r.results[0]["out"]).reshape(B, T, D)
```

```python
import concourse.bass as bass
from concourse import mybir
from contextlib import ExitStack

F32 = mybir.dt.float32
BF16 = mybir.dt.bfloat16
U32 = mybir.dt.uint32
I32 = mybir.dt.int32
ALU = mybir.AluOpType
ACT = mybir.ActivationFunctionType
AX = mybir.AxisListType

B, T, D, H, R = 4, 1024, 128, 16, 64
HD = D // H
P = 128
TT = T // P
NT = B * TT
CH = 512
NC = B * T // CH
HG = 4
NG = H // HG
E, I = 8, 512
NE = E + 1
IT = I // P
F32_ROW = D + 2
W_COL, DEST_COL = D, D + 1
SLOTS = 256
ST = SLOTS // P
MOST = B * T // SLOTS
NS = 2 * MOST + E - 1
NOWHERE = 1 << 20
SCHUNK = 6
EPS = 1e-5
NEG = -1.0e30
KA = 9 * HD
KB = KA + 3
SCALE = float(HD) ** -0.5


def pack(width):
    return {128: 4, 256: 2}.get(width, 1)


def row_fills():
    out = []
    for i in range(TT):
        for c in range(0, P * (i + 1), CH):
            w = min(CH, P * (i + 1) - c)
            out += [(i, c, w, h, pack(w)) for h in range(0, HG, pack(w))]
    return out


def col_units():
    return [(c, j, max(P * j, CH * c), CH * (c + 1) - max(P * j, CH * c))
            for c in range(T // CH) for j in range(4 * (c + 1))]


ROWS = row_fills()
UNITS = col_units()
NR = len(ROWS)
NU = len(UNITS)
COLS_PER_UNIT = [HG // pack(u[3]) for u in UNITS]
AREA = HG * sum(u[3] for u in UNITS)
NX = sum(COLS_PER_UNIT)
LEAD = 15
XR = 2
PR = 4
TURN_APART = 1.6
RR = 3
FAR_AHEAD = 6
BEHIND, AHEAD = 1, 2
CHORE_UNITS = (0, 1, 4, 5, 6, 7, 8)
LAG = 2


SIDE_WEIGHTS = {"max": (0.1, 0.2, 0), "maxstat": (0, 0, 0.2), "evac": (0, 0.5, 0), "norm": (0.5, 0, 0.6), "q": (0.9, 1, 0),
              "k": (0.9, 1, 0), "v": (0.9, 0.5, 0), "stat": (0, 0, 1.6), "scale": (0, 0, 1.1), "turn": (0.5, 0.5, 0),
              "proj": (0.9, 0, 0.7), "var2": (0, 0, 1.6)}


class Clock:

    def __init__(self):
        self.pe = self.act = self.dve = 0.0
        self.exp_read = [0.0] * XR
        self.row_read = [0.0] * RR

    def exp(self, cols):
        self.pe = max(self.pe, self.exp_read[0]) + cols / 2400
        self.act = max(self.act, self.pe + 0.2) + cols / 1200 + 0.07
        self.exp_read = self.exp_read[1:] + [self.act + 0.05]

    def row(self, cols, heads, diagonal):
        self.pe = max(self.pe, self.row_read[0]) + cols / 2400 + (heads * P / 2400 if diagonal else 0)
        self.dve = max(self.dve, self.pe + 0.2) + cols / 960 + 0.07
        self.row_read = self.row_read[1:] + [self.dve + 0.05]

    def pv(self, cols):
        self.pe += HG * cols / 2400 + 0.08

    def side(self, step):
        pe, act, dve = SIDE_WEIGHTS.get(step[0] if step[0] not in ("prep", "post") else step[1], (0, 0, 0))
        self.pe, self.act, self.dve = self.pe + pe, max(self.act, self.pe) + act, max(self.dve, self.pe) + dve


def plan(kind):
    last = kind == "last"
    steps = []
    row_at = NR + LEAD
    row_end = NG * NR if last else (NG + 1) * NR + LEAD
    pending = []
    clock = 0
    time = Clock()
    queue = []
    chores = []
    if not last:
        queue += [((), ("stat", 0)), ((), ("stat", 1)), ((), ("scale", 0)), ((), ("scale", 1))]
        for c in range(2):
            for what in ("norm", "q", "k", "v"):
                before = [("split", 0, "qk".index(what), 2)] if c and what in "qk" else []
                queue.append((before, ("prep", what, c)))
        queue.append(([("split", 1, 1, 2)], ("load",)))
    if kind != "first":
        for c in range(2):
            queue.append(((), ("ask", c)))
        for c in range(2):
            queue += [([("fetch", c, 0)], ("post", "turn", c)), ([("fetch", c, 1)], ("post", "proj", c)),
                      ((), ("var2", c))]

    def rows_to(n):
        nonlocal row_at
        while row_at < min(n, row_end):
            i, c0, w, h0, nh = ROWS[row_at % NR]
            time.row(w * nh, nh, c0 + w == P * (i + 1))
            steps.append(("row", row_at // NR, row_at % NR))
            row_at += 1
            if row_at % NR == 0:
                pending.append((clock + 1, ("maxstat", row_at // NR - 1)))
                pending.append((clock + 2, ("max", row_at // NR - 1)))

    def rows_fit(n):
        rows_to(n - BEHIND)
        while row_at < min(n + AHEAD, row_end) and time.row_read[0] <= time.pe + 0.05:
            rows_to(row_at + 1)

    turned = 0.0

    def turn_fits(step):
        nonlocal turned
        if step[0] in ("max", "norm", "prep", "post"):
            if time.pe < turned + TURN_APART:
                return False
            turned = time.pe
        return True

    def due(u):
        for item in sorted([p for p in pending if p[0] <= clock], key=lambda p: p[0]):
            if not turn_fits(item[1]):
                break
            pending.remove(item)
            steps.append(item[1])
            time.side(item[1])
        if queue and all(x in steps for x in queue[0][0]) and turn_fits(queue[0][1]):
            _, step = queue.pop(0)
            if step[0] == "ask":
                chores.extend((clock, ("fetch", step[1], n)) for n in range(2))
            else:
                steps.append(step)
                time.side(step)
            if step[0] == "prep" and step[1] in ("q", "k"):
                chores.extend((clock + 1, ("split", step[2], "qk".index(step[1]), n)) for n in range(3))
            if step[0] == "var2":
                chores.extend((clock + 1, ("rows2", step[1], n)) for n in range(5))
        if chores and chores[0][0] <= clock and u in CHORE_UNITS:
            steps.append(chores.pop(0)[1])

    pvs = []

    def pv():
        q, u = pvs.pop(0)
        steps.append(("pv", q, u))
        time.pv(UNITS[u][3])
        if u in (3, NU - 1):
            pending.append((clock + 1, ("evac", q, u // 4 // 2)))
            pending.append((clock + 2, ("norm", q, u // 4 // 2)))

    for q in range(NG):
        done = 0
        for u in range(NU):
            w = UNITS[u][3]
            for k in range(COLS_PER_UNIT[u]):
                ahead = NR * (q + 1) + LEAD + NR * done // (2 * AREA) + FAR_AHEAD
                while (time.exp_read[0] > time.pe + 0.1 and time.row_read[0] <= time.pe + 0.05
                        and row_at < min(ahead, row_end, NR * (NG + 1) + LEAD - 3)):
                    rows_to(row_at + 1)
                steps.append(("exp", q, u, k))
                time.exp(w * pack(w))
                done += w * pack(w)
                rows_fit(NR * (q + 1) + LEAD + NR * done // (2 * AREA)
                         - (3 if (q, u) == (NG - 1, NU - 1) else 0))
                if k == (COLS_PER_UNIT[u] - 1) // 2 and len(pvs) >= LAG:
                    pv()
                    done += HG * UNITS[u - LAG][3]
            pvs.append((q, u))
            rows_fit(NR * (q + 1) + LEAD + NR * done // (2 * AREA) - (3 if (q, u) == (NG - 1, NU - 1) else 0))
            if (q, u) == (NG - 1, NU - 1):
                rows_to(NR * NG + LEAD + NR - 2)
                pv()
                rows_to(NR * NG + LEAD + NR)
                pv()
            clock += 1
            due(u)
    while queue or chores or pending:
        clock += 100
        turned = -TURN_APART
        due(0)
    return steps


def first_rows():
    steps = [("row", 0, f) for f in range(NR)] + [("maxstat", 0)]
    steps += [("row", 1, f) for f in range(LEAD // 2)] + [("max", 0)]
    return steps + [("row", 1, f) for f in range(LEAD // 2, LEAD)]


PLAN = {kind: plan(kind) for kind in ("first", "mid", "last")}
PREP = [(c, what) for c in range(2) for what in ("norm", "q", "k", "v")]
DIAG = [n for n in range(NU) if UNITS[n][1] // 4 == UNITS[n][0]]
USES = {kind: [s for s in PLAN[kind] if s[0] in ("max", "norm", "prep", "post")] for kind in PLAN}
TURN0 = len(PREP) + 1
BATCH_TURNS = TURN0 + len(USES["first"]) + (B - 2) * len(USES["mid"]) + len(USES["last"])


def turn(b, kind, step):
    before = 0 if kind == "first" else len(USES["first"]) + len(USES["mid"]) * (b - 1)
    return TURN0 + before + USES[kind].index(step)


def ring(fills, banks):
    last_user = {k % banks: k - fills for k in range(fills)}
    out = []
    for k in range(fills):
        out.append((k % banks, last_user[k % banks]))
        last_user[k % banks] = k
    return out


XBANK = ring(NG * NX, XR)
RBANK = ring(NG * NR, RR)
SLOT_COUNT = 6 * 16
PART_COUNT = 16
SHIFT_COUNT = 16
PV_FREE = PR


def adaln_block(nc, x, qaT, kaT, qb, kb, vwT, owT, v_b, o_b, cT, wmod, gate_w, gate_b,
                up_w, up_b, down_w, down_b, sw_up, sb_up, sw_down, sb_down, out):
    parts_dram = nc.dram_tensor("qk_parts", [B, 2, 3, NG, HD, HG * T], BF16).ap()
    routed_dram = nc.dram_tensor("routed_rows", [NS * SLOTS, F32_ROW], F32).ap()
    result_dram = nc.dram_tensor("routed_results", [2 * B * T, D], F32).ap()
    ctx = ExitStack()
    with ctx:
        def sb(name, shape, dt=F32):
            return ctx.enter_context(nc.sbuf_tensor(name, shape, dt))

        def sem(name):
            return ctx.enter_context(nc.semaphore(name))

        x_sb = sb("x_sb", [P, NT, D])
        y_all = sb("y_all", [P, NT, D])
        v_all = sb("v_all", [P, NT, D])
        QK = sb("QK", [P, 2 * NG * HG * T], BF16)
        probs = sb("probs", [P, PR * HG * CH])
        vg = sb("vg", [P, 2, TT, HG, 32])
        xn = sb("xn", [P, 2, 4, D])
        hT = sb("hT", [P, 2, CH])
        qf = sb("qf", [P, 2, CH])
        rest = sb("rest", [P, 2, CH])
        parts = sb("parts", [P, 2, 3, CH], BF16)
        o_sb = sb("o_sb", [P, 2, CH])
        stats = sb("stats", [P, 2, 4, 6])
        mv = sb("mv", [P, 2, 4, 2])
        rstd = sb("rstd", [P, 2, 4])
        mhalf = sb("mhalf", [P, 4])
        rowmax = sb("rowmax", [P, 2, HG, TT, 2])
        gmax = sb("gmax", [P, 2, HG * TT])
        grest = sb("grest", [P, 2, HG * TT])
        gparts = sb("gparts", [P, 2, 3, HG * TT], BF16)
        shift = sb("shift", [3 * HG * TT, 2, P], BF16)
        rden = sb("rden", [P, 2, 4 * HG])
        ident = sb("ident", [P, P])
        identb = sb("identb", [P, P], BF16)
        maskb = sb("maskb", [P, P], BF16)
        ones16 = sb("ones16", [16, T], BF16)
        wq = sb("wq", [P, D])
        wk = sb("wk", [P, D])
        wv = sb("wv", [P, D])
        wo = sb("wo", [P, D])
        wog = sb("wog", [P, B, D])
        vb_sb = sb("vb_sb", [P, D])
        ob_sb = sb("ob_sb", [P, D])
        obg = sb("obg", [P, B, D])
        cT_sb = sb("cT_sb", [P, B])
        silu = sb("silu", [P, 3, B])
        wm = sb("wm", [P, 6 * D])
        modT = sb("modT", [P, 6, B])
        modc = sb("modc", [P, 2])
        gates = sb("gates", [P, 2, B, D])
        gw = sb("gw", [P, 32])
        gb_sb = sb("gb_sb", [P, 1])
        ub = sb("ub", [P, NE, IT])
        db_sb = sb("db_sb", [NE, D])
        score = sb("score", [P, NT, E])
        below = sb("below", [P, E, E])
        rank = sb("rank", [P, NT, E])
        wsum = sb("wsum", [P, NT])
        wts = sb("wts", [P, NT, NE])
        st2 = sb("st2", [P, 2, 4, 6])
        mv2 = sb("mv2", [P, 2, 4, 2])
        rs2 = sb("rs2", [P, 2, 4])
        amax = sb("amax", [P, 2, 4])
        scale_row = sb("scale_row", [P, B, D])
        empty_row = sb("empty_row", [P, F32_ROW])
        earlier = sb("earlier", [P, P])
        tile_start = sb("tile_start", [P, MOST])
        tile_number = sb("tile_number", [1, NS])
        expert_tiles = sb("expert_tiles", [P, 3, E])
        expert_f = sb("expert_f", [1, NS])
        expert_of = sb("expert_of", [1, NS], I32)
        row_at = sb("row_at", [P, 2, NT], U32)
        ubr = sb("ubr", [P, SCHUNK, IT])
        QS, KS = QK[:, 0:NG * HG * T], QK[:, NG * HG * T:2 * NG * HG * T]
        QS4 = QS[:, :].rearrange("p (g h t) -> p g h t", g=NG, h=HG)
        KS4 = KS[:, :].rearrange("p (g h t) -> p g h t", g=NG, h=HG)
        pr4 = probs[:, :].rearrange("p (s h t) -> p s h t", s=PR, h=HG)
        qaT_sb = probs[:, 0:1024].rearrange("p (n d) -> p n d", n=8)
        kaT_sb = probs[:, 1024:2048].rearrange("p (n d) -> p n d", n=8)
        qbd = probs[:, 2048:2176].rearrange("p (n d) -> p n d", n=8)
        kbd = probs[:, 2176:2304].rearrange("p (n d) -> p n d", n=8)
        siluB = probs[:, 2304:2304 + B * P].rearrange("p (b m) -> p b m", b=B)
        gsign = probs[:, 2816:2816 + 2 * B * D].rearrange("p (j b d) -> p j b d", j=2, b=B)
        qk = QK[:, :].bitcast(F32)
        rows_end = NT * 2 * F32_ROW
        h2rows = qk[:, 0:rows_end].rearrange("p (n r d) -> p n r d", n=NT, r=2)
        routed = qk[:, 0:2 * NT * D].rearrange("p (r n d) -> p r n d", r=2, n=NT)
        at = rows_end + E * I
        uw = qk[:, rows_end:at].rearrange("p (e i) -> p e i", e=E)
        shared_uw = qk[:, at:at + I]
        shared_dw = qk[:, at + I:at + 2 * I].rearrange("p (c h) -> p c h", c=IT)
        at += 2 * I
        larger = QK[:, 2 * at:2 * at + NT * E * E].rearrange("p (n e f) -> p n e f", n=NT, e=E)
        equal = QK[:, 2 * at + NT * E * E:2 * at + 2 * NT * E * E].rearrange("p (n e f) -> p n e f", n=NT, e=E)
        fin = qk[:, rows_end:rows_end + NC * CH].rearrange("p (s n d) -> p s n d", s=NC, n=4)
        shift_row = wm[:, 0:B * D].rearrange("p (b d) -> p b d", b=B)
        not_first = wm[:, B * D:B * D + E * NT].rearrange("p (e n) -> p e n", e=E)
        ones128 = wo
        by_rank = xn[:, :, :, :].rearrange("p a n d -> p (a n d)").rearrange("p (a n e) -> p a n e", a=4, n=NT)
        qf_flat = qf[:, :, :].rearrange("p a t -> p (a t)")
        chosen = qf_flat[:, 0:NT * E].rearrange("p (n e) -> p n e", n=NT)
        position = qf_flat[:, NT * E:2 * NT * E].rearrange("p (n e) -> p n e", n=NT)
        totals = qf_flat[:, NT * E:2 * NT * E].rearrange("p (e n) -> p e n", e=E)
        running = qf_flat[:, 2 * NT * E:3 * NT * E].rearrange("p (e n) -> p e n", e=E)
        before_tile = qf_flat[:, 3 * NT * E:4 * NT * E].rearrange("p (e n) -> p e n", e=E)
        picked = wk[:, 0:4 * NT].rearrange("p (a n) -> p a n", a=4)
        filled = wq[:, 0:E * MOST].rearrange("p (e k) -> p e k", e=E)
        past = ones16[0:1, 0:2 * NS * E].bitcast(F32).rearrange("p (k e) -> p k e", k=NS)
        amax_inv = rs2
        dw = v_all[:, :, :].rearrange("p (e c) h -> p e c h", e=E)
        wT = rest[0:NE, :, :]
        y_chunk, yT = rest, hT
        logitsT = rest
        h2T = probs[:, NT * P:2 * NT * P]
        xn2 = y_all
        acc = y_all
        hact = probs[:, 0:2 * IT * CH].rearrange("p (s c t) -> p s c t", s=2, c=IT)
        vg_flat = vg[:, :, :, :, :].rearrange("p s j h d -> p (s j h d)")
        ur = vg_flat[:, 0:2 * I].rearrange("p (s i) -> p s i", s=2)
        dr = vg_flat[:, 2 * I:4 * I].rearrange("p (s c h) -> p s c h", s=2, c=IT)
        ring = SCHUNK * ST * F32_ROW
        slot_rows = qk[:, 0:ring].rearrange("p (s t d) -> p s t d", s=SCHUNK, t=ST)
        slotT = hT[:, :, 0:SLOTS]
        slot_out = qk[:, ring:ring + SCHUNK * ST * D].rearrange("p (s t d) -> p s t d", s=SCHUNK, t=ST)

        ps = [ctx.enter_context(nc.psum_tensor(f"bank{n}", [P, CH], F32)) for n in range(8)]
        row_bank, exp_bank, out_bank, turn_bank = ps[0:RR], ps[RR:RR + XR], ps[RR + XR:RR + XR + 2], ps[7]
        turn_b16 = turn_bank[0:3 * HG * TT, 0:P // 2].bitcast(BF16)

        waited_pool = sem("waited_pool")
        waited_dve = sem("waited_dve")
        x_first = sem("x_first")
        x_rest = sem("x_rest")
        small_loaded = sem("small_loaded")
        lowrank_loaded = sem("lowrank_loaded")
        lowrank_zeroed = sem("lowrank_zeroed")
        consts_zeroed = sem("consts_zeroed")
        consts_made = sem("consts_made")
        vg_ready = sem("vg_ready")
        ones_stored = sem("ones_stored")
        silu_exp = sem("silu_exp")
        silu_step = sem("silu_step")
        silu_done = sem("silu_done")
        qk_folded = sem("qk_folded")
        qk_copied = sem("qk_copied")
        mod_filled = sem("mod_filled")
        gates_filled = sem("gates_filled")
        o_folded = sem("o_folded")
        mod_step = sem("mod_step")
        mod_done = sem("mod_done")
        modrow_done = sem("modrow_done")
        turn_filled = sem("turn_filled")
        turn_free = sem("turn_free")
        stat_step = sem("stat_step")
        var_done = sem("var_done")
        rstd_done = sem("rstd_done")
        norm_done = sem("norm_done")
        split_step = [sem("q_split_step"), sem("k_split_step")]
        split_done = [sem("q_split_done"), sem("k_split_done")]
        parts_stored = [sem("q_parts_stored"), sem("k_parts_stored")]
        slot_loaded = [sem(f"slot_loaded{q}") for q in range(NG)]
        shift_loaded = [sem(f"shift_loaded{q}") for q in range(NG)]
        vg_done = sem("vg_done")
        row_filled = sem("row_filled")
        row_free = sem("row_free")
        gmax_done = sem("gmax_done")
        gpart_step = sem("gpart_step")
        exp_filled = sem("exp_filled")
        exp_done = sem("exp_done")
        tri_done = sem("tri_done")
        pv_done = sem("pv_done")
        out_copied = sem("out_copied")
        rden_done = sem("rden_done")
        ffn_loaded = sem("ffn_loaded")
        bias_loaded = sem("bias_loaded")
        var2_done = sem("var2_done")
        y_fetched = sem("y_fetched")
        var2_step = sem("var2_step")
        rows2_step = sem("rows2_step")
        rows2_done = sem("rows2_done")
        last_rows2_step = sem("last_rows2_step")
        last_rows2_done = sem("last_rows2_done")
        last_rstd = sem("last_rstd")
        gate_zeroed = sem("gate_zeroed")
        ones_made = sem("ones_made")
        logits_filled = sem("logits_filled")
        logits_copied = sem("logits_copied")
        h2_filled = sem("h2_filled")
        h2_done = sem("h2_done")
        gate_filled = sem("gate_filled")
        gate_exp = sem("gate_exp")
        route_step = sem("route_step")
        rank_step = sem("rank_step")
        wts_done = sem("wts_done")
        wt_filled = sem("wt_filled")
        wt_copied = sem("wt_copied")
        bias_filled = sem("bias_filled")
        acc_started = sem("acc_started")
        prefilled = sem("prefilled")
        route_consts = sem("route_consts")
        chosen_ready = sem("chosen_ready")
        counted = sem("counted")
        shared_loaded = sem("shared_loaded")
        totals_done = sem("totals_done")
        table_done = sem("table_done")
        positions_done = sem("positions_done")
        dest_made = sem("dest_made")
        h2rows_done = sem("h2rows_done")
        second_rows = sem("second_rows")
        rows_sent = sem("rows_sent")
        shared_up = sem("shared_up")
        shared_gelu = sem("shared_gelu")
        shared_down = sem("shared_down")
        shared_copied = sem("shared_copied")
        slot_rows_loaded = [sem(f"slot_rows_loaded{k}") for k in range(SCHUNK)]
        slotT_filled = sem("slotT_filled")
        slotT_copied = sem("slotT_copied")
        up_copied = sem("up_copied")
        down_copied = sem("down_copied")
        slot_gelu = sem("slot_gelu")
        slot_up = sem("slot_up")
        slot_down = sem("slot_down")
        slot_weighted = sem("slot_weighted")
        results_sent = [sem(f"results_sent{k}") for k in range(SCHUNK)]
        results_loaded = [sem(f"results_loaded{c}") for c in range(NC)]
        rank0_added = sem("rank0_added")
        fin_step = sem("fin_step")
        inverted = sem("inverted")
        normalised = sem("normalised")
        gated = sem("gated")
        fin_done = sem("fin_done")
        stored = sem("stored")

        block = ctx.enter_context(nc.Block())
        xt = x.rearrange("(n p) d -> p n d", p=P)
        ot = out.rearrange("(n p) d -> p n d", p=P)

        def batches(eng, body):
            body(0, "first")
            with eng.Fori(1, B - 1) as b:
                body(b, "mid")
            body(B - 1, "last")

        def slot_tiles(eng, step):
            for k in range(SCHUNK):
                step(0, k, False)
            with eng.Fori(1, NS // SCHUNK) as turn_of_ring:
                for k in range(SCHUNK):
                    step(turn_of_ring, k, False)
            for k in range(NS % SCHUNK):
                step(NS // SCHUNK, k, True)


        def split(eng, b, c, side, t, n):
            if n == 0:
                eng.wait_ge(turn_free, t + 1)
                eng.tensor_tensor(rest[:, side, :], qf[:, side, :], parts[:, side, 0, :], ALU.subtract)\
                    .then_inc(split_step[side], 1)
            elif n == 1:
                eng.wait_ge(split_step[side], 2 * (2 * b + c) + 1)
                eng.sem_inc(waited_pool if eng is nc.gpsimd else waited_dve, 1)
                eng.tensor_copy(parts[:, side, 1, :], rest[:, side, :]).then_inc(split_step[side], 1)
            else:
                eng.wait_ge(split_step[side], 2 * (2 * b + c) + 2)
                eng.tensor_tensor(parts[:, side, 2, :], rest[:, side, :], parts[:, side, 1, :], ALU.subtract)\
                    .then_inc(split_done[side], 1)

        def units(b, q):
            return NU * (NG * b + q) + PV_FREE

        def exps(b, q, u):
            return NX * (NG * b + q) + sum(COLS_PER_UNIT[:u + 1]) + XR

        @block.sync
        def _(sp):
            sp.dma_start(x_sb[:, 0:TT, :], xt[:, 0:TT, :]).then_inc(x_first, 16)
            sp.wait_ge(ones_made, 1)
            for r in range(KA, KB):
                sp.dma_start(KS[r:r + 1, :], ones16[:, :]).then_inc(ones_stored, 16)
            sp.dma_start(cT_sb[:, :], cT).then_inc(small_loaded, 16)
            sp.dma_start(wm[:, :], wmod).then_inc(small_loaded, 16)
            sp.dma_start(wv[:, :], vwT).then_inc(small_loaded, 16)
            sp.dma_start(wo[:, :], owT).then_inc(small_loaded, 16)
            sp.dma_start(vb_sb[:, :], v_b.broadcast_to([P, D])).then_inc(small_loaded, 16)
            sp.dma_start(ob_sb[:, :], o_b.broadcast_to([P, D])).then_inc(small_loaded, 16)
            sp.wait_ge(gate_zeroed, 2)
            sp.dma_start(gw[:, 0:E], gate_w).then_inc(bias_loaded, 16)
            for q in range(4):
                sp.dma_start(gb_sb[32 * q:32 * q + E, :], gate_b).then_inc(bias_loaded, 16)
            sp.dma_start(ub[:, 0:E, :], up_b).then_inc(bias_loaded, 16)
            sp.dma_start(ub[:, E, :], sb_up).then_inc(bias_loaded, 16)
            sp.dma_start(db_sb[0:E, :], down_b).then_inc(bias_loaded, 16)
            sp.dma_start(db_sb[E:NE, :], sb_down).then_inc(bias_loaded, 16)

            def store_parts(b, c, side):
                sp.wait_ge(split_done[side], 2 * b + c + 1)
                dst = parts_dram[bass.ds(b, 1), side, :, :, :, :].rearrange("b j g d (h t) -> (b g d h) j t", h=HG)
                sp.dma_start(dst[:, :, CH * c:CH * c + CH], parts[:, side, :, :]).then_inc(parts_stored[side], 16)

            def load_slot(b, q):
                for i in range(3):
                    at = slice(3 * HD * i, 3 * HD * (i + 1))
                    q_part = parts_dram[bass.ds(b, 1), 0, i, q, :, :].rearrange("b d f -> (b d) f")
                    sp.dma_start(QS[at, HG * T * q:HG * T * (q + 1)], q_part.unsqueeze(0).broadcast_to([3, HD, HG * T]))\
                      .then_inc(slot_loaded[q], 16)
                    k_parts = parts_dram[bass.ds(b, 1), 1, :, q, :, :].rearrange("b j d f -> (b j) d f")
                    sp.dma_start(KS[at, HG * T * q:HG * T * (q + 1)], k_parts).then_inc(slot_loaded[q], 16)

            def store_shift(b, q, t):
                sp.wait_ge(turn_free, t + 1)
                sp.dma_start(QS4[KA:KB, q % NG, :, :], shift[:, q % 2, :]).then_inc(shift_loaded[q % NG], 16)

            for c in range(2):
                for side in range(2):
                    store_parts(0, c, side)
            for side in range(2):
                sp.wait_ge(parts_stored[side], 2 * PART_COUNT)
            load_slot(0, 0)
            sp.dma_start(x_sb[:, TT:NT, :], xt[:, TT:NT, :]).then_inc(x_rest, 16)
            for q in range(1, NG):
                load_slot(0, q)
            store_shift(0, 0, TURN0 - 1)
            sp.wait_ge(route_consts, 6)
            sp.dma_start(routed_dram.rearrange("(n p) d -> p n d", p=P),
                         empty_row[:, :].unsqueeze(1).broadcast_to([P, NS * ST, F32_ROW])).then_inc(prefilled, 16)

            def body(b, kind):
                last = kind == "last"
                for s in PLAN[kind]:
                    if s[0] == "max":
                        store_shift(b, s[1], turn(b, kind, s))
                    elif s[0] == "split" and s[3] == 2:
                        store_parts(b + 1, s[1], s[2])
                    elif s[0] == "exp" and s[2:] == (4, 0) and s[1] >= 1 and not last:
                        q = s[1] - 1
                        if q >= 1:
                            sp.wait_ge(exp_filled, NX * (NG * b + q + 1))
                            load_slot(b + 1, q)
                    if s[0] == "load":
                        for side in range(2):
                            sp.wait_ge(parts_stored[side], 2 * PART_COUNT * (b + 2))
                        sp.wait_ge(exp_filled, NX * (NG * b + 1))
                        load_slot(b + 1, 0)
                if not last:
                    sp.wait_ge(exp_filled, NX * NG * (b + 1))
                    load_slot(b + 1, NG - 1)

            batches(sp, body)
            sp.wait_ge(exp_filled, NX * NG * B)
            sp.wait_ge(row_filled, NR * NG * B)
            sp.dma_start(shared_uw, sw_up).then_inc(shared_loaded, 16)
            sp.dma_start(shared_dw, sw_down.rearrange("(c p) h -> p c h", p=P)).then_inc(shared_loaded, 16)
            sp.dma_start(uw, up_w).then_inc(ffn_loaded, 16)
            sp.wait_ge(vg_done, NG * B)
            for e in range(E):
                sp.dma_start(dw[:, e, :, :], down_w[e, :, :].rearrange("(c p) h -> p c h", p=P)).then_inc(ffn_loaded, 16)

            sp.wait_ge(rows_sent, 16 * 2 * NT)
            rd = routed_dram.rearrange("(n t p) d -> p n t d", t=ST, p=P)

            def load(j, k, peeled):
                if not isinstance(j, int) or j > 0:
                    sp.wait_ge(results_sent[k], 16 * ST * j)
                sp.dma_start(slot_rows[:, k, :, :],
                             rd[:, bass.ds(SCHUNK * j + k, 1), :, :].rearrange("p n t d -> p (n t) d"))\
                  .then_inc(slot_rows_loaded[k], 16)

            slot_tiles(sp, load)
            for k in range(SCHUNK):
                sp.wait_ge(results_sent[k], 16 * ST * ((NS + SCHUNK - 1 - k) // SCHUNK))
            res = result_dram.rearrange("(r n p) d -> p r n d", r=2, p=P)
            for c in range(NC):
                for r in range(2):
                    sp.dma_start(routed[:, r, 4 * c:4 * c + 4, :], res[:, r, 4 * c:4 * c + 4, :])\
                      .then_inc(results_loaded[c], 16)
            for m in range(NC):
                sp.wait_ge(fin_done, m + 1)
                sp.dma_start(ot[:, 4 * m:4 * m + 4, :], fin[:, m, :, :]).then_inc(stored, 16)
            sp.wait_ge(stored, 16 * NC)

        @block.gpsimd
        def _(pool):
            pool.memset(ident[:, :], 0.0).then_inc(consts_zeroed, 1)
            pool.memset(identb[:, :], 0.0).then_inc(consts_zeroed, 1)
            pool.memset(maskb[:, :], 0.0).then_inc(consts_zeroed, 1)
            pool.memset(below[:, :, :], 1.0).then_inc(consts_zeroed, 1)
            pool.memset(mhalf[:, :], -0.5).then_inc(consts_zeroed, 1)
            pool.memset(vg[:, :, :, :, :], 0.0).then_inc(consts_zeroed, 1)
            pool.wait_ge(consts_zeroed, 6)
            for m in (ident, identb):
                pool.affine_select(out=m[:, :], in_=m[:, :], compare_op=ALU.not_equal, fill=1.0, base=0,
                                   pattern=[[-1, P]], channel_multiplier=1).then_inc(consts_made, 1)
            pool.affine_select(out=maskb[:, :], in_=maskb[:, :], compare_op=ALU.is_ge, fill=NEG, base=0,
                               pattern=[[-1, P]], channel_multiplier=1).then_inc(consts_made, 1)
            pool.affine_select(out=below[:, :, :], in_=below[:, :, :], compare_op=ALU.is_gt, fill=0.0, base=0,
                               pattern=[[1, E], [-1, E]], channel_multiplier=0).then_inc(consts_made, 1)
            pool.memset(vg[:, :, :, :, HD:HD + 1], 1.0).then_inc(vg_ready, 1)
            pool.memset(earlier[:, :], 1.0).then_inc(route_consts, 1)
            pool.memset(empty_row[:, :], 0.0).then_inc(route_consts, 1)
            pool.wait_ge(route_consts, 2)
            pool.iota(empty_row[:, DEST_COL:DEST_COL + 1].bitcast(U32), pattern=[[0, 1]], base=NOWHERE,
                      channel_multiplier=0).then_inc(route_consts, 1)
            pool.sem_inc(waited_pool, 1)
            pool.affine_select(out=earlier[:, :], in_=earlier[:, :], compare_op=ALU.is_gt, fill=0.0, base=0,
                               pattern=[[1, P]], channel_multiplier=-1).then_inc(route_consts, 1)
            pool.iota(tile_start[:, :], pattern=[[SLOTS, MOST]], base=0, channel_multiplier=0,
                      allow_small_or_imprecise_dtypes=True).then_inc(route_consts, 1)
            pool.iota(tile_number[:, :], pattern=[[1, NS]], base=0, channel_multiplier=0,
                      allow_small_or_imprecise_dtypes=True).then_inc(route_consts, 1)

            def norm(b, c):
                m = 2 * b + c
                pool.wait_ge(var_done, m + 1)
                pool.tensor_tensor(rstd[:, c, :], rstd[:, c, :], mhalf[:, 0:4], ALU.pow).then_inc(rstd_done, 1)

            def fetch(b, c, n, splits):
                if n == 0:
                    pool.wait_ge(split_done[c], splits // 2)
                    pool.sem_inc(waited_pool, 1)
                    pool.tensor_copy(y_chunk[:, c, :], y_all[:, bass.ds(TT * b + 4 * c, 4), :].rearrange(
                        "p n d -> p (n d)")).then_inc(y_fetched, 1)
                    return
                xc = x_sb[:, bass.ds(TT * b + 4 * c, 4), :]
                pool.tensor_tensor(xc, xc, obg[:, bass.ds(b, 1), :].broadcast_to([P, 4, D]), ALU.add)\
                    .then_inc(y_fetched, 1)

            def rows2(b, c, n):
                if n == 0:
                    pool.wait_ge(var2_done, 2 * b + c + 1)
                    pool.tensor_tensor(rs2[:, c, :], rs2[:, c, :], mhalf[:, :], ALU.pow).then_inc(rows2_step, 1)
                    return
                src = x_sb[:, bass.ds(TT * b + 4 * c, 4), :]
                dst = xn2[:, bass.ds(TT * b + 4 * c, 4), :]
                other, op = ((mv2[:, c, :, 0:1].broadcast_to([P, 4, D]), ALU.subtract),
                             (rs2[:, c, :].unsqueeze(2).broadcast_to([P, 4, D]), ALU.mult),
                             (scale_row[:, bass.ds(b, 1), :].broadcast_to([P, 4, D]), ALU.mult),
                             (shift_row[:, bass.ds(b, 1), :].broadcast_to([P, 4, D]), ALU.add))[n - 1]
                pool.wait_ge(rows2_step, 4 * (2 * b + c) + n)
                pool.sem_inc(waited_pool, 1)
                pool.tensor_tensor(dst, src if n == 1 else dst, other, op).then_inc(
                    rows2_step if n < 4 else rows2_done, 1)

            def group_v(b, q):
                pool.sem_inc(waited_pool, 1)
                last = pool.tensor_tensor(
                    vg[:, q % 2, :, :, 0:HD],
                    v_all[:, bass.ds(TT * b, TT), 32 * q:32 * q + 32].rearrange("p n (h d) -> p n h d", h=HG),
                    vb_sb[:, 32 * q:32 * q + 32].rearrange("p (h d) -> p h d", h=HG).unsqueeze(1).broadcast_to(
                        [P, TT, HG, HD]), ALU.add)
                last.then_inc(vg_done, 1)

            def maxima(b, q):
                n, r = NG * b + q, q % 2
                pool.wait_ge(gmax_done, n + 1)
                pool.sem_inc(waited_pool, 1)
                pool.tensor_scalar(gparts[:, r, 0, :], gmax[:, r, :], -1.0, None, ALU.mult).then_inc(gpart_step, 1)
                pool.tensor_scalar(grest[:, r, :], gmax[:, r, :], -1.0, None, ALU.mult).then_inc(gpart_step, 1)
                pool.wait_ge(gpart_step, 5 * n + 2)
                pool.tensor_tensor(grest[:, r, :], grest[:, r, :], gparts[:, r, 0, :], ALU.subtract)\
                    .then_inc(gpart_step, 1)
                pool.wait_ge(gpart_step, 5 * n + 3)
                pool.sem_inc(waited_pool, 1)
                pool.tensor_copy(gparts[:, r, 1, :], grest[:, r, :]).then_inc(gpart_step, 1)
                pool.wait_ge(gpart_step, 5 * n + 4)
                pool.tensor_tensor(gparts[:, r, 2, :], grest[:, r, :], gparts[:, r, 1, :], ALU.subtract)\
                    .then_inc(gpart_step, 1)

            pool.wait_ge(x_first, 16)
            norm(0, 0)
            norm(0, 1)
            for t, (c, what) in enumerate(PREP):
                if what == "q":
                    for n in range(3):
                        split(pool, 0, c, 0, t, n)
            pool.wait_ge(vg_ready, 1)
            pool.wait_ge(turn_free, len(PREP))
            group_v(0, 0)
            maxima(0, 0)
            pool.wait_ge(x_rest, 16)

            def body(b, kind):
                last = kind == "last"
                for s in PLAN[kind]:
                    if s[0] == "exp":
                        _, q, u, k = s
                        if (u, k) == (4, 0) and q < NG - 1:
                            pool.wait_ge(pv_done, units(b, q))
                            group_v(b, q + 1)
                        if u in DIAG and k == COLS_PER_UNIT[u] - 1:
                            pool.wait_ge(exp_done, exps(b, q, u))
                            pool.sem_inc(waited_pool, 1)
                            pool.affine_select(out=pr4[:, u % PR, :, 0:P], in_=pr4[:, u % PR, :, 0:P],
                                               compare_op=ALU.is_ge, fill=0.0, base=0,
                                               pattern=[[0, HG], [1, P]], channel_multiplier=-1)\
                                .then_inc(tri_done, 1)
                    elif s[0] == "maxstat":
                        maxima(b, s[1])
                    elif s[0] == "fetch":
                        if s[1:] == (0, 0):
                            pool.wait_ge(turn_free, TURN0 + len(USES["first"]) + len(USES["mid"]) * (b - 1))
                        fetch(b - 1, s[1], s[2], 4 * B if last else 4 * (b + 2))
                    elif s[0] == "rows2":
                        rows2(b - 1, s[1], s[2])
                    elif s[0] == "stat":
                        norm(b + 1, s[1])
                    elif s[0] == "split":
                        _, c, side, n = s
                        split(pool, b + 1, c, side, turn(b, kind, ("prep", "qk"[side], c)), n)
                if not last:
                    pool.wait_ge(turn_free, turn(b, kind, ("prep", "v", 1)) + 1)
                    pool.wait_ge(pv_done, units(b, NG - 1))
                    group_v(b + 1, 0)

            batches(pool, body)
            pool.wait_ge(turn_free, BATCH_TURNS)
            for c in range(2):
                fetch(B - 1, c, 1, 4 * B)
            for c in range(2):
                pool.wait_ge(var2_done, 2 * (B - 1) + c + 1)
                pool.tensor_tensor(rs2[:, c, :], rs2[:, c, :], mhalf[:, :], ALU.pow).then_inc(last_rstd, 1)
            pool.iota(h2rows[:, :, :, DEST_COL].bitcast(U32), pattern=[[P, NT], [B * T, 2]], base=0,
                      channel_multiplier=1).then_inc(dest_made, 1)
            pool.wait_ge(prefilled, 16)
            pool.wait_ge(dest_made, 1)
            pool.wait_ge(positions_done, 1)
            for r in range(2):
                for n in range(NT):
                    if n % 4 == 0:
                        if r == 0:
                            pool.wait_ge(h2rows_done, n // 4 + 1)
                        else:
                            pool.wait_ge(second_rows, n // 4 + 1)
                    pool.indirect_dma_start(routed_dram, bass.IndirectOffsetOnAxis(ap=row_at[:, r, n:n + 1], axis=0),
                                            h2rows[:, n, r, :], None).then_inc(rows_sent, 16)

            def send(j, k, peeled):
                pool.wait_ge(slot_weighted, SCHUNK * j + k + 1 + 2)
                pool.sem_inc(waited_pool, 1)
                for t in range(ST):
                    pool.indirect_dma_start(
                        result_dram, bass.IndirectOffsetOnAxis(ap=slot_rows[:, k, t, DEST_COL:DEST_COL + 1].bitcast(U32),
                                                               axis=0),
                        slot_out[:, k, t, :], None, bounds_check=2 * B * T - 1, oob_is_err=False)\
                        .then_inc(results_sent[k], 16)

            slot_tiles(pool, send)

            for m in range(NC + 2):
                if m < NC:
                    pool.wait_ge(results_loaded[m], 32)
                    a = acc[:, 4 * m:4 * m + 4, :]
                    pool.tensor_tensor(a, a, routed[:, 0, 4 * m:4 * m + 4, :], ALU.add).then_inc(rank0_added, 1)
                if m >= 2:
                    pool.wait_ge(gated, m - 1)
                    pool.tensor_tensor(fin[:, m - 2, :, :], fin[:, m - 2, :, :], x_sb[:, 4 * m - 8:4 * m - 4, :],
                                       ALU.add).then_inc(fin_done, 1)

        @block.scalar
        def _(act):
            act.dma_start(qaT_sb, qaT).then_inc(lowrank_loaded, 16)
            act.dma_start(kaT_sb, kaT).then_inc(lowrank_loaded, 16)
            act.wait_ge(lowrank_zeroed, 1)
            for dst, src in ((qbd, qb), (kbd, kb)):
                for h2 in range(2):
                    act.dma_start(dst[R * h2:R * h2 + R, :, HD * h2:HD * h2 + HD], src[R * h2:R * h2 + R, :, :])\
                        .then_inc(lowrank_loaded, 16)
            act.wait_ge(small_loaded, 16 * 6)
            act.activation(silu[:, 0, :], cT_sb[:, :], ACT.Exp, scale=-1.0).then_inc(silu_exp, 1)

            def prep_read(b, c, what, t, first=False):
                act.wait_ge(turn_filled, t + 1)
                if what == "norm":
                    act.activation(hT[:, c, :], turn_bank[:, :], ACT.Identity, bias=modc[:, 0:1], scale=modc[:, 1:2])\
                        .then_inc(turn_free, 1)
                elif what == "v":
                    act.activation(v_all[:, bass.ds(TT * b + 4 * c, 4), :],
                                   turn_bank[:, :].rearrange("p (n d) -> p n d", n=4), ACT.Copy).then_inc(turn_free, 1)
                else:
                    side = "qk".index(what)
                    if not first:
                        act.wait_ge(split_done[side], 2 * b + c)
                        act.wait_ge(parts_stored[side], PART_COUNT * (2 * b + c))
                    scale = SCALE if what == "q" else 1.0
                    act.activation(qf[:, side, :], turn_bank[:, :], ACT.Copy, scale=scale)
                    act.activation(parts[:, side, 0, :], turn_bank[:, :], ACT.Copy, scale=scale).then_inc(turn_free, 1)

            def take_yT(c, t):
                act.wait_ge(turn_filled, t + 1)
                act.activation(yT[:, c, :], turn_bank[:, :], ACT.Copy).then_inc(turn_free, 1)

            def max_read(q, t):
                act.wait_ge(turn_filled, t + 1)
                act.activation(shift[:, q % 2, :], turn_b16, ACT.Copy).then_inc(turn_free, 1)

            act.wait_ge(mod_done, 1)
            for t, (c, what) in enumerate(PREP):
                prep_read(0, c, what, t, first=(c == 0))
            max_read(0, TURN0 - 1)

            def body(b, kind):
                last = kind == "last"
                nx = 0
                for s in PLAN[kind]:
                    if s[0] == "exp":
                        _, q, u, k = s
                        w = UNITS[u][3]
                        h = k * pack(w)
                        if k == 0:
                            act.wait_ge(pv_done, units(b, q) + u + 1 - PR)
                        act.wait_ge(exp_filled, NG * NX * b + nx + 1)
                        act.activation(pr4[:, u % PR, h:h + pack(w), 0:w],
                                       exp_bank[XBANK[nx][0]][:, 0:w * pack(w)].rearrange(
                                           "p (h t) -> p h t", h=pack(w)), ACT.Exp).then_inc(exp_done, 1)
                        nx += 1
                    elif s[0] == "evac":
                        _, q, c = s
                        act.wait_ge(pv_done, units(b, q) + (4 if c == 0 else NU))
                        act.activation(o_sb[:, c, :], out_bank[c][:, :], ACT.Copy).then_inc(out_copied, 1)
                    elif s[0] == "max":
                        max_read(s[1], turn(b, kind, s))
                    elif s[0] == "prep":
                        prep_read(b + 1, s[2], s[1], turn(b, kind, s))
                    elif s[:2] == ("post", "turn"):
                        take_yT(s[2], turn(b, kind, s))

            batches(act, body)
            def take_h2T(c):
                act.wait_ge(h2_filled, c + 1)
                act.activation(h2T[:, CH * c:CH * c + CH], ps[4 + c % 2][:, :], ACT.Copy).then_inc(h2_done, 1)

            def take_logits(g):
                act.wait_ge(logits_filled, g + 1)
                act.activation(logitsT[:, g, :], ps[6][:, :], ACT.Identity, bias=gb_sb[:, 0:1]).then_inc(logits_copied, 1)

            def take_gate(g):
                act.wait_ge(gate_filled, g + 1)
                act.activation(score[:, 16 * g:16 * g + 16, :].rearrange("p (q n) e -> p q n e", q=4),
                               ps[(2, 7)[g]][:, :].rearrange("p (n q k) -> p q n k", n=4, q=4)[:, :, :, 0:E], ACT.Exp,
                               scale=-1.0).then_inc(gate_exp, 1)

            take_yT(0, BATCH_TURNS)
            take_h2T(0)
            take_h2T(1)
            take_h2T(2)
            take_yT(1, BATCH_TURNS + 2)
            take_h2T(3)
            take_logits(0)
            take_h2T(4)
            take_h2T(5)
            take_gate(0)
            take_h2T(6)
            take_h2T(7)
            take_logits(1)
            take_gate(1)
            act.wait_ge(bias_loaded, 16 * 9)

            def shared(c, first=False, copies=True):
                par = c % 2 if isinstance(c, int) else c[1]
                n = c if isinstance(c, int) else c[0]
                for i in range(IT):
                    act.wait_ge(shared_up, IT * n + i + 1)
                    act.wait_ge(shared_down, n + 1)
                    act.activation(hact[:, par, i, :], ps[i][:, :], ACT.Gelu, bias=ub[:, E, i:i + 1])\
                        .then_inc(shared_gelu, 1)
                if not first:
                    copy_out(n - 1, 1 - par)
                act.wait_ge(h2rows_done, n + 1)
                act.activation(h2rows[:, bass.ds(4 * n, 4), 1, 0:D], h2rows[:, bass.ds(4 * n, 4), 0, 0:D], ACT.Copy)\
                    .then_inc(second_rows, 1)

            def copy_out(n, par):
                act.wait_ge(shared_down, n + 1 + 2)
                act.activation(acc[:, bass.ds(4 * n, 4), :].rearrange("p n d -> p (n d)"), ps[4 + par][:, :], ACT.Copy)\
                    .then_inc(shared_copied, 1)

            shared(0, first=True)
            shared(1)
            with act.Fori(1, NC // 2) as j:
                for par in range(2):
                    shared((2 * j + par, par))
            copy_out(NC - 1, 1)
            for c in range(NC):
                act.wait_ge(wt_filled, c + 1)
                if c >= 2:
                    act.wait_ge(bias_filled, c - 1)
                act.activation(wT[:, c % 2, :], ps[c % 2][0:NE, :], ACT.Copy).then_inc(wt_copied, 1)

            def take(j, k):
                act.wait_ge(slotT_filled, SCHUNK * j + k + 1)
                act.activation(slotT[:, k % 2, :], ps[6 + k % 2][:, 0:SLOTS], ACT.Copy).then_inc(slotT_copied, 1)

            def gelus(j, k):
                act.wait_ge(up_copied, SCHUNK * j + k + 1)
                act.wait_ge(slot_down, SCHUNK * j + k + 1)
                for m in range(IT):
                    act.wait_ge(slot_up, IT * (SCHUNK * j + k) + m + 1)
                    act.activation(hact[:, k % 2, m, 0:SLOTS], ps[m][:, 0:SLOTS], ACT.Gelu,
                                   bias=ubr[:, k % SCHUNK, m:m + 1]).then_inc(slot_gelu, 1)

            take(0, 0)
            take(0, 1)
            gelus(0, 0)

            def step(j, k, peeled):
                if not peeled or k + 2 < NS % SCHUNK:
                    take(j, k + 2)
                if not peeled or k + 1 < NS % SCHUNK:
                    gelus(j, k + 1)

            slot_tiles(act, step)

            for m in range(NC):
                act.wait_ge(inverted, m + 1)
                for t in range(4):
                    ins = act.activation(fin[:, m, t, :], acc[:, 4 * m + t, :], ACT.Copy,
                                         scale=amax_inv[:, m % 2, t:t + 1])
                ins.then_inc(normalised, 1)

        @block.tensor
        def _(pe):
            mm, tr = nc.tensor.matmul, nc.tensor.transpose
            pe.wait_ge(lowrank_loaded, 16 * 6)
            for side, (a, bd) in enumerate(((qaT_sb, qbd), (kaT_sb, kbd))):
                for n in range(8):
                    m = mm(ps[0][:, D * side + 16 * n:D * side + 16 * n + 16], a[:, n, :], bd[:, n, :],
                           start=True, stop=True)
            m.then_inc(qk_folded, 1)
            pe.wait_ge(silu_done, 1)
            for j in range(6):
                m = mm(ps[1][:, B * j:B * j + B], wm[:, D * j:D * j + D], silu[:, 2, :], start=True, stop=True)
            m.then_inc(mod_filled, 1)
            pe.wait_ge(consts_made, 4)
            pe.wait_ge(ones_made, 1)
            pe.wait_ge(ones_stored, 48)

            def prep(b, c, what, t):
                m = 2 * b + c
                if t is not None:
                    pe.wait_ge(turn_free, t)
                if what == "norm":
                    pe.wait_ge(norm_done, m + 1)
                    for n in range(4):
                        last = tr(turn_bank[:, P * n:P * n + P], xn[:, c, n, :], ident[:, :])
                elif what == "v":
                    for n in range(4):
                        last = mm(turn_bank[:, P * n:P * n + P], hT[:, c, P * n:P * n + P], wv[:, :],
                                  start=True, stop=True)
                else:
                    last = mm(turn_bank[:, :], (wq if what == "q" else wk)[:, :], hT[:, c, :], start=True, stop=True)
                last.then_inc(turn_filled, 1)

            pe.wait_ge(qk_copied, 2)
            for t, (c, what) in enumerate(PREP):
                prep(0, c, what, t if t else None)
                if t == 3:
                    for bank, j in ((2, 2), (3, 5), (4, 3), (5, 4)):
                        for b in range(B):
                            m = mm(ps[bank][:, D * b:D * b + D], siluB[:, b, :], wm[:, D * j:D * j + D],
                                   start=True, stop=True)
                    m.then_inc(gates_filled, 1)

            def rows(b, q, f, first=False):
                i, c0, w, h0, nh = ROWS[f]
                if f == 0:
                    pe.wait_ge(slot_loaded[q % NG], SLOT_COUNT * (b + 1 + q // NG))
                bank, user = RBANK[NR * (q % NG) + f]
                if not first:
                    pe.wait_ge(row_free, NR * (NG * b + q) + (user + 1 - NR * (q % NG)))
                bank = row_bank[bank]
                diagonal = c0 + w == P * (i + 1)
                for n in range(nh):
                    m = mm(bank[:, w * n:w * n + w], QS4[0:KA, q % NG, h0 + n, P * i:P * i + P],
                           KS4[0:KA, q % NG, h0 + n, c0:c0 + w], start=True, stop=not diagonal)
                    if diagonal:
                        m = mm(bank[:, w * n + w - P:w * n + w], identb[:, :], maskb[:, :],
                               start=False, stop=True)
                m.then_inc(row_filled, 1)

            def max_turn(b, q, t):
                pe.wait_ge(gpart_step, 5 * (NG * b + q) + 5)
                pe.wait_ge(turn_free, t)
                tr(turn_b16, gparts[:, q % 2, :, :].rearrange("p a n -> p (a n)"), identb[:, :])\
                    .then_inc(turn_filled, 1)

            def post(b, step, c, t, at_end=False):
                pe.wait_ge(turn_free, t)
                if step == "turn" and not at_end:
                    pe.wait_ge(y_fetched, 2 * (2 * b + c) + 1)
                for n in range(4):
                    if step == "turn":
                        y_tile = y_all[:, TT * b + 4 * c + n, :] if at_end else y_chunk[:, c, P * n:P * n + P]
                        m = tr(turn_bank[:, P * n:P * n + P], y_tile, ident[:, :])
                    else:
                        m = mm(turn_bank[:, P * n:P * n + P], yT[:, c, P * n:P * n + P],
                               wog[:, bass.ds(b, 1), :].rearrange("p n d -> p (n d)"), start=True, stop=True)
                m.then_inc(turn_filled, 1)

            pe.wait_ge(o_folded, 1)
            for s in first_rows():
                if s[0] == "row":
                    n = NR * s[1] + s[2]
                    rows(0, s[1], s[2], first=n < RR)
                elif s[0] == "max":
                    max_turn(0, 0, TURN0 - 1)

            def body(b, kind):
                last = kind == "last"
                nx = 0
                for s in PLAN[kind]:
                    if s[0] == "row":
                        _, q, f = s
                        rows(b, q, f)
                    elif s[0] == "exp":
                        _, q, u, k = s
                        c, j, t0, w = UNITS[u]
                        h = k * pack(w)
                        if (u, k) == (0, 0):
                            pe.wait_ge(shift_loaded[q], SHIFT_COUNT * (b + 1))
                        bank, user = XBANK[nx]
                        pe.wait_ge(exp_done, NG * NX * b + user + 1 + XR)
                        for n in range(pack(w)):
                            m = mm(exp_bank[bank][:, w * n:w * n + w], KS4[0:KB, q, h + n, P * j:P * j + P],
                                   QS4[0:KB, q, h + n, t0:t0 + w], start=True, stop=True)
                        m.then_inc(exp_filled, 1)
                        nx += 1
                    elif s[0] == "pv":
                        _, q, u = s
                        c, j, t0, w = UNITS[u]
                        if u == 0:
                            pe.wait_ge(vg_done, NG * b + q + 1)
                        if j == 0:
                            pe.wait_ge(out_copied, 2 * (NG * b + q) + c + 1)
                        if u in DIAG:
                            pe.wait_ge(tri_done, len(DIAG) * (NG * b + q) + DIAG.index(u) + 1)
                        else:
                            pe.wait_ge(exp_done, exps(b, q, u))
                        for h in range(HG):
                            m = mm(out_bank[c][32 * h:32 * h + 32, t0 - CH * c:CH], vg[:, q % 2, j, h, :],
                                   pr4[:, u % PR, h, 0:w], start=(j == 0), stop=(j == 4 * c + 3))
                        m.then_inc(pv_done, 1)
                    elif s[0] == "max":
                        max_turn(b, s[1], turn(b, kind, s))
                    elif s[0] == "norm":
                        _, q, c = s
                        pe.wait_ge(out_copied, 2 * (NG * b + q) + c + 1 + 2)
                        pe.wait_ge(turn_free, turn(b, kind, s))
                        for n in range(4):
                            m = tr(turn_bank[:, P * n:P * n + P], o_sb[:, c, P * n:P * n + P], ident[:, :])
                        m.then_inc(turn_filled, 1)
                    elif s[0] == "prep":
                        prep(b + 1, s[2], s[1], turn(b, kind, s))
                    elif s[0] == "post":
                        post(b - 1, s[1], s[2], turn(b, kind, s))

            batches(pe, body)

            def turn_h2(c):
                if c < 2 * (B - 1):
                    pe.wait_ge(rows2_done, c + 1)
                else:
                    pe.wait_ge(last_rows2_done, c - 2 * (B - 1) + 1)
                if c >= 2:
                    pe.wait_ge(h2_done, c - 1)
                for n in range(4):
                    m = tr(ps[4 + c % 2][:, P * n:P * n + P], xn2[:, 4 * c + n, :], ident[:, :])
                m.then_inc(h2_filled, 1)

            def route(g):
                pe.wait_ge(h2_done, 4 * g + 4)
                for q in range(4):
                    c = 4 * g + q
                    m = mm(ps[6][32 * q:32 * q + 32, :], gw[:, :], h2T[:, CH * c:CH * c + CH], start=True, stop=True)
                m.then_inc(logits_filled, 1)

            def turn_logits(g):
                pe.wait_ge(logits_copied, g + 1)
                if g:
                    pe.wait_ge(turn_free, BATCH_TURNS + 4)
                for n in range(4):
                    m = tr(ps[(2, 7)[g]][:, P * n:P * n + P], logitsT[:, g, P * n:P * n + P], ident[:, :])
                m.then_inc(gate_filled, 1)

            pe.wait_ge(exp_done, NG * NX * B + XR)
            pe.wait_ge(row_free, NR * NG * B)
            pe.wait_ge(bias_loaded, 16 * 9)
            post(B - 1, "turn", 0, BATCH_TURNS, at_end=True)
            turn_h2(0)
            turn_h2(1)
            post(B - 1, "proj", 0, BATCH_TURNS + 1)
            turn_h2(2)
            post(B - 1, "turn", 1, BATCH_TURNS + 2, at_end=True)
            turn_h2(3)
            post(B - 1, "proj", 1, BATCH_TURNS + 3)
            route(0)
            turn_h2(4)
            turn_h2(5)
            turn_logits(0)
            turn_h2(6)
            turn_h2(7)
            route(1)
            turn_logits(1)
            pe.wait_ge(shared_loaded, 32)

            def shared_ups(n, par):
                for i in range(IT):
                    pe.wait_ge(shared_gelu, IT * n + i + 1)
                    mm(ps[i][:, :], shared_uw[:, P * i:P * i + P], h2T[:, bass.ds(CH * n, CH)],
                       start=True, stop=True).then_inc(shared_up, 1)

            def shared_downs(n, par):
                pe.wait_ge(shared_gelu, IT * (n + 2))
                pe.wait_ge(shared_copied, n + 1)
                for t in range(4):
                    for i in range(IT):
                        m = mm(ps[4 + par][:, P * t:P * t + P], hact[:, par, i, P * t:P * t + P],
                               shared_dw[:, i, :], start=(i == 0), stop=(i == IT - 1))
                m.then_inc(shared_down, 1)

            shared_ups(0, 0)
            shared_ups(1, 1)
            pe.wait_ge(chosen_ready, 1)
            picks = chosen[:, :, :].rearrange("p n e -> p (n e)")
            mm(ps[7][:, 0:NT * E], earlier[:, :], picks, start=True, stop=True)
            mm(ps[7][:, NT * E:2 * NT * E], ones128[:, :], picks, start=True, stop=True).then_inc(counted, 1)
            shared_downs(0, 0)
            with pe.Fori(1, NC // 2) as j:
                for par in range(2):
                    shared_ups(2 * j + par, par)
                    shared_downs(2 * j + par - 1, 1 - par)
            shared_downs(NC - 1, 1)
            pe.wait_ge(wts_done, 2)
            pe.wait_ge(bias_loaded, 16 * 9)
            pe.wait_ge(shared_gelu, IT * (NC + 1))

            def turn_weights(c):
                if c >= 2:
                    pe.wait_ge(wt_copied, c - 1)
                for n in range(4):
                    m = tr(ps[c % 2][0:NE, P * n:P * n + P], wts[:, 4 * c + n, :], ident[:, :])
                m.then_inc(wt_filled, 1)

            turn_weights(0)
            for c in range(NC):
                if c + 1 < NC:
                    turn_weights(c + 1)
                if c >= 2:
                    pe.wait_ge(acc_started, c - 1)
                pe.wait_ge(wt_copied, c + 1)
                for n in range(4):
                    m = mm(ps[2 + c % 2][:, P * n:P * n + P], wT[:, c % 2, P * n:P * n + P], db_sb[:, :],
                           start=True, stop=True)
                m.then_inc(bias_filled, 1)
            pe.wait_ge(acc_started, NC)

            def turn_rows(j, k):
                pe.wait_ge(slot_rows_loaded[k % SCHUNK], 16 * (j + k // SCHUNK + 1))
                pe.wait_ge(slotT_copied, SCHUNK * j + k + 1)
                for t in range(ST):
                    m = tr(ps[6 + k % 2][:, P * t:P * t + P], slot_rows[:, k % SCHUNK, t, 0:D], ident[:, :])
                m.then_inc(slotT_filled, 1)

            def up(j, k):
                pe.wait_ge(up_copied, SCHUNK * j + k + 1)
                pe.wait_ge(slotT_copied, SCHUNK * j + k + 1 + 2)
                for m in range(IT):
                    pe.wait_ge(slot_gelu, IT * (SCHUNK * j + k) + m + 1)
                    mm(ps[m][:, 0:SLOTS], ur[:, k % 2, P * m:P * m + P], slotT[:, k % 2, :],
                       start=True, stop=True).then_inc(slot_up, 1)

            turn_rows(0, 0)
            turn_rows(0, 1)
            up(0, 0)

            def step(j, k, peeled):
                if not peeled or k + 2 < NS % SCHUNK:
                    turn_rows(j, k + 2)
                if not peeled or k + 1 < NS % SCHUNK:
                    up(j, k + 1)
                pe.wait_ge(slot_gelu, IT * (SCHUNK * j + k + 2))
                pe.wait_ge(down_copied, SCHUNK * j + k + 1)
                pe.wait_ge(slot_weighted, SCHUNK * j + k + 1)
                for t in range(ST):
                    for m in range(IT):
                        last = mm(ps[4 + k % 2][:, P * t:P * t + P], hact[:, k % 2, m, P * t:P * t + P],
                                  dr[:, k % 2, m, :], start=(m == 0), stop=(m == IT - 1))
                last.then_inc(slot_down, 1)

            slot_tiles(pe, step)

        @block.vector
        def _(dve):
            dve.memset(probs[:, 2048:2304], 0.0).then_inc(lowrank_zeroed, 1)
            dve.memset(ones16[:, :], 1.0).then_inc(ones_made, 1)
            dve.memset(gw[:, :], 0.0).then_inc(gate_zeroed, 1)
            dve.memset(gb_sb[:, :], 0.0).then_inc(gate_zeroed, 1)

            def stat(b, c):
                m = 2 * b + c
                for t in range(4):
                    ins = dve.bn_stats(stats[:, c, t, :], x_sb[:, bass.ds(TT * b + 4 * c + t, 1), :].rearrange(
                        "p n d -> p (n d)"))
                ins.then_inc(stat_step, 1)
                dve.wait_ge(stat_step, 2 * m + 1)
                dve.sem_inc(waited_dve, 1)
                for t in range(4):
                    ins = dve.bn_aggr(mv[:, c, t, :], stats[:, c, t, :])
                ins.then_inc(stat_step, 1)
                dve.wait_ge(stat_step, 2 * m + 2)
                dve.tensor_scalar(rstd[:, c, :], mv[:, c, :, 1:2].rearrange("p n a -> p (n a)"), EPS, None, ALU.add)\
                    .then_inc(var_done, 1)

            def norm(b, c):
                dve.wait_ge(rstd_done, 2 * b + c + 1)
                for t in range(4):
                    ins = dve.tensor_scalar(xn[:, c, t, :], x_sb[:, bass.ds(TT * b + 4 * c + t, 1), :].rearrange(
                        "p n d -> p (n d)"), mv[:, c, t, 0:1], rstd[:, c, t:t + 1], ALU.subtract, ALU.mult)
                ins.then_inc(norm_done, 1)

            dve.wait_ge(x_first, 16)
            stat(0, 0)
            stat(0, 1)
            norm(0, 0)
            norm(0, 1)
            dve.memset(rowmax[:, :, :, :, :], -3.0e38)
            dve.wait_ge(silu_exp, 1)
            dve.tensor_scalar(silu[:, 1, :], silu[:, 0, :], 1.0, None, ALU.add).then_inc(silu_step, 1)
            dve.wait_ge(silu_step, 1)
            dve.reciprocal(silu[:, 0, :], silu[:, 1, :]).then_inc(silu_step, 1)
            dve.wait_ge(silu_step, 2)
            dve.tensor_tensor(silu[:, 2, :], silu[:, 0, :], cT_sb[:, :], ALU.mult).then_inc(silu_step, 1)
            dve.wait_ge(silu_step, 3)
            dve.tensor_copy(siluB[:, :, :], silu[:, 2, :].unsqueeze(2).broadcast_to([P, B, P])).then_inc(silu_done, 1)
            dve.wait_ge(qk_folded, 1)
            for side, w in enumerate((wq, wk)):
                dve.tensor_copy(w[:, :].rearrange("p (g d h) -> p g h d", g=NG, d=HD),
                                ps[0][:, D * side:D * side + D].rearrange("p (g h d) -> p g h d", g=NG, h=HG))\
                    .then_inc(qk_copied, 1)
            dve.wait_ge(mod_filled, 1)
            dve.tensor_copy(modT[:, :, :], ps[1][:, 0:6 * B].rearrange("p (j b) -> p j b", j=6)).then_inc(mod_step, 1)
            dve.wait_ge(mod_step, 1)
            dve.tensor_scalar(modT[:, 1:5:3, :], modT[:, 1:5:3, :], 1.0, None, ALU.add).then_inc(mod_step, 1)
            dve.wait_ge(mod_step, 2)
            dve.tensor_copy(modc[:, :], modT[:, 0:2, 0:1].rearrange("p j b -> p (j b)")).then_inc(mod_done, 1)
            for n in range(3):
                split(dve, 0, 0, 1, 2, n)
            dve.wait_ge(gates_filled, 1)
            dve.tensor_copy(wm[:, 0:B * D], ps[4][:, :]).then_inc(modrow_done, 1)
            dve.tensor_scalar(scale_row[:, :, :].rearrange("p b d -> p (b d)"), ps[5][:, :], 1.0, None, ALU.add)\
                .then_inc(modrow_done, 1)
            dve.memset(not_first[:, :, :], 1.0).then_inc(modrow_done, 1)
            dve.wait_ge(modrow_done, 3)
            dve.memset(not_first[:, :, 0:1], 0.0)
            for n in range(3):
                split(dve, 0, 1, 1, 6, n)
            gate_flat = gates[:, :, :, :].rearrange("p j b d -> p j (b d)")
            sign_flat = gsign[:, :, :, :].rearrange("p j b d -> p j (b d)")
            for j in range(2):
                dve.tensor_scalar(sign_flat[:, j], ps[2 + j][:, :], 0.0, 2.0, ALU.is_ge, ALU.mult).then_inc(mod_step, 1)
            dve.wait_ge(mod_step, 4)
            for j in range(2):
                dve.scalar_tensor_tensor(out=gate_flat[:, j], in0=sign_flat[:, j], scalar=-1.0, in1=ps[2 + j][:, :],
                                         op0=ALU.add, op1=ALU.mult).then_inc(mod_step, 1)
            dve.wait_ge(mod_step, 6)
            dve.tensor_scalar(gate_flat[:, :], gate_flat[:, :], 0.25, None, ALU.max).then_inc(mod_step, 1)
            dve.wait_ge(mod_step, 7)
            dve.scalar_tensor_tensor(out=gate_flat[:, :], in0=sign_flat[:, :], scalar=-1.0, in1=gate_flat[:, :],
                                     op0=ALU.add, op1=ALU.mult).then_inc(mod_step, 1)
            dve.wait_ge(mod_step, 8)
            dve.tensor_tensor(wog[:, :, :], gates[:, 0, :, :], wo[:, :].unsqueeze(1).broadcast_to([P, B, D]), ALU.mult)
            dve.tensor_tensor(obg[:, :, :], gates[:, 0, :, :], ob_sb[:, :].unsqueeze(1).broadcast_to([P, B, D]),
                              ALU.mult).then_inc(o_folded, 1)
            dve.wait_ge(o_folded, 1)
            dve.memset(ones128[:, :], 1.0)
            for free, count in ((exp_done, XR), (pv_done, PV_FREE), (out_copied, 2), (shared_gelu, IT),
                                (shared_down, 2), (shared_copied, 1), (slotT_copied, 2), (slot_gelu, IT),
                                (slot_down, 2), (slot_weighted, 2)):
                dve.sem_inc(free, count)
            dve.memset(wts[:, :, E:NE], 1.0)

            def row_max(b, q, f):
                i, c0, w, h0, nh = ROWS[f]
                n = NR * (NG * b + q) + f
                dve.wait_ge(row_filled, n + 1)
                bank = row_bank[RBANK[NR * (q % NG) + f][0]]
                dve.tensor_reduce(rowmax[:, q % 2, h0:h0 + nh, i, c0 // CH],
                                  bank[:, 0:w * nh].rearrange("p (h s) -> p h s", h=nh), AX.X, ALU.max).then_inc(row_free, 1)

            def group_max(b, q):
                n, r = NG * b + q, q % 2
                dve.wait_ge(row_free, NR * (n + 1))
                m = rowmax[:, r, :, :, :].rearrange("p h i c -> p (h i) c")
                dve.tensor_tensor(gmax[:, r, :], m[:, :, 0], m[:, :, 1], ALU.max).then_inc(gmax_done, 1)

            def add_residual(b, c, t, at_end=False):
                dve.wait_ge(turn_filled, t + 1)
                dve.wait_ge(y_fetched, 2 * (2 * b + c) + 2 - (c + 1 if at_end else 0))
                xc = x_sb[:, bass.ds(TT * b + 4 * c, 4), :].rearrange("p n d -> p (n d)")
                dve.tensor_tensor(xc, turn_bank[:, :], xc, ALU.add).then_inc(turn_free, 1)

            def var2(b, c, t):
                k = 2 * (2 * b + c)
                dve.wait_ge(turn_free, t + 1)
                dve.sem_inc(waited_dve, 1)
                for n in range(4):
                    ins = dve.bn_stats(st2[:, c, n, :], x_sb[:, bass.ds(TT * b + 4 * c + n, 1), :].rearrange(
                        "p n d -> p (n d)"))
                ins.then_inc(var2_step, 1)
                dve.wait_ge(var2_step, k + 1)
                dve.sem_inc(waited_dve, 1)
                for n in range(4):
                    ins = dve.bn_aggr(mv2[:, c, n, :], st2[:, c, n, :])
                ins.then_inc(var2_step, 1)
                dve.wait_ge(var2_step, k + 2)
                dve.tensor_scalar(rs2[:, c, :], mv2[:, c, :, 1], EPS, None, ALU.add).then_inc(var2_done, 1)

            for s in first_rows():
                if s[0] == "row":
                    row_max(0, s[1], s[2])
                elif s[0] == "maxstat":
                    group_max(0, 0)
            dve.wait_ge(x_rest, 16)

            def body(b, kind):
                last = kind == "last"
                for s in PLAN[kind]:
                    if s[0] == "row":
                        row_max(b, s[1], s[2])
                    elif s[0] == "maxstat":
                        group_max(b, s[1])
                    elif s[0] == "stat":
                        if s[1] == 0:
                            dve.tensor_copy(modc[:, :], modT[:, 0:2, bass.ds(b + 1, 1)].rearrange("p j b -> p (j b)"))
                        stat(b + 1, s[1])
                    elif s[0] == "scale":
                        norm(b + 1, s[1])
                    elif s[:2] == ("post", "proj"):
                        add_residual(b - 1, s[2], turn(b, kind, s))
                    elif s[0] == "var2":
                        var2(b - 1, s[1], turn(b, kind, ("post", "proj", s[1])))
                    elif s[0] == "norm":
                        _, q, c = s
                        dve.wait_ge(turn_filled, turn(b, kind, s) + 1)
                        o = turn_bank[:, :].rearrange("p (n h k) -> p n h k", n=4, h=HG)
                        dve.reciprocal(rden[:, c, :].rearrange("p (n h) -> p n h", n=4), o[:, :, :, HD])\
                            .then_inc(rden_done, 1)
                        dve.wait_ge(rden_done, 2 * (NG * b + q) + c + 1)
                        dve.tensor_tensor(
                            y_all[:, bass.ds(TT * b + 4 * c, 4), 32 * q:32 * q + 32].rearrange(
                                "p n (h d) -> p n h d", h=HG), o[:, :, :, 0:HD],
                            rden[:, c, :].rearrange("p (n h) -> p n h", n=4).unsqueeze(3).broadcast_to([P, 4, HG, HD]),
                            ALU.mult).then_inc(turn_free, 1)

            batches(dve, body)

            def copy_rows(c):
                dve.tensor_copy(h2rows[:, 4 * c:4 * c + 4, 0, 0:D], xn2[:, 4 * c:4 * c + 4, :]).then_inc(h2rows_done, 1)

            for c in range(NC - 2):
                dve.wait_ge(rows2_done, c + 1)
                copy_rows(c)
            for c in range(2):
                add_residual(B - 1, c, BATCH_TURNS + 2 * c + 1, True)
                var2(B - 1, c, BATCH_TURNS + 2 * c + 1)
            for c in range(2):
                dve.wait_ge(last_rstd, c + 1)
                n0 = NT - 8 + 4 * c
                for n in range(4):
                    ins = dve.tensor_scalar(xn2[:, n0 + n, :], x_sb[:, n0 + n, :], mv2[:, c, n, 0:1],
                                            rs2[:, c, n:n + 1], ALU.subtract, ALU.mult)
                ins.then_inc(last_rows2_step, 1)
                dve.wait_ge(last_rows2_step, 2 * c + 1)
                rows = xn2[:, n0:n0 + 4, :]
                dve.tensor_tensor(rows, rows, scale_row[:, B - 1:B, :].broadcast_to([P, 4, D]), ALU.mult)\
                    .then_inc(last_rows2_step, 1)
                dve.wait_ge(last_rows2_step, 2 * c + 2)
                dve.tensor_tensor(rows, rows, shift_row[:, B - 1:B, :].broadcast_to([P, 4, D]), ALU.add)\
                    .then_inc(last_rows2_done, 1)

            for g in range(2):
                half = slice(NT // 2 * g, NT // 2 * (g + 1))
                tiles = [P, NT // 2, E, E]
                dve.wait_ge(gate_exp, g + 1)
                dve.tensor_scalar(score[:, half, :], score[:, half, :], 1.0, None, ALU.add).then_inc(rank_step, 1)
                dve.wait_ge(rank_step, 6 * g + 1)
                dve.reciprocal(score[:, half, :], score[:, half, :]).then_inc(rank_step, 1)
                dve.wait_ge(rank_step, 6 * g + 2)
                other = score[:, half, :].unsqueeze(2).broadcast_to(tiles)
                own = score[:, half, :].unsqueeze(3).broadcast_to(tiles)
                dve.tensor_tensor(equal[:, half], other, own, ALU.is_equal).then_inc(rank_step, 1)
                dve.tensor_tensor(larger[:, half], other, own, ALU.is_gt)
                dve.wait_ge(rank_step, 6 * g + 3)
                dve.tensor_tensor(equal[:, half], equal[:, half], below[:, :, :].unsqueeze(1).broadcast_to(tiles),
                                  ALU.mult).then_inc(rank_step, 1)
                dve.wait_ge(rank_step, 6 * g + 4)
                dve.tensor_tensor(larger[:, half], larger[:, half], equal[:, half], ALU.add).then_inc(rank_step, 1)
                dve.wait_ge(rank_step, 6 * g + 5)
                dve.tensor_reduce(rank[:, half, :], larger[:, half], AX.X, ALU.add).then_inc(rank_step, 1)
            dve.wait_ge(rank_step, 12)
            dve.tensor_scalar(chosen[:, :, :], rank[:, :, :], 1.5, None, ALU.is_lt).then_inc(chosen_ready, 1)
            dve.scalar_tensor_tensor(out=wts[:, :, 0:E], in0=rank[:, :, :], scalar=1.5, in1=score[:, :, :],
                                     op0=ALU.is_lt, op1=ALU.mult).then_inc(route_step, 1)
            dve.wait_ge(route_step, 1)
            dve.tensor_reduce(wsum[:, :], wts[:, :, 0:E], AX.X, ALU.add).then_inc(route_step, 1)
            dve.wait_ge(route_step, 2)
            dve.tensor_scalar(wsum[:, :], wsum[:, :], 1e-6, None, ALU.add).then_inc(route_step, 1)
            dve.wait_ge(route_step, 3)
            dve.reciprocal(wsum[:, :], wsum[:, :]).then_inc(route_step, 1)
            dve.wait_ge(route_step, 4)
            dve.tensor_tensor(wts[:, :, 0:E], wts[:, :, 0:E], wsum[:, :].unsqueeze(2).broadcast_to([P, NT, E]), ALU.mult)\
                .then_inc(wts_done, 2)
            dve.wait_ge(wts_done, 2)
            for r in range(2):
                dve.scalar_tensor_tensor(out=by_rank[:, 2 + r, :, :], in0=rank[:, :, :], scalar=float(r),
                                         in1=wts[:, :, 0:E], op0=ALU.is_equal, op1=ALU.mult).then_inc(route_step, 1)
            dve.wait_ge(counted, 1)
            dve.tensor_copy(totals[:, :, :], ps[7][:, NT * E:2 * NT * E].rearrange("p (n e) -> p e n", n=NT))\
                .then_inc(totals_done, 1)
            dve.wait_ge(totals_done, 1)
            within = ps[7][:, 0:NT * E].rearrange("p (n e) -> p n e", n=NT)
            dve.tensor_tensor_scan(running[:, :, :].rearrange("p e n -> p (e n)"),
                                   not_first[:, :, :].rearrange("p e n -> p (e n)"),
                                   totals[:, :, :].rearrange("p e n -> p (e n)"), 0.0, ALU.mult, ALU.add)\
                .then_inc(route_step, 1)
            dve.wait_ge(route_step, 7)
            dve.tensor_tensor(filled[:, :, :], running[:, :, NT - 1:NT].broadcast_to([P, E, MOST]),
                              tile_start[:, :].unsqueeze(1).broadcast_to([P, E, MOST]), ALU.is_gt)\
                .then_inc(route_step, 1)
            dve.tensor_tensor(before_tile[:, :, :], running[:, :, :], totals[:, :, :], ALU.subtract)\
                .then_inc(route_step, 1)
            dve.wait_ge(route_step, 9)
            dve.tensor_reduce(expert_tiles[:, 0, :], filled[:, :, :], AX.X, ALU.add).then_inc(route_step, 1)
            dve.wait_ge(route_step, 10)
            dve.tensor_tensor_scan(expert_tiles[:, 1, :], ones128[:, 0:E], expert_tiles[:, 0, :], 0.0,
                                   ALU.mult, ALU.add).then_inc(route_step, 1)
            dve.wait_ge(route_step, 11)
            dve.tensor_tensor(expert_tiles[:, 2, :], expert_tiles[:, 1, :], expert_tiles[:, 0, :], ALU.subtract)\
                .then_inc(route_step, 1)
            dve.wait_ge(route_step, 12)
            dve.scalar_tensor_tensor(out=before_tile[:, :, :],
                                     in0=expert_tiles[:, 2, :].unsqueeze(2).broadcast_to([P, E, NT]),
                                     scalar=float(SLOTS), in1=before_tile[:, :, :], op0=ALU.mult, op1=ALU.add)\
                .then_inc(route_step, 1)
            dve.wait_ge(route_step, 13)
            dve.tensor_tensor(position[:, :, :], within, before_tile[:, :, :].rearrange("p e n -> p n e"), ALU.add)\
                .then_inc(route_step, 1)
            dve.wait_ge(route_step, 14)
            for r in range(2):
                dve.scalar_tensor_tensor(out=by_rank[:, r, :, :], in0=rank[:, :, :], scalar=float(r),
                                         in1=position[:, :, :], op0=ALU.is_equal, op1=ALU.mult).then_inc(route_step, 1)
            dve.wait_ge(route_step, 16)
            dve.tensor_reduce(picked[:, :, :], by_rank[:, :, :, :], AX.X, ALU.add).then_inc(route_step, 1)
            dve.wait_ge(route_step, 17)
            dve.tensor_copy(h2rows[:, :, :, W_COL], picked[:, 2:4, :].rearrange("p r n -> p n r"))
            dve.tensor_copy(row_at[:, :, :], picked[:, 0:2, :]).then_inc(positions_done, 1)
            dve.wait_ge(last_rows2_done, 2)
            copy_rows(NC - 2)
            copy_rows(NC - 1)
            dve.tensor_tensor(past[:, :, :], tile_number[:, :].unsqueeze(2).broadcast_to([1, NS, E]),
                              expert_tiles[0:1, 1, :].unsqueeze(1).broadcast_to([1, NS, E]), ALU.is_ge)\
                .then_inc(route_step, 1)
            dve.wait_ge(route_step, 18)
            dve.tensor_reduce(expert_f[:, :], past[:, :, :], AX.X, ALU.add).then_inc(route_step, 1)
            dve.wait_ge(route_step, 19)
            dve.tensor_scalar(expert_of[:, :], expert_f[:, :], float(E - 1), None, ALU.min).then_inc(table_done, 1)

            def copy_up(j, k):
                e = dve.value_load(expert_of[0:1, bass.ds(SCHUNK * j + k, 1)], min_val=0, max_val=E - 1)
                dve.tensor_copy(ubr[:, k % SCHUNK, :], ub[:, bass.ds(e, 1), :].rearrange("p n d -> p (n d)"))
                dve.tensor_copy(ur[:, k % 2, :], uw[:, bass.ds(e, 1), :].rearrange("p n d -> p (n d)"))\
                    .then_inc(up_copied, 1)

            def copy_down(j, k):
                e = dve.value_load(expert_of[0:1, bass.ds(SCHUNK * j + k, 1)], min_val=0, max_val=E - 1)
                dve.tensor_copy(dr[:, k % 2, :, :].rearrange("p c h -> p (c h)"),
                                dw[:, bass.ds(e, 1), :, :].rearrange("p n c h -> p (n c h)")).then_inc(down_copied, 1)

            dve.wait_ge(table_done, 1)
            dve.wait_ge(bias_loaded, 16 * 9)
            dve.wait_ge(ffn_loaded, 16 * (1 + E))
            copy_up(0, 0)
            copy_down(0, 0)
            copy_up(0, 1)
            copy_down(0, 1)
            for c in range(NC):
                dve.wait_ge(bias_filled, c + 1)
                dve.wait_ge(shared_copied, c + 1 + 1)
                a = acc[:, 4 * c:4 * c + 4, :].rearrange("p n d -> p (n d)")
                dve.tensor_tensor(a, ps[2 + c % 2][:, :], a, ALU.add).then_inc(acc_started, 1)
            dve.wait_ge(slot_up, IT)
            copy_up(0, 2)

            def step(j, k, peeled):
                dve.wait_ge(slot_down, SCHUNK * j + k + 1 + 2)
                if not isinstance(j, int) or j > 0:
                    dve.wait_ge(results_sent[k], 16 * ST * j)
                for t in range(ST):
                    last = dve.tensor_scalar(slot_out[:, k, t, :], ps[4 + k % 2][:, P * t:P * t + P],
                                             slot_rows[:, k, t, W_COL:W_COL + 1], None, ALU.mult)
                last.then_inc(slot_weighted, 1)
                if not peeled or k + 2 < NS % SCHUNK:
                    copy_down(j, k + 2)
                if not peeled or k + 3 < NS % SCHUNK:
                    copy_up(j, k + 3)

            slot_tiles(dve, step)

            for m in range(NC + 1):
                if m < NC:
                    cc = m % 2
                    sums = acc[:, 4 * m:4 * m + 4, :]
                    dve.wait_ge(rank0_added, m + 1)
                    dve.tensor_tensor(sums, sums, routed[:, 1, 4 * m:4 * m + 4, :], ALU.add).then_inc(fin_step, 1)
                    dve.wait_ge(fin_step, 3 * m + 1)
                    dve.tensor_reduce(amax[:, cc, :], sums, AX.X, ALU.max, apply_absolute_value=True)\
                        .then_inc(fin_step, 1)
                    dve.wait_ge(fin_step, 3 * m + 2)
                    dve.tensor_scalar(amax[:, cc, :], amax[:, cc, :], 0.1, 1e-6, ALU.mult, ALU.add).then_inc(fin_step, 1)
                    dve.wait_ge(fin_step, 3 * m + 3)
                    if m >= 2:
                        dve.wait_ge(normalised, m - 1)
                    dve.reciprocal(amax_inv[:, cc, :], amax[:, cc, :]).then_inc(inverted, 1)
                if m >= 1:
                    cc = (m - 1) % 2
                    dve.wait_ge(normalised, m)
                    dve.scalar_tensor_tensor(out=fin[:, m - 1, :, :], in0=fin[:, m - 1, :, :], scalar=0.1,
                                             in1=gates[:, 1, (m - 1) // 2:(m - 1) // 2 + 1, :].broadcast_to([P, 4, D]),
                                             op0=ALU.mult, op1=ALU.mult).then_inc(gated, 1)


def kernel(**inputs):
    import numpy as np
    import concourse.bacc as bacc
    from concourse.bass_utils import run_bass_kernel_spmd as run

    a = {k.removeprefix("L0_"): np.asarray(v) for k, v in inputs.items()}

    def low(m):
        return m.transpose(0, 2, 1).reshape(H // 2, 2 * R, D).transpose(1, 0, 2)

    def high(m):
        return m.reshape(H // 2, 2 * R, HD).transpose(1, 0, 2)

    arrays = dict(
        x=a["attn_hidden_states"].reshape(B * T, D), qaT=low(a["attn_q_a"]), kaT=low(a["attn_k_a"]),
        qb=high(a["attn_q_b"]), kb=high(a["attn_k_b"]), vwT=a["attn_v_w"].T, owT=a["attn_o_w"].T,
        v_b=a["attn_v_b"].reshape(1, D), o_b=a["attn_o_b"].reshape(1, D), cT=a["c"].T, wmod=a["wmod"],
        gate_w=a["ffn_gate_w"], gate_b=a["ffn_bias"].reshape(E, 1), up_w=a["ffn_up_w"].transpose(1, 0, 2),
        up_b=a["ffn_up_b"].reshape(E, IT, P).transpose(2, 0, 1), down_w=a["ffn_down_w"], down_b=a["ffn_down_b"],
        sw_up=a["ffn_sw_up"], sb_up=a["ffn_sb_up"].reshape(IT, P).T, sw_down=a["ffn_sw_down"],
        sb_down=a["ffn_sb_down"].reshape(1, D))
    arrays = {f"in_{k}": np.ascontiguousarray(v) for k, v in arrays.items()}
    nc = bacc.Bacc("TRN2", target_bir_lowering=False, num_devices=1)
    args = [nc.dram_tensor(k, v.shape, mybir.dt.from_np(v.dtype), kind="ExternalInput").ap()
            for k, v in arrays.items()]
    args.append(nc.dram_tensor("out", (B * T, D), F32, kind="ExternalOutput").ap())
    adaln_block(nc, *args)
    r = run(nc, [arrays], core_ids=[0])
    return np.asarray(r.results[0]["out"]).reshape(B, T, D)
```
